# Optimizing a Trainium2 kernel written in Bass

```python
import numpy as np
import jax
import jax.numpy as jnp

def _softmax(x, axis=-1):
    return jax.nn.softmax(x, axis=axis)

def _gelu(x):
    return jax.nn.gelu(x, approximate=True)

def _silu(x):
    return jax.nn.silu(x)

def _sigmoid(x):
    return jax.nn.sigmoid(x)

def _layernorm(x, axis=-1, eps=1e-05):
    m = jnp.mean(x, axis=axis, keepdims=True)
    v = jnp.var(x, axis=axis, keepdims=True)
    return (x - m) / jnp.sqrt(v + eps)

def _scatter_add(tgt, idx, src, axis=0):
    return tgt.at[idx].add(src)

def _segment_sum(src, seg, n):
    return jax.ops.segment_sum(src, seg, n)
kernel_name = 'mk_decoder_postln_d1_seqx_r2_e98b5b'

def setup_inputs(seed: int=0):
    np.random.seed(seed)
    _w = jnp.asarray

    def _rec_inputs():
        import jax
        import jax.numpy as jnp
        _rk = jax.random.key(seed)
        x = 7.22e-05 + 1 * jax.random.normal(jax.random.fold_in(_rk, 1), (8, 512, 512), jnp.float32)
        _lenS = 512 - jax.random.randint(jax.random.fold_in(_rk, 7), (8,), 0, max(1, 512 // 4) + 1, jnp.int32)
        _lenS2 = 512 - jax.random.randint(jax.random.fold_in(_rk, 8), (8,), 0, max(1, 512 // 4) + 1, jnp.int32)
        _ctx_1024P = jax.random.normal(jax.random.fold_in(_rk, 11), (8, 16, 512), jnp.float32)
        _ctx_1024c = jax.random.dirichlet(jax.random.fold_in(_rk, 511), 0.3 * jnp.ones((16,), jnp.float32), (8, 512))
        _ctx_1024t = jnp.einsum('bsk,bkd->bsd', _ctx_1024c, _ctx_1024P)
        _ctx_1024t = _ctx_1024t * jax.lax.rsqrt(jnp.mean(jnp.square(_ctx_1024t)) + 1e-12) * 0.953939
        ctx_1024 = 4.13588e-05 + 0.999923 * (_ctx_1024t + 0.3 * jax.random.normal(jax.random.fold_in(_rk, 611), (8, 512, 512), jnp.float32))
        return (x, ctx_1024)
    x, ctx_1024 = _rec_inputs()

    def _L0_attn_setup():
        import jax, jax.numpy as jnp
        import numpy as np
        BATCH, SEQ, D_MODEL = (4, 1024, 512)
        D_STATE, D_CONV, EXPAND, HEADDIM = (64, 4, 2, 64)
        D_INNER = EXPAND * D_MODEL
        NHEADS = D_INNER // HEADDIM
        CONV_DIM = D_INNER + 2 * D_STATE
        D_IN_PROJ = 2 * D_INNER + 2 * D_STATE + NHEADS
        EPS = 1e-05

        def mamba2(X, W_in, conv_w, conv_b, dt_bias, A_log, D, norm_w, W_out):
            b, l, _ = X.shape
            zxbcdt = X @ W_in.T
            z, xBC, dt = jnp.split(zxbcdt, [D_INNER, D_INNER + CONV_DIM], axis=-1)
            dt = jax.nn.softplus(dt + dt_bias)
            xBC_t = xBC.transpose(0, 2, 1)
            ker = conv_w[:, None, :]
            xBC_c = jax.lax.conv_general_dilated(xBC_t, ker, window_strides=(1,), padding=[(D_CONV - 1, 0)], feature_group_count=CONV_DIM)
            xBC = jax.nn.silu(xBC_c.transpose(0, 2, 1) + conv_b)
            x, Bm, Cm = jnp.split(xBC, [D_INNER, D_INNER + D_STATE], axis=-1)
            xh = x.reshape(b, l, NHEADS, HEADDIM)
            A = -jnp.exp(A_log)
            dA = jnp.exp(dt * A)
            dBx = jnp.einsum('blh,bln,blhp->blhpn', dt, Bm, xh)

            def step(h, inp):
                dA_t, dBx_t, C_t = inp
                h = h * dA_t[:, :, None, None] + dBx_t
                y = jnp.einsum('bhpn,bn->bhp', h, C_t)
                return (h, y)
            h0 = jnp.zeros((b, NHEADS, HEADDIM, D_STATE), X.dtype)
            _, ys = jax.lax.scan(step, h0, (dA.transpose(1, 0, 2), dBx.transpose(1, 0, 2, 3, 4), Cm.transpose(1, 0, 2)))
            y = ys.transpose(1, 0, 2, 3) + D[None, None, :, None] * xh
            y = y.reshape(b, l, D_INNER)
            y = y * jax.nn.silu(z)
            y = y * jax.lax.rsqrt(jnp.mean(y * y, axis=-1, keepdims=True) + EPS) * norm_w
            return y @ W_out.T
        key = jax.random.key(seed)
        ks = jax.random.split(key, 6)
        s = 0.02
        return {'X': jax.random.normal(ks[0], (BATCH, SEQ, D_MODEL), jnp.float32), 'W_in': jax.random.normal(ks[1], (D_IN_PROJ, D_MODEL), jnp.float32) * s, 'conv_w': jax.random.normal(ks[2], (CONV_DIM, D_CONV), jnp.float32) * s, 'conv_b': jnp.zeros((CONV_DIM,), jnp.float32), 'dt_bias': jax.random.uniform(ks[3], (NHEADS,), jnp.float32), 'A_log': jnp.log(jax.random.uniform(ks[4], (NHEADS,), jnp.float32, minval=1.0, maxval=16.0)), 'D': jnp.ones((NHEADS,), jnp.float32), 'norm_w': jnp.ones((D_INNER,), jnp.float32), 'W_out': jax.random.normal(ks[5], (D_MODEL, D_INNER), jnp.float32) * s}
    _L0_attn_all = _L0_attn_setup()
    _L0_attn_in = {k: v for k, v in _L0_attn_all.items() if k in ('W_in', 'conv_w', 'conv_b', 'dt_bias', 'A_log', 'D', 'norm_w', 'W_out')}
    del _L0_attn_all

    def _L0_xattn_setup():
        import jax, jax.numpy as jnp
        import numpy as np
        DIM = 512
        HEADS = 16
        HEAD_DIM = DIM // HEADS
        key = jax.random.key(seed)
        ks = jax.random.split(key, 10)
        B, N, M = (4, 1024, 1024)
        s = 1.0 / np.sqrt(DIM)
        return {'x': jax.random.normal(ks[0], (B, N, DIM), jnp.float32), 'context': jax.random.normal(ks[1], (B, M, DIM), jnp.float32), 'Wq': jax.random.normal(ks[2], (DIM, DIM), jnp.float32) * s, 'bq': jnp.zeros((DIM,), jnp.float32), 'Wk': jax.random.normal(ks[3], (DIM, DIM), jnp.float32) * s, 'bk': jnp.zeros((DIM,), jnp.float32), 'Wv': jax.random.normal(ks[4], (DIM, DIM), jnp.float32) * s, 'bv': jnp.zeros((DIM,), jnp.float32), 'Wo': jax.random.normal(ks[5], (DIM, DIM), jnp.float32) * s, 'bo': jnp.zeros((DIM,), jnp.float32)}
    _L0_xattn_all = _L0_xattn_setup()
    _L0_xattn_in = {k: v for k, v in _L0_xattn_all.items() if k in ('Wq', 'bq', 'Wk', 'bk', 'Wv', 'bv', 'Wo', 'bo')}
    del _L0_xattn_all

    def _L0_ffn_setup():
        import jax, jax.numpy as jnp
        import numpy as np
        LN_EPS = 1e-05
        NORM_EPS = 1e-12

        def _layernorm(x, gamma, beta):
            mu = x.mean(axis=-1, keepdims=True)
            var = ((x - mu) ** 2).mean(axis=-1, keepdims=True)
            return (x - mu) * jax.lax.rsqrt(var + LN_EPS) * gamma + beta

        def _l2norm(x, axis):
            n = jnp.sqrt((x ** 2).sum(axis=axis, keepdims=True))
            return x / jnp.maximum(n, NORM_EPS)
        key = jax.random.key(seed)
        ks = jax.random.split(key, 4)
        B, N, D, E, S, H = (64, 128, 512, 16, 16, 128)
        x = jax.random.normal(ks[0], (B, N, D), dtype=jnp.float32)
        mu = jax.random.normal(ks[1], (D, E, S), dtype=jnp.float32) / np.sqrt(D)
        w1 = jax.random.normal(ks[2], (E, D, H), dtype=jnp.float32) * np.sqrt(2.0 / D)
        w2 = jax.random.normal(ks[3], (E, H, D), dtype=jnp.float32) * np.sqrt(2.0 / (H + D))
        return {'x': x, 'ln_gamma': jnp.ones((D,), jnp.float32), 'ln_beta': jnp.zeros((D,), jnp.float32), 'mu': mu, 'scale': jnp.ones((1,), jnp.float32), 'w1': w1, 'b1': jnp.zeros((E, H), jnp.float32), 'w2': w2, 'b2': jnp.zeros((E, D), jnp.float32)}
    _L0_ffn_all = _L0_ffn_setup()
    _L0_ffn_in = {k: v for k, v in _L0_ffn_all.items() if k in ('ln_gamma', 'ln_beta', 'mu', 'scale', 'w1', 'b1', 'w2', 'b2')}
    del _L0_ffn_all
    return {'x': x, 'ctx_1024': ctx_1024, 'L0_attn_W_in': _L0_attn_in['W_in'], 'L0_attn_conv_w': _L0_attn_in['conv_w'], 'L0_attn_conv_b': _L0_attn_in['conv_b'], 'L0_attn_dt_bias': _L0_attn_in['dt_bias'], 'L0_attn_A_log': _L0_attn_in['A_log'], 'L0_attn_D': _L0_attn_in['D'], 'L0_attn_norm_w': _L0_attn_in['norm_w'], 'L0_attn_W_out': _L0_attn_in['W_out'], 'L0_xattn_Wq': _L0_xattn_in['Wq'], 'L0_xattn_bq': _L0_xattn_in['bq'], 'L0_xattn_Wk': _L0_xattn_in['Wk'], 'L0_xattn_bk': _L0_xattn_in['bk'], 'L0_xattn_Wv': _L0_xattn_in['Wv'], 'L0_xattn_bv': _L0_xattn_in['bv'], 'L0_xattn_Wo': _L0_xattn_in['Wo'], 'L0_xattn_bo': _L0_xattn_in['bo'], 'L0_ffn_ln_gamma': _L0_ffn_in['ln_gamma'], 'L0_ffn_ln_beta': _L0_ffn_in['ln_beta'], 'L0_ffn_mu': _L0_ffn_in['mu'], 'L0_ffn_scale': _L0_ffn_in['scale'], 'L0_ffn_w1': _L0_ffn_in['w1'], 'L0_ffn_b1': _L0_ffn_in['b1'], 'L0_ffn_w2': _L0_ffn_in['w2'], 'L0_ffn_b2': _L0_ffn_in['b2']}

def reference(x, ctx_1024, L0_attn_W_in, L0_attn_conv_w, L0_attn_conv_b, L0_attn_dt_bias, L0_attn_A_log, L0_attn_D, L0_attn_norm_w, L0_attn_W_out, L0_xattn_Wq, L0_xattn_bq, L0_xattn_Wk, L0_xattn_bk, L0_xattn_Wv, L0_xattn_bv, L0_xattn_Wo, L0_xattn_bo, L0_ffn_ln_gamma, L0_ffn_ln_beta, L0_ffn_mu, L0_ffn_scale, L0_ffn_w1, L0_ffn_b1, L0_ffn_w2, L0_ffn_b2):
    import jax
    import jax.numpy as jnp

    def _L0_attn_ref(X, W_in, conv_w, conv_b, dt_bias, A_log, D, norm_w, W_out):
        import jax, jax.numpy as jnp
        import numpy as np
        BATCH, SEQ, D_MODEL = (4, 1024, 512)
        D_STATE, D_CONV, EXPAND, HEADDIM = (64, 4, 2, 64)
        D_INNER = EXPAND * D_MODEL
        NHEADS = D_INNER // HEADDIM
        CONV_DIM = D_INNER + 2 * D_STATE
        D_IN_PROJ = 2 * D_INNER + 2 * D_STATE + NHEADS
        EPS = 1e-05

        def mamba2(X, W_in, conv_w, conv_b, dt_bias, A_log, D, norm_w, W_out):
            b, l, _ = X.shape
            zxbcdt = X @ W_in.T
            z, xBC, dt = jnp.split(zxbcdt, [D_INNER, D_INNER + CONV_DIM], axis=-1)
            dt = jax.nn.softplus(dt + dt_bias)
            xBC_t = xBC.transpose(0, 2, 1)
            ker = conv_w[:, None, :]
            xBC_c = jax.lax.conv_general_dilated(xBC_t, ker, window_strides=(1,), padding=[(D_CONV - 1, 0)], feature_group_count=CONV_DIM)
            xBC = jax.nn.silu(xBC_c.transpose(0, 2, 1) + conv_b)
            x, Bm, Cm = jnp.split(xBC, [D_INNER, D_INNER + D_STATE], axis=-1)
            xh = x.reshape(b, l, NHEADS, HEADDIM)
            A = -jnp.exp(A_log)
            dA = jnp.exp(dt * A)
            dBx = jnp.einsum('blh,bln,blhp->blhpn', dt, Bm, xh)

            def step(h, inp):
                dA_t, dBx_t, C_t = inp
                h = h * dA_t[:, :, None, None] + dBx_t
                y = jnp.einsum('bhpn,bn->bhp', h, C_t)
                return (h, y)
            h0 = jnp.zeros((b, NHEADS, HEADDIM, D_STATE), X.dtype)
            _, ys = jax.lax.scan(step, h0, (dA.transpose(1, 0, 2), dBx.transpose(1, 0, 2, 3, 4), Cm.transpose(1, 0, 2)))
            y = ys.transpose(1, 0, 2, 3) + D[None, None, :, None] * xh
            y = y.reshape(b, l, D_INNER)
            y = y * jax.nn.silu(z)
            y = y * jax.lax.rsqrt(jnp.mean(y * y, axis=-1, keepdims=True) + EPS) * norm_w
            return y @ W_out.T
        return mamba2(X, W_in, conv_w, conv_b, dt_bias, A_log, D, norm_w, W_out) + X

    def _L0_xattn_ref(x, context, Wq, bq, Wk, bk, Wv, bv, Wo, bo):
        import jax, jax.numpy as jnp
        import numpy as np
        DIM = 512
        HEADS = 16
        HEAD_DIM = DIM // HEADS
        B, N, C = x.shape
        M = context.shape[1]
        scale = HEAD_DIM ** (-0.5)
        q = (x @ Wq.T + bq).reshape(B, N, HEADS, HEAD_DIM).transpose(0, 2, 1, 3)
        k = (context @ Wk.T + bk).reshape(B, M, HEADS, HEAD_DIM).transpose(0, 2, 1, 3)
        v = (context @ Wv.T + bv).reshape(B, M, HEADS, HEAD_DIM).transpose(0, 2, 1, 3)
        attn = jax.nn.softmax(jnp.einsum('bhnd,bhmd->bhnm', q, k) * scale, axis=-1)
        out = jnp.einsum('bhnm,bhmd->bhnd', attn, v)
        out = out.transpose(0, 2, 1, 3).reshape(B, N, C)
        return out @ Wo.T + bo

    def _L0_ffn_ref(x, ln_gamma, ln_beta, mu, scale, w1, b1, w2, b2):
        import jax, jax.numpy as jnp
        import numpy as np
        LN_EPS = 1e-05
        NORM_EPS = 1e-12

        def _layernorm(x, gamma, beta):
            mu = x.mean(axis=-1, keepdims=True)
            var = ((x - mu) ** 2).mean(axis=-1, keepdims=True)
            return (x - mu) * jax.lax.rsqrt(var + LN_EPS) * gamma + beta

        def _l2norm(x, axis):
            n = jnp.sqrt((x ** 2).sum(axis=axis, keepdims=True))
            return x / jnp.maximum(n, NORM_EPS)
        B, N, D = x.shape
        _, E, S = mu.shape
        xn = _layernorm(x, ln_gamma, ln_beta)
        x_unit = _l2norm(xn, axis=-1)
        mu_unit = _l2norm(mu, axis=0)
        logits = jnp.einsum('bnd,des->bnes', x_unit * scale, mu_unit)
        dispatch = jax.nn.softmax(logits, axis=1)
        combine = jax.nn.softmax(logits.reshape(B, N, E * S), axis=-1).reshape(B, N, E, S)
        slot_in = jnp.einsum('bnd,bnes->besd', xn, dispatch)
        h = jax.nn.gelu(jnp.einsum('besd,edh->besh', slot_in, w1) + b1[None, :, None, :], approximate=False)
        slot_out = jnp.einsum('besh,ehd->besd', h, w2) + b2[None, :, None, :]
        out = jnp.einsum('besd,bnes->bnd', slot_out, combine)
        return out
    x = _layernorm(x + _L0_attn_ref(x, L0_attn_W_in, L0_attn_conv_w, L0_attn_conv_b, L0_attn_dt_bias, L0_attn_A_log, L0_attn_D, L0_attn_norm_w, L0_attn_W_out), axis=-1)
    x = _layernorm(x + _L0_xattn_ref(x, ctx_1024, L0_xattn_Wq, L0_xattn_bq, L0_xattn_Wk, L0_xattn_bk, L0_xattn_Wv, L0_xattn_bv, L0_xattn_Wo, L0_xattn_bo), axis=-1)
    x = _layernorm(x + _L0_ffn_ref(x, L0_ffn_ln_gamma, L0_ffn_ln_beta, L0_ffn_mu, L0_ffn_scale, L0_ffn_w1, L0_ffn_b1, L0_ffn_w2, L0_ffn_b2), axis=-1)
    return x

_drawn_inputs = setup_inputs


def setup_inputs(seed=0):
    import zlib

    import numpy as np

    out = dict(_drawn_inputs(seed))
    spreads = {'L0_attn_conv_b': (0.0, 0.1),
     'L0_attn_D': (1.0, 0.2),
     'L0_attn_norm_w': (1.0, 0.2),
     'L0_xattn_bq': (0.0, 0.439),
     'L0_xattn_bk': (0.0, 2.0),
     'L0_xattn_bv': (0.0, 0.1),
     'L0_xattn_bo': (0.0, 0.1),
     'L0_ffn_ln_gamma': (1.0, 0.6),
     'L0_ffn_ln_beta': (0.0, 0.589),
     'L0_ffn_b1': (0.0, 0.79),
     'L0_ffn_b2': (0.0, 0.333)}
    factors = {'L0_attn_dt_bias': 29.321, 'L0_attn_A_log': 8.0, 'L0_ffn_mu': 64.0}
    for name, (base, spread) in spreads.items():
        noise = np.random.default_rng([zlib.crc32(name.encode()), seed]).standard_normal(out[name].shape)
        drawn = base * np.exp(spread * noise) if base else spread * noise
        out[name] = jnp.asarray(drawn.astype(out[name].dtype))
    for name, factor in factors.items():
        out[name] = (out[name] * factor).astype(out[name].dtype)
    return out
```

```python
from contextlib import ExitStack

import numpy as np

import concourse.bass as bass
from concourse import mybir

F32 = mybir.dt.float32
F32R = mybir.dt.float32r
ALU = mybir.AluOpType
ACT = mybir.ActivationFunctionType
AX = mybir.AxisListType

P = 128
SEQ = 512
DM = 512
KT = DM // P
TT = SEQ // P
LN_EPS = 1e-5


def at(b, per, k):
    return b * per + k


def value(eng, n):
    return n if isinstance(n, int) else eng.bass.snap(n, engines=[eng.engine])


class Chain:

    def __init__(self, eng, sem, per):
        self.eng, self.sem, self.per = eng, sem, per

    def start(self, b):
        self.base, self.k = b * self.per, 0

    def link(self, ins, before=None):
        ins.then_inc(self.sem, 1)
        self.k += 1
        if before:
            count = value(self.eng, self.base + self.k)
            met(self.eng, *before)
            self.eng.wait_ge(self.sem, count)
        else:
            self.eng.wait_ge(self.sem, self.base + self.k)

    def end(self):
        assert self.k == self.per, (self.k, self.per)


def met(eng, sem, value):
    eng.wait_ge(sem, value)


def over_sequences(eng, count, body):
    body(0, True)
    if count > 1:
        with eng.Fori(1, count) as i:
            body(i, False)


def one(ap, b):
    return ap[bass.ds(b, 1)]


DI = 1024
NH = 16
HP = 64
NS = 64
XT_TILES = DI // P
CH = 4
HG = 4
NG = NH // HG
COLS = NH + 2 * DI + 2 * NS
COL_Z, COL_X, COL_BC = NH, NH + DI, NH + 2 * DI


def mamba_stage(nc, n_seq, xT, x, winT, conv_w, conv_b, dt_bias, a_log, d_skip, norm_w, woutT, x1):
    with ExitStack() as ctx:
        def sb(name, shape, dt=F32):
            return ctx.enter_context(nc.sbuf_tensor("m_" + name, shape, dt))

        def ps(name):
            return ctx.enter_context(nc.psum_tensor("m_" + name, [P, 512], F32))

        def sem(name):
            return ctx.enter_context(nc.semaphore("m_" + name))

        win_hi = sb("win_hi", [P, KT, COLS], F32R)
        win_lo = sb("win_lo", [P, KT, COLS], F32R)
        wout = sb("wout", [P, XT_TILES, DM])
        cw = sb("cw", [P, 9, 4])
        cb = sb("cb", [P, 9])
        dcol = sb("dcol", [P, XT_TILES])
        nw = sb("nw", [P, XT_TILES])
        dtb = sb("dtb", [P, NH])
        aneg = sb("aneg", [P, NH])
        tri = sb("tri", [P, P])
        strict = sb("strict", [P, P])
        ident = sb("ident", [P, P])
        onesf = sb("onesf", [P, P])
        strict_r = sb("strict_r", [P, P], F32R)
        ones_r = sb("ones_r", [P, P], F32R)
        neg_half = sb("neg_half", [P, TT])
        xt_in = sb("xt_in", [P, 2, SEQ])
        xt_hi = sb("xt_hi", [P, KT, SEQ], F32R)
        xt_lo = sb("xt_lo", [P, KT, SEQ], F32R)
        x_tok = sb("x_tok", [P, TT, DM])
        dt_ch = sb("dt_ch", [32, SEQ])
        sm = sb("sm", [P, 8, CH * NH])
        dt = sb("dt", [P, CH, NH])
        a = sb("a", [P, CH, NH])
        a_hi = sb("a_hi", [P, CH, NH])
        a_lo = sb("a_lo", [P, CH, NH])
        a_hr = sb("a_hr", [P, CH, NH], F32R)
        wd = sb("wd", [P, 2, CH, NH])
        wdt = sb("wdt", [P, CH, NH])
        acc = sb("acc", [P, 2, SEQ])
        xc = sb("xc", [P, 2, 2, SEQ])
        zs = sb("zs", [P, 2, 2, SEQ])
        bt = sb("bt", [NS, SEQ])
        ct = sb("ct", [NS, SEQ])
        b_tok = sb("b_tok", [P, CH, NS])
        gm = sb("gm", [P, CH, P])
        rhs_hi = sb("rhs_hi", [P, 2, HG, P], F32R)
        rhs_lo = sb("rhs_lo", [P, 2, HG, P], F32R)
        dec = sb("dec", [P, CH, HG, P])
        ce = sb("ce", [NS, CH - 1, HG, P])
        xk = sb("xk", [P, CH, HG, HP])
        xdt = sb("xdt", [P, CH, HG, HP])
        xw = sb("xw", [P, CH - 1, HG, HP])
        st = sb("st", [NS, CH - 1, HG, HP])
        g = sb("g", [P, XT_TILES, SEQ])
        sq = sb("sq", [P, 2, SEQ])
        ssum = sb("ssum", [P, SEQ])
        rms = sb("rms", [P, 2, TT])
        stats = sb("stats", [P, TT, 6])
        mv = sb("mv", [P, TT, 2])
        rstd = sb("rstd", [P, 2, TT])
        staging = g[:, :, :].rearrange("p a b -> p (a b)")[:, 0:COLS]

        proj = [ps("proj0"), ps("proj1")]
        seg = [ps("seg0"), ps("seg1")]
        misc, turn = ps("misc"), ps("turn")
        yp = [ps("y0"), ps("y1")]

        w_in = sem("w_in")
        w_used = sem("w_used")
        small_in = sem("small_in")
        const = sem("const")
        setup = sem("setup")
        setup_a = sem("setup_a")
        xt_landed = [sem("xt_landed0"), sem("xt_landed1")]
        xt_split = sem("xt_split")
        xt_hi_s = sem("xt_hi_s")
        x_in = sem("x_in")
        x_dbl = sem("x_dbl")
        tile_done = sem("tile_done")
        dt_read = sem("dt_read")
        dt_turned = sem("dt_turned")
        a_ready = sem("a_ready")
        sums_done = sem("sums_done")
        wd_ready = sem("wd_ready")
        wdt_ready = sem("wdt_ready")
        dtv = sem("dtv")
        dta = sem("dta")
        taps0 = sem("taps0")
        conv_read = sem("conv_read")
        conv_v = sem("conv_v")
        bc_ready = sem("bc_ready")
        xc_ready = sem("xc_ready")
        z_ready = sem("z_ready")
        bg_done = sem("bg_done")
        bg_read = sem("bg_read")
        rhs_ready = sem("rhs_ready")
        seg_done = sem("seg_done")
        dec_ready = sem("dec_ready")
        m_ready = sem("m_ready")
        ebc_done = sem("ebc_done")
        e_ready = sem("e_ready")
        ce_ready = sem("ce_ready")
        xk_done = sem("xk_done")
        xk_ready = sem("xk_ready")
        xdt_ready = sem("xdt_ready")
        xw_ready = sem("xw_ready")
        st_done = sem("st_done")
        st_v = sem("st_v")
        st_ready = sem("st_ready")
        y_done = sem("y_done")
        y_read = sem("y_read")
        g_ready = sem("g_ready")
        sq_ready = sem("sq_ready")
        sq_used = sem("sq_used")
        rms_done = sem("rms_done")
        rms_in = sem("rms_in")
        rms_ready = sem("rms_ready")
        out_done = sem("out_done")
        out_read = sem("out_read")
        ln_v = sem("ln_v")
        var_ready = sem("var_ready")
        rstd_ready = sem("rstd_ready")
        x1_ready = sem("x1_ready")
        x1_out = sem("x1_out")

        block = ctx.enter_context(nc.Block())

        @block.sync
        def _(sp):
            for k in range(KT):
                if k:
                    sp.wait_ge(w_used, k)
                sp.dma_start(staging, winT[k * P:(k + 1) * P, :]).then_inc(w_in, 16)
                if k == 0:
                    sp.dma_start(cw[:, :, :], conv_w).then_inc(small_in, 16)
                    sp.dma_start(cb[:, :], conv_b).then_inc(small_in, 16)
                    sp.dma_start(nw[:, :], norm_w).then_inc(small_in, 16)
                    sp.dma_start(dtb[:, :], dt_bias.partition_broadcast(P)).then_inc(small_in, 16)
                    sp.dma_start(aneg[:, :], a_log.partition_broadcast(P)).then_inc(small_in, 16)
                    for half in range(2):
                        sp.dma_start(dcol[half * HP:(half + 1) * HP, :],
                                     d_skip[half].partition_broadcast(HP)
                                     ).then_inc(small_in, 16)
                    sp.dma_start(wout[:, :, :], woutT.rearrange("(c p) n -> p c n", p=P)).then_inc(small_in, 16)

            def sequence(b, first):
                for k in range(KT):
                    if k >= 2 or not first:
                        sp.wait_ge(xt_split, at(b, KT, k - 1))
                    sp.dma_start(xt_in[:, k % 2, :],
                                 one(xT, b)[:, k * P:(k + 1) * P, :].rearrange("a p n -> p (a n)")).then_inc(xt_landed[k % 2], 16)
                if not first:
                    sp.wait_ge(x1_out, at(b, 16 * TT, 0))
                sp.dma_start(x_tok[:, :, :], one(x, b).rearrange("a (t p) n -> p (a t) n", p=P)).then_inc(x_in, 16)
                for t in range(TT):
                    sp.wait_ge(x1_ready, at(b, TT, t + 1))
                    sp.dma_start(one(x1, b)[:, t * P:(t + 1) * P, :].rearrange("a p n -> p (a n)"),
                                 x_tok[:, t, :]).then_inc(x1_out, 16)

            over_sequences(sp, n_seq, sequence)
            sp.wait_ge(x1_out, 16 * TT * n_seq)

        @block.gpsimd
        def _(pool):
            pool.memset(onesf[:, :], 1.0).then_inc(const, 1)
            pool.memset(neg_half[:, :], -0.5).then_inc(const, 1)
            pool.wait_ge(const, 2)
            pool.affine_select(out=tri[:, :], in_=onesf[:, :], compare_op=ALU.is_ge, fill=0.0,
                               base=0, pattern=[[1, P]], channel_multiplier=-1).then_inc(const, 1)
            pool.affine_select(out=strict[:, :], in_=onesf[:, :], compare_op=ALU.is_ge, fill=0.0,
                               base=-1, pattern=[[-1, P]], channel_multiplier=1).then_inc(const, 1)
            pool.affine_select(out=ident[:, :], in_=onesf[:, :], compare_op=ALU.is_equal, fill=0.0,
                               base=0, pattern=[[-1, P]], channel_multiplier=1).then_inc(const, 1)
            pool.wait_ge(const, 5)

            def masked_decays(b, first, gr, c):
                if c >= 2:
                    if c == 2:
                        pool.wait_ge(seg_done, at(b, NG * CH, gr * CH + 1))
                    else:
                        pool.wait_ge(ebc_done, at(b, NG * (CH - 1), gr * (CH - 1) + 1))
                elif gr or not first:
                    pool.wait_ge(ebc_done, at(b, NG * (CH - 1), (gr - 1) * (CH - 1) + 2 + c))
                heads = slice(gr * HG, (gr + 1) * HG)
                shape = [P, HG, P]
                m = tri[:, :].unsqueeze(1).to_broadcast(shape)
                pool.tensor_tensor(rhs_hi[:, c % 2], a_hi[:, c, heads].unsqueeze(2).to_broadcast(shape), m, ALU.mult)
                pool.tensor_tensor(rhs_lo[:, c % 2], a_lo[:, c, heads].unsqueeze(2).to_broadcast(shape), m,
                                   ALU.mult).then_inc(rhs_ready, 1)

            def weighted_x(b, first, gr):
                pool.wait_ge(xk_ready, at(b, 2 * NG, 2 * gr + 2))
                if gr == 0:
                    pool.wait_ge(wdt_ready, at(b, 1, 1))
                if gr or not first:
                    pool.wait_ge(st_done, at(b, NG * (CH - 1), gr * (CH - 1)))
                w = wdt[:, 0:CH - 1, gr * HG:(gr + 1) * HG].unsqueeze(3).to_broadcast([P, CH - 1, HG, HP])
                pool.tensor_tensor(xw[:, :, :, :], xk[:, 0:CH - 1], w, ALU.mult).then_inc(xw_ready, 1)

            def sum_squares(b, first, gr):
                for j in range(2):
                    n = 2 * gr + j
                    if n == 0:
                        squares = value(pool, at(b, XT_TILES, 1))
                        met(pool, const, 5)
                        pool.wait_ge(sq_ready, squares)
                        if not first:
                            pool.wait_ge(rms_done, at(b, 1, 0))
                        pool.tensor_copy(ssum[:, :], sq[:, 0, :]).then_inc(sq_used, 1)
                    else:
                        pool.wait_ge(sq_ready, at(b, XT_TILES, n + 1))
                        pool.wait_ge(sq_used, at(b, XT_TILES, n))
                        pool.tensor_tensor(ssum[:, :], ssum[:, :], sq[:, j, :], ALU.add).then_inc(sq_used, 1)

            def sequence(b, first):
                pool.wait_ge(a_ready, at(b, 1, 1))
                for gr in range(NG):
                    for c in range(CH):
                        masked_decays(b, first, gr, c)
                    weighted_x(b, first, gr)
                    if gr:
                        sum_squares(b, first, gr - 1)
                sum_squares(b, first, NG - 1)
                pool.wait_ge(rms_in, at(b, 1, 1))
                pool.tensor_tensor(rms[:, 1], rms[:, 0], neg_half[:, :], ALU.pow).then_inc(rms_ready, 1)
                for t in range(TT):
                    pool.wait_ge(var_ready, at(b, TT, t + 1))
                    pool.tensor_tensor(rstd[:, 1, t:t + 1], rstd[:, 0, t:t + 1], neg_half[:, 0:1],
                                       ALU.pow).then_inc(rstd_ready, 1)

            over_sequences(pool, n_seq, sequence)

        @block.scalar
        def _(act):
            act.wait_ge(small_in, 16 * 8)
            act.activation(aneg[:, :], aneg[:, :], ACT.Exp).then_inc(setup_a, 1)

            def conv_tap0(b, n, tile, slot):
                act.wait_ge(tile_done, at(b, 18, tile + 1))
                act.activation(acc[:, slot, :], proj[tile % 2][:, :], ACT.Identity, bias=cb[:, n:n + 1],
                               scale=cw[:, n, 3:4]).then_inc(taps0, 1)

            def projections(b, first, gr):
                for j in range(2):
                    n = 2 * gr + j
                    if n == 0:
                        act.wait_ge(bc_ready, at(b, 1, 1))
                    elif n == 1:
                        if not first:
                            act.wait_ge(xc_ready, at(b, XT_TILES, 0))
                    else:
                        act.wait_ge(xc_ready, at(b, XT_TILES, n - 1))
                    conv_tap0(b, (DI // P) * 0 + n, 2 + 4 * gr + j, j)
                for j in range(2):
                    n = 2 * gr + j
                    act.wait_ge(conv_read, at(b, 9, n + 2))
                    if gr >= 2 or not first:
                        act.wait_ge(g_ready, at(b, XT_TILES, 2 * (gr - 2) + 2))
                    act.activation(xc[:, gr % 2, j, :], acc[:, j, :], ACT.Silu).then_inc(xc_ready, 1)
                for j in range(2):
                    act.wait_ge(tile_done, at(b, 18, 2 + 4 * gr + 2 + j + 1))
                    act.activation(zs[:, gr % 2, j, :], proj[j][:, :], ACT.Silu).then_inc(z_ready, 1)

            def decays(b, first, gr):
                for h in range(2):
                    act.wait_ge(xk_done, at(b, 2 * NG, 2 * gr + h + 1))
                    if h == 0 and (gr or not first):
                        act.wait_ge(xdt_ready, at(b, 2 * NG, 2 * gr))
                        act.wait_ge(xw_ready, at(b, NG, gr))
                    act.activation(xk[:, 2 * h:2 * h + 2].rearrange("p c h d -> p (c h d)"),
                                   turn[:, :], ACT.Copy).then_inc(xk_ready, 1)
                for c in range(CH):
                    act.wait_ge(seg_done, at(b, NG * CH, gr * CH + c + 1))
                    if c == 0 and (gr or not first):
                        act.wait_ge(y_done, at(b, XT_TILES, 2 * gr))
                    act.activation(dec[:, c], seg[c % 2][:, :], ACT.Exp).then_inc(dec_ready, 1)
                    if c:
                        act.wait_ge(ebc_done, at(b, NG * (CH - 1), gr * (CH - 1) + c))
                        act.activation(ce[:, c - 1], misc[0:NS, :], ACT.Exp).then_inc(e_ready, 1)

            def squares(b, first, gr):
                for j in range(2):
                    n = 2 * gr + j
                    act.wait_ge(g_ready, at(b, XT_TILES, n + 1))
                    if n >= 2 or not first:
                        act.wait_ge(sq_used, at(b, XT_TILES, n - 1))
                    act.activation(sq[:, j, :], g[:, n, :], ACT.Square).then_inc(sq_ready, 1)

            def sequence(b, first):
                act.wait_ge(tile_done, at(b, 18, 1))
                if not first:
                    act.wait_ge(dt_turned, at(b, 1, 0))
                act.activation(dt_ch[0:NH, :], proj[0][0:NH, :], ACT.Copy).then_inc(dt_read, 1)
                if not first:
                    act.wait_ge(xc_ready, at(b, XT_TILES, -1))
                conv_tap0(b, 8, 1, 0)
                act.wait_ge(conv_read, at(b, 9, 1))
                if not first:
                    act.wait_ge(bg_done, at(b, 1, 0))
                    act.wait_ge(ce_ready, at(b, NG * (CH - 1), 0))
                act.activation(bt[:, :], acc[0:NS, 0, :], ACT.Silu)
                act.activation(ct[:, :], acc[NS:P, 0, :], ACT.Silu).then_inc(bc_ready, 1)
                act.wait_ge(x_in, at(b, 16, 16))
                act.activation(x_tok[:, :, :], x_tok[:, :, :], ACT.Copy, scale=2.0).then_inc(x_dbl, 1)
                projections(b, first, 0)
                act.wait_ge(dtv, at(b, 14, 3))
                act.activation(sm[:, 2], sm[:, 1], ACT.Exp).then_inc(dta, 1)
                act.wait_ge(dtv, at(b, 14, 4))
                act.activation(sm[:, 4], sm[:, 3], ACT.Ln).then_inc(dta, 1)
                act.wait_ge(sums_done, at(b, 1, 1))
                if not first:
                    act.wait_ge(st_ready, at(b, NG * (CH - 1), 0))
                act.activation(wd[:, :, :, :].rearrange("p a c h -> p (a c h)"), turn[:, 0:2 * CH * NH],
                               ACT.Exp).then_inc(wd_ready, 1)
                for gr in range(NG):
                    decays(b, first, gr)
                    if gr + 1 < NG:
                        projections(b, first, gr + 1)
                    squares(b, first, gr)

            over_sequences(act, n_seq, sequence)

        @block.vector
        def _(dve):
            chain = Chain(dve, setup, 0)
            chain.start(0)
            dve.wait_ge(const, 5)
            dve.tensor_copy(strict_r[:, :], strict[:, :])
            dve.tensor_copy(ones_r[:, :], onesf[:, :])
            dve.wait_ge(setup_a, 1)
            dve.tensor_scalar(aneg[:, :], aneg[:, :], -1.0, -1e30, ALU.mult, ALU.max)
            for k in range(KT):
                dve.wait_ge(w_in, 16 * (k + 1))
                chain.link(dve.tensor_copy(win_hi[:, k, :], staging))
                dve.tensor_tensor(win_lo[:, k, :], staging, win_hi[:, k, :], ALU.subtract).then_inc(w_used, 1)
            for k in range(XT_TILES):
                ins = dve.tensor_scalar(wout[:, k, :], wout[:, k, :], nw[:, k:k + 1], None, ALU.mult)
            chain.link(ins)

            dt_chain = Chain(dve, dtv, 14)
            conv_chain = Chain(dve, conv_v, 18)
            st_chain = Chain(dve, st_v, 8)
            ln_chain = Chain(dve, ln_v, 2 * TT)

            def conv(b, n, tile, slot, done):
                dve.wait_ge(taps0, at(b, 9, done))
                for i in range(3):
                    s = i + 1
                    ins = dve.scalar_tensor_tensor(out=acc[:, slot, s:SEQ], in0=proj[tile % 2][:, 0:SEQ - s],
                                                   scalar=cw[:, n, 2 - i:3 - i], in1=acc[:, slot, s:SEQ],
                                                   op0=ALU.mult, op1=ALU.add)
                    if i < 2:
                        conv_chain.link(ins)
                ins.then_inc(conv_read, 1)

            def split_x(b, first):
                if not first:
                    dve.wait_ge(tile_done, at(b, 18, 0))
                for k in range(KT):
                    dve.wait_ge(xt_landed[k % 2], at(b, 16 * KT // 2, 16 * (k // 2 + 1)))
                    dve.tensor_copy(xt_hi[:, k, :], xt_in[:, k % 2, :]).then_inc(xt_hi_s, 1)
                    dve.wait_ge(xt_hi_s, at(b, KT, k + 1))
                    dve.tensor_tensor(xt_lo[:, k, :], xt_in[:, k % 2, :], xt_hi[:, k, :],
                                      ALU.subtract).then_inc(xt_split, 1)

            def step_sizes(b, first):
                dt_chain.start(b)
                sc = [sm[:, i] for i in range(8)]
                dve.wait_ge(dt_turned, at(b, 1, 1))
                if not first:
                    dve.wait_ge(rhs_ready, at(b, NG * CH, 0))
                    dve.wait_ge(xw_ready, at(b, NG, 0))
                dt_chain.link(dve.tensor_tensor(sc[0].rearrange("p (c h) -> p c h", h=NH),
                                                turn[:, 0:CH * NH].rearrange("p (c h) -> p c h", h=NH),
                                                dtb[:, :].unsqueeze(1).to_broadcast([P, CH, NH]), ALU.add))
                dt_chain.link(dve.tensor_scalar(sc[5], sc[0], -1.0, None, ALU.mult))
                dt_chain.link(dve.tensor_tensor(sc[1], sc[0], sc[5], ALU.min))
                dve.wait_ge(dta, at(b, 2, 1))
                dt_chain.link(dve.tensor_scalar(sc[3], sc[2], 1.0, None, ALU.add))
                dt_chain.link(dve.tensor_scalar(sc[7], sc[3], 1.0, None, ALU.is_equal))
                dt_chain.link(dve.scalar_tensor_tensor(out=sc[5], in0=sc[3], scalar=-1.0, in1=sc[7],
                                                       op0=ALU.add, op1=ALU.add))
                dt_chain.link(dve.reciprocal(sc[6], sc[5]))
                dve.wait_ge(dta, at(b, 2, 2))
                dt_chain.link(dve.tensor_tensor(sc[4], sc[4], sc[6], ALU.mult))
                dt_chain.link(dve.tensor_tensor(sc[5], sc[4], sc[7], ALU.add))
                dt_chain.link(dve.tensor_tensor(sc[6], sc[5], sc[2], ALU.mult))
                flat = dt[:, :, :].rearrange("p c h -> p (c h)")
                dt_chain.link(dve.scalar_tensor_tensor(out=flat, in0=sc[0], scalar=0.0, in1=sc[6],
                                                       op0=ALU.max, op1=ALU.add))
                dt_chain.link(dve.tensor_tensor(a[:, :, :], dt[:, :, :],
                                                aneg[:, :].unsqueeze(1).to_broadcast([P, CH, NH]), ALU.mult))
                dt_chain.link(dve.tensor_copy(a_hr[:, :, :], a[:, :, :]))
                dt_chain.link(dve.tensor_copy(a_hi[:, :, :], a_hr[:, :, :].bitcast(F32)))
                dve.tensor_tensor(a_lo[:, :, :], a[:, :, :], a_hi[:, :, :], ALU.subtract).then_inc(a_ready, 1)
                dt_chain.end()

            def group_factors(b, first, gr):
                heads = slice(gr * HG, (gr + 1) * HG)
                for h in range(2):
                    dve.wait_ge(xk_ready, at(b, 2 * NG, 2 * gr + h + 1))
                    if h == 0 and (gr or not first):
                        dve.wait_ge(y_done, at(b, XT_TILES, 2 * gr))
                    c = slice(2 * h, 2 * h + 2)
                    dve.tensor_tensor(xdt[:, c], xk[:, c], dt[:, c, heads].unsqueeze(3).to_broadcast([P, 2, HG, HP]),
                                      ALU.mult).then_inc(xdt_ready, 1)
                for c in range(CH):
                    dve.wait_ge(dec_ready, at(b, NG * CH, gr * CH + c + 1))
                    dve.tensor_tensor(dec[:, c], dec[:, c], gm[:, c, :].unsqueeze(1).to_broadcast([P, HG, P]),
                                      ALU.mult).then_inc(m_ready, 1)
                    if c:
                        dve.wait_ge(e_ready, at(b, NG * (CH - 1), gr * (CH - 1) + c))
                        dve.tensor_tensor(ce[:, c - 1], ce[:, c - 1],
                                          ct[:, c * P:(c + 1) * P].unsqueeze(1).to_broadcast([NS, HG, P]),
                                          ALU.mult).then_inc(ce_ready, 1)

            def states(b, first, gr):
                for c in range(CH - 1):
                    src = (turn[0:NS, c * 256:(c + 1) * 256] if c < 2 else misc[0:NS, 0:256])
                    src = src.rearrange("p (h d) -> p h d", h=HG)
                    dve.wait_ge(st_done, at(b, NG * (CH - 1), gr * (CH - 1) + max(c + 1, 2)))
                    if c == 0:
                        dve.tensor_copy(st[:, 0], src).then_inc(st_ready, 1)
                    else:
                        dve.wait_ge(st_ready, at(b, NG * (CH - 1), gr * (CH - 1) + c))
                        whole = wd[0:NS, 1, c, gr * HG:(gr + 1) * HG].unsqueeze(2).to_broadcast([NS, HG, HP])
                        st_chain.link(dve.tensor_tensor(st[:, c], st[:, c - 1], whole, ALU.mult))
                        dve.tensor_tensor(st[:, c], st[:, c], src, ALU.add).then_inc(st_ready, 1)

            def gate(b, first, gr):
                for j in range(2):
                    n = 2 * gr + j
                    dve.wait_ge(y_done, at(b, XT_TILES, n + 1))
                    if n == 0 and not first:
                        dve.wait_ge(out_done, at(b, TT, 0))
                    dve.scalar_tensor_tensor(out=g[:, n, :], in0=xc[:, gr % 2, j, :], scalar=dcol[:, n:n + 1],
                                             in1=yp[j][:, :], op0=ALU.mult, op1=ALU.add).then_inc(y_read, 1)
                for j in range(2):
                    n = 2 * gr + j
                    dve.wait_ge(z_ready, at(b, XT_TILES, n + 1))
                    dve.wait_ge(y_read, at(b, XT_TILES, n + 1))
                    dve.tensor_tensor(g[:, n, :], g[:, n, :], zs[:, gr % 2, j, :], ALU.mult).then_inc(g_ready, 1)

            def norm(b, first):
                ln_chain.start(b)
                dve.wait_ge(rms_done, at(b, 1, 1))
                dve.tensor_scalar(rms[:, 0], misc[:, 0:TT], 1.0 / DI, LN_EPS, ALU.mult, ALU.add).then_inc(rms_in, 1)
                dve.wait_ge(x_dbl, at(b, 1, 1))
                dve.wait_ge(rms_ready, at(b, 1, 1))

                def apply(t):
                    dve.wait_ge(rstd_ready, at(b, TT, t + 1))
                    dve.tensor_scalar(x_tok[:, t, :], x_tok[:, t, :], mv[:, t, 0:1], rstd[:, 1, t:t + 1],
                                      ALU.subtract, ALU.mult).then_inc(x1_ready, 1)

                for t in range(TT):
                    dve.wait_ge(out_done, at(b, TT, t + 1))
                    dve.scalar_tensor_tensor(out=x_tok[:, t, :], in0=proj[t % 2][:, :], scalar=rms[:, 1, t:t + 1],
                                             in1=x_tok[:, t, :], op0=ALU.mult, op1=ALU.add).then_inc(out_read, 1)
                    dve.wait_ge(out_read, at(b, TT, t + 1))
                    ln_chain.link(dve.bn_stats(stats[:, t, :], x_tok[:, t, :]), (const, 5))
                    ln_chain.link(dve.bn_aggr(mv[:, t, :], stats[:, t, :]))
                    dve.tensor_scalar(rstd[:, 0, t:t + 1], mv[:, t, 1:2], LN_EPS, None, ALU.add).then_inc(var_ready, 1)
                    if t:
                        apply(t - 1)
                apply(TT - 1)
                ln_chain.end()

            def sequence(b, first):
                st_chain.start(b)
                conv_chain.start(b)
                split_x(b, first)
                conv(b, 8, 1, 0, 1)
                conv(b, 0, 2, 0, 2)
                conv(b, 1, 3, 1, 3)
                dve.wait_ge(bg_done, at(b, 1, 1))
                dve.tensor_tensor(gm[:, :, :], misc[:, :].rearrange("p (c t) -> p c t", c=CH),
                                  tri[:, :].unsqueeze(1).to_broadcast([P, CH, P]), ALU.mult)
                dve.tensor_copy(b_tok[:, :, :].rearrange("p c n -> p (c n)"),
                                yp[0][:, 0:CH * NS]).then_inc(bg_read, 1)
                step_sizes(b, first)
                dve.wait_ge(wd_ready, at(b, 1, 1))
                dve.tensor_tensor(wdt[:, :, :], wd[:, 0], dt[:, :, :], ALU.mult).then_inc(wdt_ready, 1)
                for gr in range(NG):
                    group_factors(b, first, gr)
                    if gr + 1 < NG:
                        for j in range(2):
                            conv(b, 2 * gr + 2 + j, 2 + 4 * (gr + 1) + j, j, 2 * gr + 4 + j)
                    states(b, first, gr)
                    gate(b, first, gr)
                norm(b, first)
                conv_chain.end()
                st_chain.end()

            over_sequences(dve, n_seq, sequence)

        @block.tensor
        def _(pe):
            pe.wait_ge(w_used, KT)
            pe.wait_ge(setup, KT + 1)

            def in_proj(b, first, n, col):
                bank = proj[n % 2]
                if n == 0:
                    if not first:
                        pe.wait_ge(out_read, at(b, TT, -1))
                elif n == 1:
                    if not first:
                        pe.wait_ge(out_read, at(b, TT, 0))
                elif n == 2:
                    pe.wait_ge(dt_read, at(b, 1, 1))
                elif n == 3:
                    pe.wait_ge(conv_read, at(b, 9, 1))
                elif (n - 2) % 4 < 2:
                    pe.wait_ge(z_ready, at(b, XT_TILES, 2 * ((n - 2) // 4 - 1) + (n - 2) % 4 + 1))
                else:
                    pe.wait_ge(conv_read, at(b, 9, 2 * ((n - 2) // 4) + (n - 2) % 4 - 2 + 2))
                for k in range(KT):
                    if n == 0:
                        pe.wait_ge(xt_split, at(b, KT, k + 1))
                    wh, wl = win_hi[:, k, col:col + P], win_lo[:, k, col:col + P]
                    pe.matmul(bank[:, :], wh, xt_hi[:, k, :], start=(k == 0), stop=False)
                    pe.matmul(bank[:, :], wh, xt_lo[:, k, :], start=False, stop=False)
                    ins = pe.matmul(bank[:, :], wl, xt_hi[:, k, :], start=False, stop=(k == KT - 1))
                ins.then_inc(tile_done, 1)

            def group_projections(b, first, gr):
                for j in range(2):
                    in_proj(b, first, 2 + 4 * gr + j, COL_X + (2 * gr + j) * P)
                for j in range(2):
                    in_proj(b, first, 4 + 4 * gr + j, COL_Z + (2 * gr + j) * P)

            def decays(b, first, gr):
                for h in range(2):
                    if h == 0:
                        pe.wait_ge(xc_ready, at(b, XT_TILES, 2 * gr + 2))
                        if gr == 0:
                            pe.wait_ge(wd_ready, at(b, 1, 1))
                        else:
                            pe.wait_ge(st_ready, at(b, NG * (CH - 1), gr * (CH - 1)))
                    else:
                        pe.wait_ge(xk_ready, at(b, 2 * NG, 2 * gr + 1))
                    for c in range(2):
                        for j in range(2):
                            t0 = (2 * h + c) * P
                            ins = pe.transpose(turn[:, c * 256 + j * P:c * 256 + (j + 1) * P],
                                               xc[:, gr % 2, j, t0:t0 + P], ident[:, :])
                    ins.then_inc(xk_done, 1)
                for c in range(CH):
                    pe.wait_ge(rhs_ready, at(b, NG * CH, gr * CH + c + 1))
                    if gr or c >= 2 or not first:
                        pe.wait_ge(dec_ready, at(b, NG * CH, gr * CH + c - 1))
                    hi = rhs_hi[:, c % 2].rearrange("p h t -> p (h t)")
                    lo = rhs_lo[:, c % 2].rearrange("p h t -> p (h t)")
                    pe.matmul(seg[c % 2][:, :], strict_r[:, :], hi, start=True, stop=False)
                    pe.matmul(seg[c % 2][:, :], strict_r[:, :], lo, start=False, stop=True).then_inc(seg_done, 1)
                    if c:
                        if c > 1:
                            pe.wait_ge(e_ready, at(b, NG * (CH - 1), gr * (CH - 1) + c - 1))
                        elif gr == 0:
                            pe.wait_ge(bg_read, at(b, 1, 1))
                        pe.matmul(misc[:, :], ones_r[:, :], hi, start=True, stop=False)
                        pe.matmul(misc[:, :], ones_r[:, :], lo, start=False, stop=True).then_inc(ebc_done, 1)

            def outputs(b, first, gr):
                pe.wait_ge(xw_ready, at(b, NG, gr + 1))
                pe.wait_ge(e_ready, at(b, NG * (CH - 1), (gr + 1) * (CH - 1)))
                for c in range(CH - 1):
                    dst = turn[0:NS, c * 256:(c + 1) * 256] if c < 2 else misc[0:NS, 0:256]
                    pe.matmul(dst, b_tok[:, c, :], xw[:, c].rearrange("p h d -> p (h d)"),
                              start=True, stop=True).then_inc(st_done, 1)
                if gr or not first:
                    pe.wait_ge(y_read, at(b, XT_TILES, 2 * gr))
                if gr == 0:
                    pe.wait_ge(bg_read, at(b, 1, 1))
                pe.wait_ge(xdt_ready, at(b, 2 * NG, 2 * gr + 2))
                for c in range(CH):
                    pe.wait_ge(m_ready, at(b, NG * CH, gr * CH + c + 1))
                    for j in range(2):
                        for h in range(2):
                            pe.matmul(yp[j][h * HP:(h + 1) * HP, c * P:(c + 1) * P], xdt[:, c, 2 * j + h, :],
                                      dec[:, c, 2 * j + h, :], start=(c == 0), stop=False, skip_group_check=True)
                for j in range(2):
                    for c in range(1, CH):
                        if j == 0:
                            met(pe, w_used, KT)
                            pe.wait_ge(st_ready, at(b, NG * (CH - 1), gr * (CH - 1) + c))
                            pe.wait_ge(ce_ready, at(b, NG * (CH - 1), gr * (CH - 1) + c))
                        for h in range(2):
                            ins = pe.matmul(yp[j][h * HP:(h + 1) * HP, c * P:(c + 1) * P], st[:, c - 1, 2 * j + h, :],
                                            ce[:, c - 1, 2 * j + h, :], start=False, stop=(c == CH - 1),
                                            skip_group_check=True)
                    ins.then_inc(y_done, 1)

            def sequence(b, first):
                in_proj(b, first, 0, 0)
                in_proj(b, first, 1, COL_BC)
                turn_free = value(pe, at(b, NG * (CH - 1), 0))
                raw_dt = value(pe, at(b, 1, 1))
                met(pe, w_used, KT)
                pe.wait_ge(dt_read, raw_dt)
                if not first:
                    pe.wait_ge(st_ready, turn_free)
                for c in range(CH):
                    ins = pe.transpose(turn[:, c * NH:(c + 1) * NH], dt_ch[0:NH, c * P:(c + 1) * P],
                                       ident[0:NH, 0:NH])
                ins.then_inc(dt_turned, 1)
                group_projections(b, first, 0)
                pe.wait_ge(bc_ready, at(b, 1, 1))
                if not first:
                    pe.wait_ge(rms_in, at(b, 1, 0))
                    pe.wait_ge(y_read, at(b, XT_TILES, 0))
                for c in range(CH):
                    pe.matmul(misc[:, c * P:(c + 1) * P], bt[:, c * P:(c + 1) * P], ct[:, c * P:(c + 1) * P],
                              start=True, stop=True)
                for c in range(CH):
                    ins = pe.transpose(yp[0][:, c * NS:(c + 1) * NS], bt[:, c * P:(c + 1) * P], ident[0:NS, 0:NS])
                ins.then_inc(bg_done, 1)
                pe.wait_ge(a_ready, at(b, 1, 1))
                flat = a[:, :, :].rearrange("p c h -> p (c h)")
                pe.matmul(turn[:, 0:CH * NH], strict[:, :], flat, start=True, stop=True)
                pe.matmul(turn[:, CH * NH:2 * CH * NH], onesf[:, :], flat, start=True, stop=True).then_inc(sums_done, 1)
                for gr in range(NG):
                    decays(b, first, gr)
                    if gr + 1 < NG:
                        group_projections(b, first, gr + 1)
                    outputs(b, first, gr)
                pe.wait_ge(sq_used, at(b, XT_TILES, XT_TILES))
                pe.wait_ge(st_ready, at(b, NG * (CH - 1), NG * (CH - 1)))
                for t in range(TT):
                    ins = pe.matmul(misc[:, t:t + 1], ssum[:, t * P:(t + 1) * P], onesf[:, 0:1], start=True, stop=True)
                ins.then_inc(rms_done, 1)
                for t in range(TT):
                    if t < 2:
                        pe.wait_ge(z_ready, at(b, XT_TILES, XT_TILES - 1 + t))
                    else:
                        pe.wait_ge(out_read, at(b, TT, t - 1))
                    for k in range(XT_TILES):
                        ins = pe.matmul(proj[t % 2][:, :], g[:, k, t * P:(t + 1) * P], wout[:, k, :],
                                        start=(k == 0), stop=(k == XT_TILES - 1))
                    ins.then_inc(out_done, 1)

            over_sequences(pe, n_seq, sequence)


AH = 16
AD = DM // AH
AG = P // AD
STACK = 3 * AD
SOFT_SCALE = AD ** -0.5


def attention_order():
    order = [("xt", k, 0) for k in range(KT)] + [("qk", 0, 0), ("qk", 0, 1)]
    order += [("v", t, 0) for t in range(TT)]
    order += [("p1", 0, 0), ("qk", 1, 0), ("p1", 0, 1), ("qk", 1, 1), ("p1", 0, 2), ("p1", 0, 3), ("neg", 0, 0)]
    late = None
    for gr in range(KT):
        for u in range(TT):
            if gr + 1 < KT:
                order.append(("p1", gr + 1, u))
            order.append(("st", gr, u))
            if gr + 2 < KT and u < 2:
                order.append(("qk", gr + 2, u))
            if late:
                order.append(late)
            late = ("av", gr, u)
        if gr + 1 < KT:
            order.append(("neg", gr + 1, 0))
    order.append(late)
    return order + [("out", t, 0) for t in range(TT)]


def attention_stage(nc, n_seq, x1, ctxT, wT, b_col, b_row, x2):
    order = attention_order()
    uses = []
    for kind, i, j in order:
        if kind == "p1":
            uses += [(kind, i, j, h) for h in range(AG)]
        elif kind in ("xt", "qk", "v", "neg", "out"):
            uses.append((kind, i, j, 0))
    assert len(uses) % 2 == 0
    place = {use: n for n, use in enumerate(uses)}

    with ExitStack() as ctx:
        def sb(name, shape, dt=F32):
            return ctx.enter_context(nc.sbuf_tensor("a_" + name, shape, dt))

        def ps(name, shape=(P, 512)):
            return ctx.enter_context(nc.psum_tensor("a_" + name, list(shape), F32))

        def sem(name):
            return ctx.enter_context(nc.semaphore("a_" + name))

        names = ["q", "k", "v", "o"]
        w_hi = {n: sb(f"w{n}_hi", [P, KT, DM], F32R) for n in names}
        w_lo = {n: sb(f"w{n}_lo", [P, KT, DM], F32R) for n in names}
        bcol = sb("bcol", [P, 2, KT])
        brow = sb("brow", [P, 2, DM])
        ident = sb("ident", [P, P])
        onesf = sb("onesf", [P, P])
        neg_half = sb("neg_half", [P, 1])
        x_tok = sb("x_tok", [P, TT, DM])
        xt_hi = sb("xt_hi", [P, KT, SEQ], F32R)
        xt_lo = sb("xt_lo", [P, KT, SEQ], F32R)
        c_in = sb("c_in", [P, 2, SEQ])
        c_hi = sb("c_hi", [P, KT, SEQ], F32R)
        c_lo = sb("c_lo", [P, KT, SEQ], F32R)
        qkf = sb("qkf", [P, 2, SEQ])
        qk_hi = sb("qk_hi", [P, 2, SEQ], F32R)
        qk_lo = sb("qk_lo", [P, 2, SEQ], F32R)
        qs = sb("qs", [P, 2, AG, SEQ], F32R)
        ks = sb("ks", [P, 2, AG, SEQ], F32R)
        mx = sb("mx", [P, 2, TT, AG])
        neg_hi = sb("neg_hi", [AG, SEQ], F32R)
        neg_lo = sb("neg_lo", [AG, SEQ], F32R)
        v = sb("v", [P, TT, DM])
        probs = sb("probs", [P, 2, AG, SEQ])
        o = sb("o", [P, SEQ])
        den = sb("den", [P, SEQ])
        o_hi = sb("o_hi", [P, KT, SEQ], F32R)
        o_lo = sb("o_lo", [P, KT, SEQ], F32R)
        stats = sb("stats", [P, TT, 6])
        mv = sb("mv", [P, TT, 2])
        rstd = sb("rstd", [P, 2, TT])

        sp_banks = ps("scores", (P, AG, SEQ))
        shared = [ps("shared0"), ps("shared1")]
        o_bank, den_bank = ps("o_bank"), ps("den_bank")

        def bank(use):
            return shared[place[use] % 2]

        w_in = [sem("w_in0"), sem("w_in1")]
        w_used = sem("w_used")
        w_v = sem("w_v")
        small_in = sem("small_in")
        const = sem("const")
        ones_set = sem("ones_set")
        x_in = sem("x_in")
        c_landed = [sem("c_landed0"), sem("c_landed1")]
        c_hi_s = sem("c_hi_s")
        c_split = sem("c_split")
        xt_done = sem("xt_done")
        xt_hi_s = sem("xt_hi_s")
        xt_split = sem("xt_split")
        xb_ready = sem("xb_ready")
        qk_done = sem("qk_done")
        qk_hi_s = sem("qk_hi_s")
        qk_split = sem("qk_split")
        stack_in = [sem("stack_in0"), sem("stack_in1")]
        neg_in = [sem("neg_in0"), sem("neg_in1")]
        v_done = sem("v_done")
        v_ready = sem("v_ready")
        p1_done = sem("p1_done")
        mx_ready = sem("mx_ready")
        neg_done = sem("neg_done")
        neg_v = sem("neg_v")
        neg_ready = sem("neg_ready")
        st_done = sem("st_done")
        exp_ready = sem("exp_ready")
        av_done = sem("av_done")
        o_copied = sem("o_copied")
        o_v = sem("o_v")
        o_ready = sem("o_ready")
        out_done = sem("out_done")
        out_read = sem("out_read")
        ln_v = sem("ln_v")
        var_ready = sem("var_ready")
        rstd_ready = sem("rstd_ready")
        x2_ready = sem("x2_ready")
        x2_out = sem("x2_out")

        readers = {"xt": (xt_split, KT, lambda i, j, h: i + 1),
                   "qk": (qk_hi_s, 2 * KT, lambda i, j, h: 2 * i + j + 1),
                   "v": (v_ready, TT, lambda i, j, h: i + 1),
                   "p1": (mx_ready, AG * TT * KT, lambda i, j, h: AG * (TT * i + j) + h + 1),
                   "neg": (neg_ready, KT, lambda i, j, h: i + 1),
                   "out": (out_read, TT, lambda i, j, h: i + 1)}

        block = ctx.enter_context(nc.Block())

        @block.sync
        def _(sp):
            for i, n in enumerate(names):
                if i >= 2:
                    sp.wait_ge(w_used, i - 1)
                sp.dma_start(probs[:, i % 2], wT[i].rearrange("(k p) n -> p k n", p=P)).then_inc(w_in[i % 2], 16)
            sp.dma_start(bcol[:, :, :], b_col).then_inc(small_in, 16)
            for i in range(2):
                sp.dma_start(brow[:, i, :], b_row[i].partition_broadcast(P)).then_inc(small_in, 16)

            def sequence(b, first):
                for k in range(KT):
                    if k >= 2 or not first:
                        sp.wait_ge(c_split, at(b, KT, k - 1))
                    sp.dma_start(c_in[:, k % 2, :],
                                 one(ctxT, b)[:, k * P:(k + 1) * P, :].rearrange("a p n -> p (a n)")
                                 ).then_inc(c_landed[k % 2], 16)
                if not first:
                    sp.wait_ge(x2_out, at(b, 16 * TT, 0))
                sp.dma_start(x_tok[:, :, :], one(x1, b).rearrange("a (t p) n -> p (a t) n", p=P)).then_inc(x_in, 16)
                stacked = []
                for kind, i, j in order:
                    if kind == "qk":
                        stacked.append((i, j))
                    elif kind == "neg":
                        sp.wait_ge(neg_ready, at(b, KT, i + 1))
                        for r, part in enumerate((neg_hi, neg_lo)):
                            sp.dma_start(qs[STACK + r:STACK + r + 1, i % 2].bitcast(F32), part[:, :].bitcast(F32)).then_inc(neg_in[i % 2], 16)
                    while stacked and (stacked[0][0] < 2 or (kind, i, j) == ("st", stacked[0][0] - 2, TT - 1)):
                        gr, which = stacked.pop(0)
                        split = value(sp, at(b, 2 * KT, 2 * gr + which + 1))
                        if gr >= 2 or not first:
                            stack_free = value(sp, at(b, 2 * TT * KT, 2 * TT * (gr - 1)))
                        sp.wait_ge(qk_split, split)
                        if gr >= 2 or not first:
                            sp.wait_ge(st_done, stack_free)
                        parts = (qk_hi, qk_hi, qk_lo) if which else (qk_hi, qk_lo, qk_hi)
                        for r, part in enumerate(parts):
                            dst = (ks if which else qs)[r * AD:(r + 1) * AD, gr % 2]
                            for h in range(AG):
                                sp.dma_start(dst[:, h, :].bitcast(F32),
                                             part[h * AD:(h + 1) * AD, which, :].bitcast(F32)).then_inc(stack_in[gr % 2], 16)
                for t in range(TT):
                    sp.wait_ge(x2_ready, at(b, TT, t + 1))
                    sp.dma_start(one(x2, b)[:, t * P:(t + 1) * P, :].rearrange("a p n -> p (a n)"),
                                 x_tok[:, t, :]).then_inc(x2_out, 16)

            over_sequences(sp, n_seq, sequence)
            sp.wait_ge(x2_out, 16 * TT * n_seq)

        @block.gpsimd
        def _(pool):
            pool.memset(onesf[:, :], 1.0).then_inc(const, 1)
            pool.memset(neg_half[:, :], -0.5).then_inc(const, 1)
            pool.wait_ge(const, 2)
            pool.affine_select(out=ident[:, :], in_=onesf[:, :], compare_op=ALU.is_equal, fill=0.0,
                               base=0, pattern=[[-1, P]], channel_multiplier=1).then_inc(const, 1)
            pool.wait_ge(small_in, 48)

            def sequence(b, first):
                pool.wait_ge(xt_done, at(b, KT, KT))
                pool.tensor_tensor(x_tok[:, :, :], x_tok[:, :, :],
                                   brow[:, 1, :].unsqueeze(1).to_broadcast([P, TT, DM]), ALU.add).then_inc(xb_ready, 1)
                for t in range(TT):
                    pool.wait_ge(var_ready, at(b, TT, t + 1))
                    pool.tensor_tensor(rstd[:, 1, t:t + 1], rstd[:, 0, t:t + 1], neg_half[:, :],
                                       ALU.pow).then_inc(rstd_ready, 1)

            over_sequences(pool, n_seq, sequence)

        @block.scalar
        def _(act):
            act.wait_ge(small_in, 48)

            def sequence(b, first):
                if not first:
                    act.wait_ge(qk_done, at(b, 2 * KT, 0))
                for k in range(KT):
                    act.wait_ge(c_landed[k % 2], at(b, 8 * KT, 16 * (k // 2 + 1)))
                    act.activation(c_hi[:, k, :], c_in[:, k % 2, :], ACT.Copy).then_inc(c_hi_s, 1)
                for kind, i, j in order:
                    if kind == "xt":
                        act.wait_ge(xt_done, at(b, KT, i + 1))
                        act.activation(xt_hi[:, i, :], bank((kind, i, j, 0))[:, :], ACT.Copy).then_inc(xt_hi_s, 1)
                    elif kind == "qk":
                        n = 2 * i + j
                        act.wait_ge(qk_done, at(b, 2 * KT, n + 1))
                        if n >= 2 or not first:
                            act.wait_ge(qk_split, at(b, 2 * KT, n - 1))
                            act.wait_ge(stack_in[(i - 1) % 2],
                                        at(b, 16 * 6 * AG * KT // 2, 16 * 6 * AG * ((i + 1) // 2)))
                        src = bank((kind, i, j, 0))[:, :]
                        act.activation(qkf[:, j, :], src, ACT.Identity, bias=bcol[:, j, i:i + 1])
                        act.activation(qk_hi[:, j, :], src, ACT.Identity, bias=bcol[:, j, i:i + 1]
                                       ).then_inc(qk_hi_s, 1)
                    elif kind == "st":
                        u = TT * i + j
                        for half in range(2):
                            act.wait_ge(st_done, at(b, 2 * TT * KT, 2 * u + half + 1))
                            if half == 0 and (u >= 2 or not first):
                                act.wait_ge(av_done, at(b, TT * KT, u - 1))
                            act.activation(probs[:, u % 2, 2 * half:2 * half + 2],
                                           sp_banks[:, 2 * half:2 * half + 2], ACT.Exp,
                                           scale=SOFT_SCALE).then_inc(exp_ready, 1)
                    elif kind == "av" and j == TT - 1:
                        act.wait_ge(av_done, at(b, TT * KT, TT * (i + 1)))
                        if i or not first:
                            act.wait_ge(o_ready, at(b, KT, i))
                        act.activation(o[:, :], o_bank[:, :], ACT.Copy)
                        act.activation(den[:, :], den_bank[:, :], ACT.Copy).then_inc(o_copied, 1)

            over_sequences(act, n_seq, sequence)

        @block.vector
        def _(dve):
            wchain = Chain(dve, w_v, 0)
            wchain.start(0)
            for i, n in enumerate(names):
                dve.wait_ge(w_in[i % 2], 16 * (i // 2 + 1))
                wchain.link(dve.tensor_copy(w_hi[n][:, :, :], probs[:, i % 2]))
                dve.tensor_tensor(w_lo[n][:, :, :], probs[:, i % 2], w_hi[n][:, :, :],
                                  ALU.subtract).then_inc(w_used, 1)
            dve.memset(ks[STACK:P, :, :, :].bitcast(F32), 1.0).then_inc(ones_set, 1)
            neg_chain = Chain(dve, neg_v, KT)
            o_chain = Chain(dve, o_v, 3 * KT)
            ln_chain = Chain(dve, ln_v, 2 * TT)

            def sequence(b, first):
                for c in (neg_chain, o_chain, ln_chain):
                    c.start(b)
                for k in range(KT):
                    dve.wait_ge(c_hi_s, at(b, KT, k + 1))
                    dve.tensor_tensor(c_lo[:, k, :], c_in[:, k % 2, :], c_hi[:, k, :],
                                      ALU.subtract).then_inc(c_split, 1)
                for kind, i, j in order:
                    if kind == "xt":
                        dve.wait_ge(xt_hi_s, at(b, KT, i + 1))
                        dve.tensor_tensor(xt_lo[:, i, :], bank((kind, i, j, 0))[:, :], xt_hi[:, i, :],
                                          ALU.subtract).then_inc(xt_split, 1)
                    elif kind == "qk":
                        n = 2 * i + j
                        dve.wait_ge(qk_hi_s, at(b, 2 * KT, n + 1))
                        dve.tensor_tensor(qk_lo[:, j, :], qkf[:, j, :], qk_hi[:, j, :],
                                          ALU.subtract).then_inc(qk_split, 1)
                    elif kind == "v":
                        dve.wait_ge(v_done, at(b, TT, i + 1))
                        if i == 0:
                            dve.wait_ge(small_in, 48)
                            if not first:
                                dve.wait_ge(av_done, at(b, TT * KT, 0))
                        dve.tensor_tensor(v[:, i, :], bank((kind, i, j, 0))[:, :], brow[:, 0, :],
                                          ALU.add).then_inc(v_ready, 1)
                    elif kind == "p1":
                        for h in range(AG):
                            n = AG * (TT * i + j) + h
                            dve.wait_ge(p1_done, at(b, AG * TT * KT, n + 1))
                            if h == 0 and j == 0 and (i >= 2 or not first):
                                dve.wait_ge(neg_done, at(b, KT, i - 1))
                            dve.tensor_reduce(mx[:, i % 2, j, h:h + 1], bank((kind, i, j, h))[:, :], AX.X,
                                              ALU.max).then_inc(mx_ready, 1)
                    elif kind == "neg":
                        dve.wait_ge(neg_done, at(b, KT, i + 1))
                        if i or not first:
                            dve.wait_ge(neg_in[(i - 1) % 2], at(b, 32 * KT // 2, 32 * ((i + 1) // 2)))
                        src = bank((kind, i, j, 0))[0:AG, :]
                        neg_chain.link(dve.tensor_scalar(neg_hi[:, :], src, -1.0, None, ALU.mult))
                        dve.scalar_tensor_tensor(out=neg_lo[:, :], in0=src, scalar=-1.0, in1=neg_hi[:, :].bitcast(F32),
                                                 op0=ALU.mult, op1=ALU.subtract).then_inc(neg_ready, 1)
                    elif kind == "av" and j == TT - 1:
                        dve.wait_ge(o_copied, at(b, KT, i + 1))
                        if i == 0 and not first:
                            dve.wait_ge(out_done, at(b, TT, 0))
                        o_chain.link(dve.reciprocal(den[:, :], den[:, :]))
                        o_chain.link(dve.tensor_tensor(o[:, :], o[:, :], den[:, :], ALU.mult))
                        o_chain.link(dve.tensor_copy(o_hi[:, i, :], o[:, :]))
                        dve.tensor_tensor(o_lo[:, i, :], o[:, :], o_hi[:, i, :].bitcast(F32),
                                          ALU.subtract).then_inc(o_ready, 1)

                def apply(t):
                    dve.wait_ge(rstd_ready, at(b, TT, t + 1))
                    dve.tensor_scalar(x_tok[:, t, :], x_tok[:, t, :], mv[:, t, 0:1], rstd[:, 1, t:t + 1],
                                      ALU.subtract, ALU.mult).then_inc(x2_ready, 1)

                dve.wait_ge(xb_ready, at(b, 1, 1))
                for t in range(TT):
                    dve.wait_ge(out_done, at(b, TT, t + 1))
                    dve.tensor_tensor(x_tok[:, t, :], bank(("out", t, 0, 0))[:, :], x_tok[:, t, :],
                                      ALU.add).then_inc(out_read, 1)
                    dve.wait_ge(out_read, at(b, TT, t + 1))
                    ln_chain.link(dve.bn_stats(stats[:, t, :], x_tok[:, t, :]), (const, 3))
                    ln_chain.link(dve.bn_aggr(mv[:, t, :], stats[:, t, :]))
                    dve.tensor_scalar(rstd[:, 0, t:t + 1], mv[:, t, 1:2], LN_EPS, None, ALU.add).then_inc(var_ready, 1)
                    if t:
                        apply(t - 1)
                apply(TT - 1)
                for c in (neg_chain, o_chain, ln_chain):
                    c.end()

            over_sequences(dve, n_seq, sequence)

        @block.tensor
        def _(pe):
            pe.wait_ge(const, 3)
            pe.wait_ge(ones_set, 1)

            def take(b, first, use):
                n = place[use]
                if n < 2 and first:
                    return
                kind, i, j, h = uses[n - 2]
                s, per, count = readers[kind]
                pe.wait_ge(s, at(b, per, count(i, j, h) - (per if n < 2 else 0)))

            def project(b, first, use, w, x_parts, cols, w_moves, done):
                take(b, first, use)
                wh, wl = w
                for k in range(KT):
                    for n, (wp, xp) in enumerate(((wh, x_parts[0]), (wh, x_parts[1]), (wl, x_parts[0]))):
                        pair = ((xp[:, k, cols], wp[:, k, :]) if w_moves else (wp[:, k, cols], xp[:, k, :]))
                        ins = pe.matmul(bank(use)[:, :], *pair, start=(k == n == 0), stop=(k == KT - 1 and n == 2))
                ins.then_inc(done, 1)

            def sequence(b, first):
                pe.wait_ge(x_in, at(b, 16, 16))
                for kind, i, j in order:
                    tile = slice(i * P, (i + 1) * P)
                    use = (kind, i, j, 0)
                    if kind == "xt":
                        take(b, first, use)
                        for t in range(TT):
                            ins = pe.transpose(bank(use)[:, t * P:(t + 1) * P], x_tok[:, t, tile], ident[:, :])
                        ins.then_inc(xt_done, 1)
                    elif kind == "qk":
                        if i == 0:
                            pe.wait_ge(*((c_split, at(b, KT, KT)) if j else (xt_split, at(b, KT, KT))))
                        n = names[j]
                        project(b, first, use, (w_hi[n], w_lo[n]), (c_hi, c_lo) if j else (xt_hi, xt_lo),
                                tile, False, qk_done)
                    elif kind == "v":
                        project(b, first, use, (w_hi["v"], w_lo["v"]), (c_hi, c_lo), tile, True, v_done)
                    elif kind == "p1":
                        if j == 0:
                            pe.wait_ge(stack_in[i % 2], at(b, 16 * 6 * AG * KT // 2, 16 * 6 * AG * (i // 2 + 1)))
                        for h in range(AG):
                            use = (kind, i, j, h)
                            take(b, first, use)
                            pe.matmul(bank(use)[:, :], qs[0:STACK, i % 2, h, j * P:(j + 1) * P],
                                      ks[0:STACK, i % 2, h, :], start=True, stop=True).then_inc(p1_done, 1)
                    elif kind == "neg":
                        take(b, first, use)
                        pe.wait_ge(mx_ready, at(b, AG * TT * KT, AG * TT * (i + 1)))
                        for t in range(TT):
                            ins = pe.transpose(bank(use)[0:AG, t * P:(t + 1) * P], mx[:, i % 2, t, :], ident[:, :])
                        ins.then_inc(neg_done, 1)
                    elif kind == "st":
                        u = TT * i + j
                        if j == 0:
                            pe.wait_ge(neg_in[i % 2], at(b, 32 * KT // 2, 32 * (i // 2 + 1)))
                        for h in range(AG):
                            if h % 2 == 0 and (u or not first):
                                pe.wait_ge(exp_ready, at(b, 2 * TT * KT, 2 * u + h // 2 - 1))
                            ins = pe.matmul(sp_banks[:, h, :], ks[0:STACK + 2, i % 2, h, j * P:(j + 1) * P],
                                            qs[0:STACK + 2, i % 2, h, :], start=True, stop=True)
                            if h % 2:
                                ins.then_inc(st_done, 1)
                    elif kind == "av":
                        u = TT * i + j
                        pe.wait_ge(exp_ready, at(b, 2 * TT * KT, 2 * u + 2))
                        if u == 0:
                            pe.wait_ge(v_ready, at(b, TT, TT))
                        if j == 0 and (i or not first):
                            pe.wait_ge(o_copied, at(b, KT, i))
                        for h in range(AG):
                            rows = slice(h * AD, (h + 1) * AD)
                            pe.matmul(o_bank[rows, :], v[:, j, i * P + h * AD:i * P + (h + 1) * AD],
                                      probs[:, u % 2, h, :], start=(j == 0), stop=(j == TT - 1))
                        for h in range(AG):
                            rows = slice(h * AD, (h + 1) * AD)
                            ins = pe.matmul(den_bank[rows, :], onesf[:, 0:AD], probs[:, u % 2, h, :],
                                            start=(j == 0), stop=(j == TT - 1))
                        ins.then_inc(av_done, 1)
                    elif kind == "out":
                        if i == 0:
                            pe.wait_ge(o_ready, at(b, KT, KT))
                        project(b, first, use, (w_hi["o"], w_lo["o"]), (o_hi, o_lo), tile, True, out_done)

            over_sequences(pe, n_seq, sequence)


NE = 16
SL = 16
SLOTS = NE * SL
ST_TILES = SLOTS // P
EH = 128
W_SLOTS = 4
NORM_EPS = 1e-12


def is_zero(b):
    return isinstance(b, int) and b == 0


def at_pair(b, p, per):
    return (b - p) * (per // 2) + per


def over_pairs(eng, count, front, back):
    front(0, 0, True)
    front(1, 1, True)
    back(0, 0, True)
    if count > 2:
        with eng.Fori(0, count // 2 - 1) as i:
            front(i * 2 + 2, 0, False)
            back(i * 2 + 1, 1, False)
            front(i * 2 + 3, 1, False)
            back(i * 2 + 2, 0, False)
    back(count - 1, 1, False)


def nothing(b, p):
    pass


def over_routed(eng, count, turn=nothing, start=nothing, back=nothing, mid=nothing):
    def step(b, p, before):
        turn(before, 1 - p)
        start(b, p)
        back(before, 1 - p)
        mid(b, p)

    start(0, 0)
    mid(0, 0)
    step(1, 1, 0)
    if count > 2:
        with eng.Fori(1, count // 2) as i:
            step(i * 2, 0, i * 2 - 1)
            step(i * 2 + 1, 1, i * 2)
    turn(count - 1, 1)
    back(count - 1, 1)


def moe_stage(nc, n_seq, x2, gamma, beta, mu, scale, w1, b1, w2, b2, combine_t, slot_out, x3):
    with ExitStack() as ctx:
        def sb(name, shape, dt=F32):
            return ctx.enter_context(nc.sbuf_tensor("e_" + name, shape, dt))

        def ps(name, shape=(P, 512)):
            return ctx.enter_context(nc.psum_tensor("e_" + name, list(shape), F32))

        def sem(name):
            return ctx.enter_context(nc.semaphore("e_" + name))

        grow = sb("grow", [P, DM])
        berow = sb("berow", [P, DM])
        mu_u = sb("mu_u", [P, KT, SLOTS])
        mu_sq = sb("mu_sq", [P, KT, SLOTS])
        mu_n = sb("mu_n", [P, 2, SLOTS])
        scol = sb("scol", [P, 1])
        b1col = sb("b1col", [P, NE])
        b2t = sb("b2t", [P, ST_TILES, DM])
        ident = sb("ident", [P, P])
        onesf = sb("onesf", [P, P])
        neg_half = sb("neg_half", [P, SLOTS])
        x = sb("x", [P, 2, TT, DM])
        stats = sb("stats", [P, TT, 6])
        mv = sb("mv", [P, TT, 2])
        rstd = sb("rstd", [P, 2, TT])
        junk = sb("junk", [P, TT, DM])
        ss = sb("ss", [P, 3, TT])
        rs = sb("rs", [P, TT])
        xnt = sb("xnt", [P, KT, SEQ])
        lg = sb("lg", [P, TT, SLOTS])
        disp_t = sb("disp_t", [P, ST_TILES, SEQ])
        disp = sb("disp", [P, TT, SLOTS])
        comb = sb("comb", [P, TT, SLOTS])
        mxd = sb("mxd", [P, 2, ST_TILES])
        sd = sb("sd", [P, 2, ST_TILES])
        mxc = sb("mxc", [P, TT])
        neg_mxc = sb("neg_mxc", [P, TT])
        sc = sb("sc", [P, TT])
        rc_all = sb("rc_all", [P, n_seq, TT])
        comb_t = sb("comb_t", [P, ST_TILES, SEQ])
        slots_t = sb("slots_t", [P, KT, NE, n_seq, SL])
        w1s = sb("w1s", [P, W_SLOTS, KT, EH])
        w2s = sb("w2s", [P, W_SLOTS, DM])
        hs = sb("hs", [P, 2, P])
        so = sb("so", [P, 2, DM])
        so_in = sb("so_in", [P, 2, ST_TILES, DM])
        ct_in = sb("ct_in", [P, 2, ST_TILES, SEQ])
        rows = n_seq * SL

        turn = [ps("turn0"), ps("turn1")]
        lg_ps = ps("lg_ps", (P, TT, SLOTS))
        sl_ps = ps("sl_ps", (P, KT, SLOTS))
        ct_ps = ps("ct_ps", (P, ST_TILES, SEQ))

        const = sem("const")
        small_in = sem("small_in")
        mu_s = sem("mu_s")
        mu_ready = sem("mu_ready")
        x_in = [sem("x_in0"), sem("x_in1")]
        r_in = [sem("r_in0"), sem("r_in1")]
        st_v = sem("st_v")
        var_ready = sem("var_ready")
        rstd_ready = sem("rstd_ready")
        xg_ready = sem("xg_ready")
        xn_ready = sem("xn_ready")
        ss_ready = sem("ss_ready")
        ssb_ready = sem("ssb_ready")
        rn_ready = sem("rn_ready")
        rs_ready = sem("rs_ready")
        turn_done = sem("turn_done")
        turn_read = sem("turn_read")
        lg_done = sem("lg_done")
        lg_read = sem("lg_read")
        mx_ready = sem("mx_ready")
        mc_ready = sem("mc_ready")
        dn_ready = sem("dn_ready")
        disp_turned = sem("disp_turned")
        comb_ready = sem("comb_ready")
        disp_ready = sem("disp_ready")
        ln1_v = sem("ln1_v")
        sums_v = sem("sums_v")
        rc_ready = sem("rc_ready")
        ct_done = sem("ct_done")
        ct_read = sem("ct_read")
        ct_out = sem("ct_out")
        sl_done = sem("sl_done")
        sl_read = sem("sl_read")
        w_in = [sem(f"w_in{i}") for i in range(W_SLOTS)]
        h_done = sem("h_done")
        h_ready = sem("h_ready")
        e_done = sem("e_done")
        so_ready = sem("so_ready")
        so_out = [sem("so_out0"), sem("so_out1")]
        mu_done = sem("mu_done")
        c_in = [sem("c_in0"), sem("c_in1")]
        b2_added = sem("b2_added")
        out_done = sem("out_done")
        out_read = sem("out_read")
        ln_v = sem("ln_v")
        var2_ready = sem("var2_ready")
        rstd2_ready = sem("rstd2_ready")
        x3_ready = sem("x3_ready")
        x3_out = sem("x3_out")

        out_banks = [sl_ps[:, 0:2, :], sl_ps[:, 2:4, :], ct_ps[:, 0, :], ct_ps[:, 1, :]]

        def out_bank(e):
            return out_banks[e % 2].rearrange("p a n -> p (a n)")

        def c_bank(t):
            return out_bank(t) if t < 2 else out_banks[t]

        def second(pe, e):
            pe.wait_ge(h_ready, e + 1)
            if e >= 2:
                pe.wait_ge(so_ready, e - 1)
            pe.matmul(out_bank(e)[0:rows, :], hs[:, e % 2, 0:rows], w2s[:, e % W_SLOTS, :],
                      start=True, stop=True).then_inc(e_done, 1)

        block = ctx.enter_context(nc.Block())
        N_SMALL = 5 + NE
        TURNS = KT + ST_TILES

        @block.sync
        def _(sp):
            sp.dma_start(mu_u[:, :, :], mu.rearrange("(k p) n -> p k n", p=P)).then_inc(small_in, 16)
            sp.dma_start(grow[:, :], gamma.partition_broadcast(P)).then_inc(small_in, 16)
            sp.dma_start(berow[:, :], beta.partition_broadcast(P)).then_inc(small_in, 16)
            sp.dma_start(scol[:, :], scale.partition_broadcast(P)).then_inc(small_in, 16)
            sp.dma_start(b1col[:, :], b1).then_inc(small_in, 16)
            for e in range(NE):
                e0 = (e * SL) % P
                sp.dma_start(b2t[e0:e0 + SL, e * SL // P, :], b2[e].partition_broadcast(SL)).then_inc(small_in, 16)

            def load_expert(e):
                s = e % W_SLOTS
                if e >= W_SLOTS:
                    sp.wait_ge(e_done, e - W_SLOTS + 1)
                sp.dma_start(w1s[:, s], w1[e].rearrange("(k p) h -> p k h", p=P)).then_inc(w_in[s], 16)
                sp.dma_start(w2s[:, s], w2[e]).then_inc(w_in[s], 16)

            def store(e):
                sp.wait_ge(so_ready, e + 1)
                sp.dma_start(slot_out[e].rearrange("b s d -> (b s) d"), so[0:rows, e % 2, :]
                             ).then_inc(so_out[e % 2], 16)

            for e in range(W_SLOTS):
                load_expert(e)

            def load_x(b, p, landed):
                sp.dma_start(x[:, p], one(x2, b).rearrange("a (t p) n -> p (a t) n", p=P)).then_inc(landed[p], 16)

            def start(b, p):
                if not (isinstance(b, int) and b < 2):
                    sp.wait_ge(sl_done, at(b, 1, -1))
                load_x(b, p, x_in)

            def back(b, p):
                sp.wait_ge(ct_read, at(b, ST_TILES, ST_TILES))
                sp.dma_start(one(combine_t, b).rearrange("a (j p) n -> p (a j) n", p=P), comb_t[:, :, :]
                             ).then_inc(ct_out, 16)

            over_routed(sp, n_seq, start=start, back=back)

            for e in range(NE):
                if e >= W_SLOTS:
                    load_expert(e)
                store(e - 1) if e else None
            store(NE - 1)
            for p in range(2):
                sp.wait_ge(so_out[p], 16 * NE // 2)
            sp.wait_ge(ct_out, 16 * n_seq)

            def combine(b, p, first):
                if not first:
                    sp.wait_ge(out_done, at(b, TT, -TT))
                    sp.wait_ge(x3_out, at(b, 16 * TT, -16 * TT))
                src = slot_out.rearrange("e b s d -> b e s d")
                for j in range(ST_TILES):
                    n = P // SL
                    for e in range(n):
                        sp.dma_start(so_in[e * SL:(e + 1) * SL, p, j, :],
                                     one(src, b)[:, j * n + e].rearrange("a s d -> (a s) d")).then_inc(c_in[p], 16)
                sp.dma_start(ct_in[:, p], one(combine_t, b).rearrange("a (j p) n -> p (a j) n", p=P)
                             ).then_inc(c_in[p], 16)
                load_x(b, p, r_in)

            def stores(b, p, first):
                for t in range(TT):
                    sp.wait_ge(x3_ready, at(b, TT, t + 1))
                    sp.dma_start(one(x3, b)[:, t * P:(t + 1) * P, :].rearrange("a p n -> p (a n)"),
                                 x[:, p, t, :]).then_inc(x3_out, 16)

            over_pairs(sp, n_seq, combine, stores)
            sp.wait_ge(x3_out, 16 * TT * n_seq)

        @block.gpsimd
        def _(pool):
            pool.memset(onesf[:, :], 1.0).then_inc(const, 1)
            pool.memset(neg_half[:, :], -0.5).then_inc(const, 1)
            pool.wait_ge(const, 2)
            pool.affine_select(out=ident[:, :], in_=onesf[:, :], compare_op=ALU.is_equal, fill=0.0,
                               base=0, pattern=[[-1, P]], channel_multiplier=1).then_inc(const, 1)
            pool.wait_ge(mu_s, 2)
            pool.tensor_tensor(mu_n[:, 1], mu_n[:, 0], neg_half[:, :], ALU.pow).then_inc(mu_s, 1)

            def start(b, p):
                pool.wait_ge(var_ready, at(b, 1, 1))
                pool.tensor_tensor(rstd[:, 1], rstd[:, 0], neg_half[:, 0:TT], ALU.pow).then_inc(rstd_ready, 1)
                pool.wait_ge(xg_ready, at(b, 1, 1))
                pool.tensor_tensor(x[:, p], x[:, p], berow[:, :].unsqueeze(1).to_broadcast([P, TT, DM]),
                                   ALU.add).then_inc(xn_ready, 1)
                pool.wait_ge(ssb_ready, at(b, 1, 1))
                pool.tensor_tensor(ss[:, 2], ss[:, 1], neg_half[:, 0:TT], ALU.pow).then_inc(rn_ready, 1)

            over_routed(pool, n_seq, start=start)

            def combine(b, p, first):
                pool.wait_ge(c_in[p], at_pair(b, p, 16 * (NE + 1)))
                pool.tensor_tensor(so_in[:, p], so_in[:, p], b2t[:, :, :], ALU.add).then_inc(b2_added, 1)

            def powers(b, p, first):
                for t in range(TT):
                    pool.wait_ge(var2_ready, at(b, TT, t + 1))
                    pool.tensor_tensor(rstd[:, 1, t:t + 1], rstd[:, 0, t:t + 1], neg_half[:, 0:1],
                                       ALU.pow).then_inc(rstd2_ready, 1)

            over_pairs(pool, n_seq, combine, powers)

        @block.scalar
        def _(act):
            act.wait_ge(small_in, 16 * N_SMALL)
            act.activation(mu_sq[:, :, :], mu_u[:, :, :], ACT.Square).then_inc(mu_s, 1)

            def start(b, p):
                act.wait_ge(xn_ready, at(b, 1, 1))
                for t in range(TT):
                    ins = act.activation(junk[:, t, :], x[:, p, t, :], ACT.Square, accum_out=ss[:, 0, t:t + 1])
                ins.then_inc(ss_ready, 1)
                for k in range(KT):
                    act.wait_ge(turn_done, at(b, TURNS, k + 1))
                    act.activation(xnt[:, k, :], turn[k % 2][:, :], ACT.Copy).then_inc(turn_read, 1)
                act.wait_ge(lg_done, at(b, 1, 1))
                act.wait_ge(rs_ready, at(b, 1, 1))
                for t in range(TT):
                    ins = act.activation(lg[:, t, :], lg_ps[:, t, :], ACT.Identity, scale=rs[:, t:t + 1])
                ins.then_inc(lg_read, 1)

            def back(b, p):
                for j in range(ST_TILES):
                    act.wait_ge(ct_done, at(b, ST_TILES, j + 1))
                    if j == 0 and not is_zero(b):
                        act.wait_ge(ct_out, at(b, 16, 0))
                    act.activation(comb_t[:, j, :], ct_ps[:, j, :], ACT.Copy).then_inc(ct_read, 1)

            def mid(b, p):
                for j in range(ST_TILES):
                    act.wait_ge(turn_done, at(b, TURNS, KT + j + 1))
                    act.wait_ge(mx_ready, at(b, ST_TILES, j + 1))
                    act.activation(disp_t[:, j, :], turn[j % 2][:, :], ACT.Exp, bias=mxd[:, 1, j:j + 1],
                                   accum_out=sd[:, 0, j:j + 1]).then_inc(turn_read, 1)
                act.wait_ge(mc_ready, at(b, 1, 1))
                for t in range(TT):
                    ins = act.activation(comb[:, t, :], lg[:, t, :], ACT.Exp, bias=neg_mxc[:, t:t + 1],
                                         accum_out=sc[:, t:t + 1])
                ins.then_inc(comb_ready, 1)

            over_routed(act, n_seq, start=start, back=back, mid=mid)

            for e in range(NE):
                act.wait_ge(h_done, e + 1)
                if e >= 2:
                    act.wait_ge(e_done, e - 1)
                act.activation(hs[:, e % 2, 0:rows], turn[e % 2][:, 0:rows], ACT.Gelu,
                               bias=b1col[:, e:e + 1]).then_inc(h_ready, 1)

        @block.vector
        def _(dve):
            dve.wait_ge(mu_done, 1)
            dve.tensor_scalar(mu_n[:, 0], lg_ps[:, 0, :], NORM_EPS ** 2, None, ALU.max).then_inc(mu_s, 1)
            dve.wait_ge(mu_s, 3)
            for k in range(KT):
                ins = dve.tensor_tensor(mu_u[:, k, :], mu_u[:, k, :], mu_n[:, 1], ALU.mult)
            ins.then_inc(mu_ready, 1)
            ln = Chain(dve, ln1_v, 3)
            sums = Chain(dve, sums_v, 2 * ST_TILES + 1)

            def start(b, p):
                ln.start(b)
                dve.wait_ge(x_in[p], at_pair(b, p, 16))
                for t in range(TT):
                    ins = dve.bn_stats(stats[:, t, :], x[:, p, t, :])
                ln.link(ins, (const, 3))
                for t in range(TT):
                    ins = dve.bn_aggr(mv[:, t, :], stats[:, t, :])
                ln.link(ins)
                dve.tensor_scalar(rstd[:, 0], mv[:, :, 1], LN_EPS, None, ALU.add).then_inc(var_ready, 1)
                dve.wait_ge(rstd_ready, at(b, 1, 1))
                for t in range(TT):
                    ins = dve.tensor_scalar(x[:, p, t, :], x[:, p, t, :], mv[:, t, 0:1], rstd[:, 1, t:t + 1],
                                            ALU.subtract, ALU.mult)
                ln.link(ins)
                dve.tensor_tensor(x[:, p], x[:, p], grow[:, :].unsqueeze(1).to_broadcast([P, TT, DM]),
                                  ALU.mult).then_inc(xg_ready, 1)
                ln.end()
                dve.wait_ge(ss_ready, at(b, 1, 1))
                dve.tensor_scalar(ss[:, 1], ss[:, 0], NORM_EPS ** 2, None, ALU.max).then_inc(ssb_ready, 1)
                dve.wait_ge(rn_ready, at(b, 1, 1))
                dve.tensor_scalar(rs[:, :], ss[:, 2], scol[:, 0:1], None, ALU.mult).then_inc(rs_ready, 1)

            def mid(b, p):
                sums.start(b)
                for j in range(ST_TILES):
                    dve.wait_ge(turn_done, at(b, TURNS, KT + j + 1))
                    sums.link(dve.tensor_reduce(mxd[:, 0, j:j + 1], turn[j % 2][:, :], AX.X, ALU.max))
                    dve.tensor_scalar(mxd[:, 1, j:j + 1], mxd[:, 0, j:j + 1], -1.0, None, ALU.mult
                                      ).then_inc(mx_ready, 1)
                sums.link(dve.tensor_reduce(mxc[:, :], lg[:, :, :], AX.X, ALU.max))
                dve.tensor_scalar(neg_mxc[:, :], mxc[:, :], -1.0, None, ALU.mult).then_inc(mc_ready, 1)
                for j in range(ST_TILES):
                    dve.wait_ge(turn_read, at(b, TURNS, KT + j + 1))
                    sums.link(dve.reciprocal(sd[:, 1, j:j + 1], sd[:, 0, j:j + 1]))
                    ins = dve.tensor_scalar(disp_t[:, j, :], disp_t[:, j, :], sd[:, 1, j:j + 1], None, ALU.mult)
                ins.then_inc(dn_ready, 1)
                dve.wait_ge(comb_ready, at(b, 1, 1))
                dve.reciprocal(rc_all[:, bass.ds(b, 1), :].rearrange("p a t -> p (a t)"), sc[:, :]
                               ).then_inc(rc_ready, 1)
                sums.end()

            def turned(b, p):
                dve.wait_ge(disp_turned, at(b, 1, 1))
                for half in range(2):
                    t2 = slice(half * TT // 2, (half + 1) * TT // 2)
                    ins = dve.tensor_copy(disp[:, t2, :], lg_ps[:, t2, :])
                ins.then_inc(disp_ready, 1)

            def back(b, p):
                dve.wait_ge(sl_done, at(b, 1, 1))
                for k in range(KT):
                    ins = dve.tensor_copy(slots_t[:, k, :, bass.ds(b, 1), :].rearrange("p e a s -> p e (a s)"),
                                          sl_ps[:, k, :].rearrange("p (e s) -> p e s", s=SL))
                ins.then_inc(sl_read, 1)

            over_routed(dve, n_seq, turn=turned, start=start, back=back, mid=mid)

            for e in range(NE):
                dve.wait_ge(e_done, e + 1)
                if e >= 2:
                    dve.wait_ge(so_out[e % 2], 16 * (e // 2))
                dve.tensor_copy(so[0:rows, e % 2, :], out_bank(e)[0:rows, :]).then_inc(so_ready, 1)

            ln_chain = Chain(dve, ln_v, 2 * TT)

            def output(b, p, first):
                ln_chain.start(b)
                dve.wait_ge(r_in[p], at_pair(b, p, 16))

                def apply(t):
                    dve.wait_ge(rstd2_ready, at(b, TT, t + 1))
                    dve.tensor_scalar(x[:, p, t, :], x[:, p, t, :], mv[:, t, 0:1], rstd[:, 1, t:t + 1],
                                      ALU.subtract, ALU.mult).then_inc(x3_ready, 1)

                for t in range(TT):
                    dve.wait_ge(out_done, at(b, TT, t + 1))
                    dve.scalar_tensor_tensor(out=x[:, p, t, :], in0=c_bank(t)[:, :],
                                             scalar=rc_all[:, bass.ds(b, 1), t:t + 1].rearrange("p a t -> p (a t)"),
                                             in1=x[:, p, t, :], op0=ALU.mult, op1=ALU.add).then_inc(out_read, 1)
                    dve.wait_ge(out_read, at(b, TT, t + 1))
                    ln_chain.link(dve.bn_stats(stats[:, t, :], x[:, p, t, :]), (const, 3))
                    ln_chain.link(dve.bn_aggr(mv[:, t, :], stats[:, t, :]))
                    dve.tensor_scalar(rstd[:, 0, t:t + 1], mv[:, t, 1:2], LN_EPS, None, ALU.add).then_inc(var2_ready, 1)
                    if t:
                        apply(t - 1)
                apply(TT - 1)
                ln_chain.end()

            over_pairs(dve, n_seq, lambda b, p, first: None, output)

        @block.tensor
        def _(pe):
            pe.wait_ge(const, 3)
            pe.wait_ge(mu_s, 1)
            for k in range(KT):
                ins = pe.matmul(lg_ps[:, 0, :], onesf[:, :], mu_sq[:, k, :], start=(k == 0), stop=(k == KT - 1))
            ins.then_inc(mu_done, 1)
            pe.wait_ge(mu_ready, 1)

            def turned(b, p):
                pe.wait_ge(dn_ready, at(b, 1, 1))
                for t in range(TT):
                    for j in range(ST_TILES):
                        ins = pe.transpose(lg_ps[:, t, j * P:(j + 1) * P], disp_t[:, j, t * P:(t + 1) * P],
                                           ident[:, :])
                ins.then_inc(disp_turned, 1)

            def free_turn(b, n):
                if n >= 2 or not is_zero(b):
                    pe.wait_ge(turn_read, at(b, TURNS, n - 1))

            def start(b, p):
                pe.wait_ge(xn_ready, at(b, 1, 1))
                for k in range(KT):
                    free_turn(b, k)
                    for t in range(TT):
                        ins = pe.transpose(turn[k % 2][:, t * P:(t + 1) * P], x[:, p, t, k * P:(k + 1) * P],
                                           ident[:, :])
                    ins.then_inc(turn_done, 1)
                pe.wait_ge(turn_read, at(b, TURNS, KT))
                if not is_zero(b):
                    pe.wait_ge(disp_ready, at(b, 1, 0))
                for t in range(TT):
                    for k in range(KT):
                        ins = pe.matmul(lg_ps[:, t, :], xnt[:, k, t * P:(t + 1) * P], mu_u[:, k, :],
                                        start=(k == 0), stop=(k == KT - 1))
                ins.then_inc(lg_done, 1)

            def mid(b, p):
                pe.wait_ge(lg_read, at(b, 1, 1))
                for j in range(ST_TILES):
                    free_turn(b, KT + j)
                    for t in range(TT):
                        ins = pe.transpose(turn[j % 2][:, t * P:(t + 1) * P], lg[:, t, j * P:(j + 1) * P],
                                           ident[:, :])
                    ins.then_inc(turn_done, 1)

            def back(b, p):
                pe.wait_ge(comb_ready, at(b, 1, 1))
                if not is_zero(b):
                    pe.wait_ge(ct_read, at(b, ST_TILES, 0))
                for j in range(ST_TILES):
                    for t in range(TT):
                        ins = pe.transpose(ct_ps[:, j, t * P:(t + 1) * P], comb[:, t, j * P:(j + 1) * P],
                                           ident[:, :])
                    ins.then_inc(ct_done, 1)
                pe.wait_ge(disp_ready, at(b, 1, 1))
                if not is_zero(b):
                    pe.wait_ge(sl_read, at(b, 1, 0))
                for k in range(KT):
                    for t in range(TT):
                        ins = pe.matmul(sl_ps[:, k, :], x[:, p, t, k * P:(k + 1) * P], disp[:, t, :],
                                        start=(t == 0), stop=(t == TT - 1))
                ins.then_inc(sl_done, 1)

            over_routed(pe, n_seq, turn=turned, start=start, back=back, mid=mid)

            pe.wait_ge(sl_read, n_seq)
            for e in range(NE):
                s = e % W_SLOTS
                pe.wait_ge(w_in[s], 32 * (e // W_SLOTS + 1))
                if e >= 2:
                    pe.wait_ge(h_ready, e - 1)
                for k in range(KT):
                    ins = pe.matmul(turn[e % 2][:, 0:rows], w1s[:, s, k, :],
                                    slots_t[:, k, e].rearrange("p b s -> p (b s)"), start=(k == 0), stop=(k == KT - 1))
                ins.then_inc(h_done, 1)
                if e:
                    second(pe, e - 1)
            second(pe, NE - 1)

            def combine(b, p, first):
                pe.wait_ge(b2_added, at(b, 1, 1))
                for t in range(TT):
                    if not is_zero(b):
                        pe.wait_ge(out_read, at(b, TT, t + 1 - TT))
                    elif t == 0:
                        pe.wait_ge(so_ready, NE)
                    for j in range(ST_TILES):
                        ins = pe.matmul(c_bank(t)[:, :], ct_in[:, p, j, t * P:(t + 1) * P], so_in[:, p, j, :],
                                        start=(j == 0), stop=(j == ST_TILES - 1))
                    ins.then_inc(out_done, 1)

            over_pairs(pe, n_seq, lambda b, p, first: None, combine)


def decoder(nc, n_seq, a, out):
    def scratch(name, shape):
        return nc.dram_tensor(name, shape, F32, kind="Internal").ap()

    x1 = scratch("x1", [n_seq, SEQ, DM])
    x2 = scratch("x2", [n_seq, SEQ, DM])
    combine_t = scratch("combine_t", [n_seq, SLOTS, SEQ])
    slot_out = scratch("slot_out", [NE, n_seq, SL, DM])
    mamba_stage(nc, n_seq, a["x_t"], a["x"], a["w_in_t"], a["conv_w"], a["conv_b"], a["dt_bias"], a["a_log"],
                a["d_skip"], a["norm_w"], a["w_out_t"], x1)
    attention_stage(nc, n_seq, x1, a["context_t"], [a["wq_t"], a["wk_t"], a["wv_t"], a["wo_t"]], a["b_qk"],
                    [a["bv"], a["bo"]], x2)
    moe_stage(nc, n_seq, x2, a["gamma"], a["beta"], a["mu"], a["scale"], a["w1"], a["b1_t"], a["w2"], a["b2"],
              combine_t, slot_out, out)


def lay_out(inputs):
    i = {name: np.asarray(v) for name, v in inputs.items()}
    m, t, f = "L0_attn_", "L0_xattn_", "L0_ffn_"
    di, ds = 2 * DM, 64
    z, x, bm, cm, dt = np.split(i[m + "W_in"], [di, 2 * di, 2 * di + ds, 2 * di + 2 * ds])
    ch = (di + 2 * ds) // P
    a = {
        "x": i["x"], "x_t": i["x"].transpose(0, 2, 1), "context_t": i["ctx_1024"].transpose(0, 2, 1),
        "w_in_t": np.concatenate([dt, z, x, bm, cm]).T,
        "conv_w": i[m + "conv_w"].reshape(ch, P, -1).transpose(1, 0, 2),
        "conv_b": i[m + "conv_b"].reshape(ch, P).T,
        "dt_bias": i[m + "dt_bias"], "a_log": i[m + "A_log"],
        "d_skip": i[m + "D"].reshape(-1, 2).T, "norm_w": i[m + "norm_w"].reshape(-1, P).T,
        "w_out_t": i[m + "W_out"].T,
        "b_qk": np.stack([i[t + "bq"], i[t + "bk"]]).reshape(2, KT, P).transpose(2, 0, 1),
        "bv": i[t + "bv"], "bo": i[t + "bo"],
        "gamma": i[f + "ln_gamma"], "beta": i[f + "ln_beta"], "mu": i[f + "mu"].reshape(DM, SLOTS),
        "scale": i[f + "scale"], "w1": i[f + "w1"], "b1_t": i[f + "b1"].T, "w2": i[f + "w2"], "b2": i[f + "b2"],
    }
    for n in "qkvo":
        a[f"w{n}_t"] = i[t + "W" + n].T
    return {name: np.ascontiguousarray(v) for name, v in a.items()}


def kernel(**inputs):
    import concourse.bacc as bacc
    from concourse.bass_utils import run_bass_kernel_spmd

    nc = bacc.Bacc("TRN2", target_bir_lowering=False, num_devices=1)
    arrays = lay_out(inputs)
    a = {name: nc.dram_tensor(f"{name}_in", v.shape, mybir.dt.from_np(v.dtype), kind="ExternalInput").ap()
         for name, v in arrays.items()}
    n_seq = arrays["x"].shape[0]
    out = nc.dram_tensor("out", (n_seq, SEQ, DM), F32, kind="ExternalOutput").ap()
    decoder(nc, n_seq, a, out)
    result = run_bass_kernel_spmd(nc, [{f"{name}_in": v for name, v in arrays.items()}], core_ids=[0])
    return result.results[0]["out"]
```

```python
from contextlib import ExitStack

import numpy as np

import concourse.bass as bass
from concourse import mybir

F32 = mybir.dt.float32
F32R = mybir.dt.float32r
ALU = mybir.AluOpType
ACT = mybir.ActivationFunctionType
AX = mybir.AxisListType

P = 128
SEQ = 512
DM = 512
KT = DM // P
TT = SEQ // P
LN_EPS = 1e-5


def at(b, per, k):
    return b * per + k


def value(eng, n):
    return n if isinstance(n, int) else eng.bass.snap(n, engines=[eng.engine])


class Chain:

    def __init__(self, eng, sem, per, had=0):
        self.eng, self.sem, self.per, self.had = eng, sem, per, had

    def start(self, b):
        self.base, self.k = self.had + b * self.per, 0

    def link(self, ins, before=None):
        ins.then_inc(self.sem, 1)
        self.k += 1
        if before:
            count = value(self.eng, self.base + self.k)
            met(self.eng, *before)
            self.eng.wait_ge(self.sem, count)
        else:
            self.eng.wait_ge(self.sem, self.base + self.k)

    def end(self):
        assert self.k == self.per, (self.k, self.per)


def met(eng, sem, value):
    eng.wait_ge(sem, value)


def over_sequences(eng, count, body):
    body(0, True)
    if count > 1:
        with eng.Fori(1, count) as i:
            body(i, False)


def one(ap, b):
    return ap[bass.ds(b, 1)]


DI = 1024
NH = 16
HP = 64
NS = 64
XT_TILES = DI // P
CH = 4
HG = 4
NG = NH // HG
COLS = NH + 2 * DI + 2 * NS
COL_Z, COL_X, COL_BC = NH, NH + DI, NH + 2 * DI


def mamba_stage(nc, n_seq, xT, x, winT, conv_w, conv_b, dt_bias, a_log, d_skip, norm_w, woutT, x1):
    with ExitStack() as ctx:
        def sb(name, shape, dt=F32):
            return ctx.enter_context(nc.sbuf_tensor("m_" + name, shape, dt))

        def ps(name):
            return ctx.enter_context(nc.psum_tensor("m_" + name, [P, 512], F32))

        def sem(name):
            return ctx.enter_context(nc.semaphore("m_" + name))

        win_hi = sb("win_hi", [P, KT, COLS], F32R)
        win_lo = sb("win_lo", [P, KT, COLS], F32R)
        wout = sb("wout", [P, XT_TILES, DM])
        cw = sb("cw", [P, 9, 4])
        cb = sb("cb", [P, 9])
        dcol = sb("dcol", [P, XT_TILES])
        nw = sb("nw", [P, XT_TILES])
        dtb = sb("dtb", [P, NH])
        aneg = sb("aneg", [P, NH])
        tri = sb("tri", [P, P])
        strict = sb("strict", [P, P])
        ident = sb("ident", [P, P])
        onesf = sb("onesf", [P, P])
        strict_r = sb("strict_r", [P, P], F32R)
        ones_r = sb("ones_r", [P, P], F32R)
        neg_half = sb("neg_half", [P, TT])
        xt_in = sb("xt_in", [P, 2, SEQ])
        xt_hi = sb("xt_hi", [P, KT, SEQ], F32R)
        xt_lo = sb("xt_lo", [P, KT, SEQ], F32R)
        x_tok = sb("x_tok", [P, TT, DM])
        dt_ch = sb("dt_ch", [32, SEQ])
        sm = sb("sm", [P, 8, CH * NH])
        dt = sb("dt", [P, CH, NH])
        a = sb("a", [P, CH, NH])
        a_hi = sb("a_hi", [P, CH, NH])
        a_lo = sb("a_lo", [P, CH, NH])
        a_hr = sb("a_hr", [P, CH, NH], F32R)
        wd = sb("wd", [P, 2, CH, NH])
        wdt = sb("wdt", [P, CH, NH])
        acc = sb("acc", [P, 2, SEQ])
        xc = sb("xc", [P, 2, 2, SEQ])
        zs = sb("zs", [P, 2, 2, SEQ])
        bt = sb("bt", [NS, SEQ])
        ct = sb("ct", [NS, SEQ])
        b_tok = sb("b_tok", [P, CH, NS])
        gm = sb("gm", [P, CH, P])
        rhs_hi = sb("rhs_hi", [P, 2, HG, P], F32R)
        rhs_lo = sb("rhs_lo", [P, 2, HG, P], F32R)
        dec = sb("dec", [P, CH, HG, P])
        ce = sb("ce", [NS, CH - 1, HG, P])
        xk = sb("xk", [P, CH, HG, HP])
        xdt = sb("xdt", [P, CH, HG, HP])
        xw = sb("xw", [P, CH - 1, HG, HP])
        st = sb("st", [NS, CH - 1, HG, HP])
        g = sb("g", [P, XT_TILES, SEQ])
        sq = sb("sq", [P, 2, SEQ])
        ssum = sb("ssum", [P, SEQ])
        rms = sb("rms", [P, 2, TT])
        stats = sb("stats", [P, TT, 6])
        mv = sb("mv", [P, TT, 2])
        rstd = sb("rstd", [P, 2, TT])
        staging = g[:, :, :].rearrange("p a b -> p (a b)")[:, 0:COLS]

        proj = [ps("proj0"), ps("proj1")]
        seg = [ps("seg0"), ps("seg1")]
        misc, turn = ps("misc"), ps("turn")
        yp = [ps("y0"), ps("y1")]

        w_in = sem("w_in")
        w_used = sem("w_used")
        small_in = sem("small_in")
        const = sem("const")
        setup = sem("setup")
        setup_a = sem("setup_a")
        xt_landed = [sem("xt_landed0"), sem("xt_landed1")]
        xt_split = sem("xt_split")
        xt_hi_s = sem("xt_hi_s")
        x_in = sem("x_in")
        x_dbl = sem("x_dbl")
        tile_done = sem("tile_done")
        dt_read = sem("dt_read")
        dt_turned = sem("dt_turned")
        a_ready = sem("a_ready")
        sums_done = sem("sums_done")
        wd_ready = sem("wd_ready")
        wdt_ready = sem("wdt_ready")
        dtv = sem("dtv")
        dta = sem("dta")
        taps0 = sem("taps0")
        conv_read = sem("conv_read")
        conv_v = sem("conv_v")
        bc_ready = sem("bc_ready")
        xc_ready = sem("xc_ready")
        z_ready = sem("z_ready")
        bg_done = sem("bg_done")
        bg_read = sem("bg_read")
        rhs_ready = sem("rhs_ready")
        seg_done = sem("seg_done")
        dec_ready = sem("dec_ready")
        m_ready = sem("m_ready")
        ebc_done = sem("ebc_done")
        e_ready = sem("e_ready")
        ce_ready = sem("ce_ready")
        xk_done = sem("xk_done")
        xk_ready = sem("xk_ready")
        xdt_ready = sem("xdt_ready")
        xw_ready = sem("xw_ready")
        st_done = sem("st_done")
        st_v = sem("st_v")
        st_ready = sem("st_ready")
        y_done = sem("y_done")
        y_read = sem("y_read")
        g_ready = sem("g_ready")
        sq_ready = sem("sq_ready")
        sq_used = sem("sq_used")
        rms_done = sem("rms_done")
        rms_in = sem("rms_in")
        rms_ready = sem("rms_ready")
        out_done = sem("out_done")
        out_read = sem("out_read")
        ln_v = sem("ln_v")
        var_ready = sem("var_ready")
        rstd_ready = sem("rstd_ready")
        x1_ready = sem("x1_ready")
        x1_out = sem("x1_out")

        block = ctx.enter_context(nc.Block())

        @block.sync
        def _(sp):
            for k in range(KT):
                if k:
                    sp.wait_ge(w_used, k)
                sp.dma_start(staging, winT[k * P:(k + 1) * P, :]).then_inc(w_in, 16)
                if k == 0:
                    sp.dma_start(cw[:, :, :], conv_w).then_inc(small_in, 16)
                    sp.dma_start(cb[:, :], conv_b).then_inc(small_in, 16)
                    sp.dma_start(nw[:, :], norm_w).then_inc(small_in, 16)
                    sp.dma_start(dtb[:, :], dt_bias.partition_broadcast(P)).then_inc(small_in, 16)
                    sp.dma_start(aneg[:, :], a_log.partition_broadcast(P)).then_inc(small_in, 16)
                    for half in range(2):
                        sp.dma_start(dcol[half * HP:(half + 1) * HP, :],
                                     d_skip[half].partition_broadcast(HP)
                                     ).then_inc(small_in, 16)
                    sp.dma_start(wout[:, :, :], woutT.rearrange("(c p) n -> p c n", p=P)).then_inc(small_in, 16)

            def sequence(b, first):
                for k in range(KT):
                    if k >= 2 or not first:
                        sp.wait_ge(xt_split, at(b, KT, k - 1))
                    sp.dma_start(xt_in[:, k % 2, :],
                                 one(xT, b)[:, k * P:(k + 1) * P, :].rearrange("a p n -> p (a n)")).then_inc(xt_landed[k % 2], 16)
                if not first:
                    sp.wait_ge(x1_out, at(b, 16 * TT, 0))
                sp.dma_start(x_tok[:, :, :], one(x, b).rearrange("a (t p) n -> p (a t) n", p=P)).then_inc(x_in, 16)
                for t in range(TT):
                    sp.wait_ge(x1_ready, at(b, TT, t + 1))
                    sp.dma_start(one(x1, b)[:, t * P:(t + 1) * P, :].rearrange("a p n -> p (a n)"),
                                 x_tok[:, t, :]).then_inc(x1_out, 16)

            over_sequences(sp, n_seq, sequence)
            sp.wait_ge(x1_out, 16 * TT * n_seq)

        @block.gpsimd
        def _(pool):
            pool.memset(onesf[:, :], 1.0).then_inc(const, 1)
            pool.memset(neg_half[:, :], -0.5).then_inc(const, 1)
            pool.wait_ge(const, 2)
            pool.affine_select(out=tri[:, :], in_=onesf[:, :], compare_op=ALU.is_ge, fill=0.0,
                               base=0, pattern=[[1, P]], channel_multiplier=-1).then_inc(const, 1)
            pool.affine_select(out=strict[:, :], in_=onesf[:, :], compare_op=ALU.is_ge, fill=0.0,
                               base=-1, pattern=[[-1, P]], channel_multiplier=1).then_inc(const, 1)
            pool.affine_select(out=ident[:, :], in_=onesf[:, :], compare_op=ALU.is_equal, fill=0.0,
                               base=0, pattern=[[-1, P]], channel_multiplier=1).then_inc(const, 1)
            pool.wait_ge(const, 5)

            def masked_decays(b, first, gr, c):
                if c >= 2:
                    if c == 2:
                        pool.wait_ge(seg_done, at(b, NG * CH, gr * CH + 1))
                    else:
                        pool.wait_ge(ebc_done, at(b, NG * (CH - 1), gr * (CH - 1) + 1))
                elif gr or not first:
                    pool.wait_ge(ebc_done, at(b, NG * (CH - 1), (gr - 1) * (CH - 1) + 2 + c))
                heads = slice(gr * HG, (gr + 1) * HG)
                shape = [P, HG, P]
                m = tri[:, :].unsqueeze(1).to_broadcast(shape)
                pool.tensor_tensor(rhs_hi[:, c % 2], a_hi[:, c, heads].unsqueeze(2).to_broadcast(shape), m, ALU.mult)
                pool.tensor_tensor(rhs_lo[:, c % 2], a_lo[:, c, heads].unsqueeze(2).to_broadcast(shape), m,
                                   ALU.mult).then_inc(rhs_ready, 1)

            def weighted_x(b, first, gr):
                pool.wait_ge(xk_ready, at(b, 2 * NG, 2 * gr + 2))
                if gr == 0:
                    pool.wait_ge(wdt_ready, at(b, 1, 1))
                if gr or not first:
                    pool.wait_ge(st_done, at(b, NG * (CH - 1), gr * (CH - 1)))
                w = wdt[:, 0:CH - 1, gr * HG:(gr + 1) * HG].unsqueeze(3).to_broadcast([P, CH - 1, HG, HP])
                pool.tensor_tensor(xw[:, :, :, :], xk[:, 0:CH - 1], w, ALU.mult).then_inc(xw_ready, 1)

            def sum_squares(b, first, gr):
                for j in range(2):
                    n = 2 * gr + j
                    if n == 0:
                        squares = value(pool, at(b, XT_TILES, 1))
                        met(pool, const, 5)
                        pool.wait_ge(sq_ready, squares)
                        if not first:
                            pool.wait_ge(rms_done, at(b, 1, 0))
                        pool.tensor_copy(ssum[:, :], sq[:, 0, :]).then_inc(sq_used, 1)
                    else:
                        pool.wait_ge(sq_ready, at(b, XT_TILES, n + 1))
                        pool.wait_ge(sq_used, at(b, XT_TILES, n))
                        pool.tensor_tensor(ssum[:, :], ssum[:, :], sq[:, j, :], ALU.add).then_inc(sq_used, 1)

            def sequence(b, first):
                pool.wait_ge(a_ready, at(b, 1, 1))
                for gr in range(NG):
                    for c in range(CH):
                        masked_decays(b, first, gr, c)
                    weighted_x(b, first, gr)
                    if gr:
                        sum_squares(b, first, gr - 1)
                sum_squares(b, first, NG - 1)
                pool.wait_ge(rms_in, at(b, 1, 1))
                pool.tensor_tensor(rms[:, 1], rms[:, 0], neg_half[:, :], ALU.pow).then_inc(rms_ready, 1)
                for t in range(TT):
                    pool.wait_ge(var_ready, at(b, TT, t + 1))
                    pool.tensor_tensor(rstd[:, 1, t:t + 1], rstd[:, 0, t:t + 1], neg_half[:, 0:1],
                                       ALU.pow).then_inc(rstd_ready, 1)

            over_sequences(pool, n_seq, sequence)

        @block.scalar
        def _(act):
            act.wait_ge(small_in, 16 * 8)
            act.activation(aneg[:, :], aneg[:, :], ACT.Exp).then_inc(setup_a, 1)

            def conv_tap0(b, n, tile, slot):
                act.wait_ge(tile_done, at(b, 18, tile + 1))
                act.activation(acc[:, slot, :], proj[tile % 2][:, :], ACT.Identity, bias=cb[:, n:n + 1],
                               scale=cw[:, n, 3:4]).then_inc(taps0, 1)

            def projections(b, first, gr):
                for j in range(2):
                    n = 2 * gr + j
                    if n == 0:
                        act.wait_ge(bc_ready, at(b, 1, 1))
                    elif n == 1:
                        if not first:
                            act.wait_ge(xc_ready, at(b, XT_TILES, 0))
                    else:
                        act.wait_ge(xc_ready, at(b, XT_TILES, n - 1))
                    conv_tap0(b, (DI // P) * 0 + n, 2 + 4 * gr + j, j)
                for j in range(2):
                    n = 2 * gr + j
                    act.wait_ge(conv_read, at(b, 9, n + 2))
                    if gr >= 2 or not first:
                        act.wait_ge(g_ready, at(b, XT_TILES, 2 * (gr - 2) + 2))
                    act.activation(xc[:, gr % 2, j, :], acc[:, j, :], ACT.Silu).then_inc(xc_ready, 1)
                for j in range(2):
                    act.wait_ge(tile_done, at(b, 18, 2 + 4 * gr + 2 + j + 1))
                    act.activation(zs[:, gr % 2, j, :], proj[j][:, :], ACT.Silu).then_inc(z_ready, 1)

            def decays(b, first, gr):
                for h in range(2):
                    act.wait_ge(xk_done, at(b, 2 * NG, 2 * gr + h + 1))
                    if h == 0 and (gr or not first):
                        act.wait_ge(xdt_ready, at(b, 2 * NG, 2 * gr))
                        act.wait_ge(xw_ready, at(b, NG, gr))
                    act.activation(xk[:, 2 * h:2 * h + 2].rearrange("p c h d -> p (c h d)"),
                                   turn[:, :], ACT.Copy).then_inc(xk_ready, 1)
                for c in range(CH):
                    act.wait_ge(seg_done, at(b, NG * CH, gr * CH + c + 1))
                    if c == 0 and (gr or not first):
                        act.wait_ge(y_done, at(b, XT_TILES, 2 * gr))
                    act.activation(dec[:, c], seg[c % 2][:, :], ACT.Exp).then_inc(dec_ready, 1)
                    if c:
                        act.wait_ge(ebc_done, at(b, NG * (CH - 1), gr * (CH - 1) + c))
                        act.activation(ce[:, c - 1], misc[0:NS, :], ACT.Exp).then_inc(e_ready, 1)

            def squares(b, first, gr):
                for j in range(2):
                    n = 2 * gr + j
                    act.wait_ge(g_ready, at(b, XT_TILES, n + 1))
                    if n >= 2 or not first:
                        act.wait_ge(sq_used, at(b, XT_TILES, n - 1))
                    act.activation(sq[:, j, :], g[:, n, :], ACT.Square).then_inc(sq_ready, 1)

            def sequence(b, first):
                act.wait_ge(tile_done, at(b, 18, 1))
                if not first:
                    act.wait_ge(dt_turned, at(b, 1, 0))
                act.activation(dt_ch[0:NH, :], proj[0][0:NH, :], ACT.Copy).then_inc(dt_read, 1)
                if not first:
                    act.wait_ge(xc_ready, at(b, XT_TILES, -1))
                conv_tap0(b, 8, 1, 0)
                act.wait_ge(conv_read, at(b, 9, 1))
                if not first:
                    act.wait_ge(bg_done, at(b, 1, 0))
                    act.wait_ge(ce_ready, at(b, NG * (CH - 1), 0))
                act.activation(bt[:, :], acc[0:NS, 0, :], ACT.Silu)
                act.activation(ct[:, :], acc[NS:P, 0, :], ACT.Silu).then_inc(bc_ready, 1)
                act.wait_ge(x_in, at(b, 16, 16))
                act.activation(x_tok[:, :, :], x_tok[:, :, :], ACT.Copy, scale=2.0).then_inc(x_dbl, 1)
                projections(b, first, 0)
                act.wait_ge(dtv, at(b, 14, 3))
                act.activation(sm[:, 2], sm[:, 1], ACT.Exp).then_inc(dta, 1)
                act.wait_ge(dtv, at(b, 14, 4))
                act.activation(sm[:, 4], sm[:, 3], ACT.Ln).then_inc(dta, 1)
                act.wait_ge(sums_done, at(b, 1, 1))
                if not first:
                    act.wait_ge(st_ready, at(b, NG * (CH - 1), 0))
                act.activation(wd[:, :, :, :].rearrange("p a c h -> p (a c h)"), turn[:, 0:2 * CH * NH],
                               ACT.Exp).then_inc(wd_ready, 1)
                for gr in range(NG):
                    decays(b, first, gr)
                    if gr + 1 < NG:
                        projections(b, first, gr + 1)
                    squares(b, first, gr)

            over_sequences(act, n_seq, sequence)

        @block.vector
        def _(dve):
            chain = Chain(dve, setup, 0)
            chain.start(0)
            dve.wait_ge(const, 5)
            dve.tensor_copy(strict_r[:, :], strict[:, :])
            dve.tensor_copy(ones_r[:, :], onesf[:, :])
            dve.wait_ge(setup_a, 1)
            dve.tensor_scalar(aneg[:, :], aneg[:, :], -1.0, -1e30, ALU.mult, ALU.max)
            for k in range(KT):
                dve.wait_ge(w_in, 16 * (k + 1))
                chain.link(dve.tensor_copy(win_hi[:, k, :], staging))
                dve.tensor_tensor(win_lo[:, k, :], staging, win_hi[:, k, :], ALU.subtract).then_inc(w_used, 1)
            for k in range(XT_TILES):
                ins = dve.tensor_scalar(wout[:, k, :], wout[:, k, :], nw[:, k:k + 1], None, ALU.mult)
            chain.link(ins)

            dt_chain = Chain(dve, dtv, 14)
            conv_chain = Chain(dve, conv_v, 18)
            st_chain = Chain(dve, st_v, 8)
            ln_chain = Chain(dve, ln_v, 2 * TT)

            def conv(b, n, tile, slot, done):
                dve.wait_ge(taps0, at(b, 9, done))
                for i in range(3):
                    s = i + 1
                    ins = dve.scalar_tensor_tensor(out=acc[:, slot, s:SEQ], in0=proj[tile % 2][:, 0:SEQ - s],
                                                   scalar=cw[:, n, 2 - i:3 - i], in1=acc[:, slot, s:SEQ],
                                                   op0=ALU.mult, op1=ALU.add)
                    if i < 2:
                        conv_chain.link(ins)
                ins.then_inc(conv_read, 1)

            def split_x(b, first):
                if not first:
                    dve.wait_ge(tile_done, at(b, 18, 0))
                for k in range(KT):
                    dve.wait_ge(xt_landed[k % 2], at(b, 16 * KT // 2, 16 * (k // 2 + 1)))
                    dve.tensor_copy(xt_hi[:, k, :], xt_in[:, k % 2, :]).then_inc(xt_hi_s, 1)
                    dve.wait_ge(xt_hi_s, at(b, KT, k + 1))
                    dve.tensor_tensor(xt_lo[:, k, :], xt_in[:, k % 2, :], xt_hi[:, k, :],
                                      ALU.subtract).then_inc(xt_split, 1)

            def step_sizes(b, first):
                dt_chain.start(b)
                sc = [sm[:, i] for i in range(8)]
                dve.wait_ge(dt_turned, at(b, 1, 1))
                if not first:
                    dve.wait_ge(rhs_ready, at(b, NG * CH, 0))
                    dve.wait_ge(xw_ready, at(b, NG, 0))
                dt_chain.link(dve.tensor_tensor(sc[0].rearrange("p (c h) -> p c h", h=NH),
                                                turn[:, 0:CH * NH].rearrange("p (c h) -> p c h", h=NH),
                                                dtb[:, :].unsqueeze(1).to_broadcast([P, CH, NH]), ALU.add))
                dt_chain.link(dve.tensor_scalar(sc[5], sc[0], -1.0, None, ALU.mult))
                dt_chain.link(dve.tensor_tensor(sc[1], sc[0], sc[5], ALU.min))
                dve.wait_ge(dta, at(b, 2, 1))
                dt_chain.link(dve.tensor_scalar(sc[3], sc[2], 1.0, None, ALU.add))
                dt_chain.link(dve.tensor_scalar(sc[7], sc[3], 1.0, None, ALU.is_equal))
                dt_chain.link(dve.scalar_tensor_tensor(out=sc[5], in0=sc[3], scalar=-1.0, in1=sc[7],
                                                       op0=ALU.add, op1=ALU.add))
                dt_chain.link(dve.reciprocal(sc[6], sc[5]))
                dve.wait_ge(dta, at(b, 2, 2))
                dt_chain.link(dve.tensor_tensor(sc[4], sc[4], sc[6], ALU.mult))
                dt_chain.link(dve.tensor_tensor(sc[5], sc[4], sc[7], ALU.add))
                dt_chain.link(dve.tensor_tensor(sc[6], sc[5], sc[2], ALU.mult))
                flat = dt[:, :, :].rearrange("p c h -> p (c h)")
                dt_chain.link(dve.scalar_tensor_tensor(out=flat, in0=sc[0], scalar=0.0, in1=sc[6],
                                                       op0=ALU.max, op1=ALU.add))
                dt_chain.link(dve.tensor_tensor(a[:, :, :], dt[:, :, :],
                                                aneg[:, :].unsqueeze(1).to_broadcast([P, CH, NH]), ALU.mult))
                dt_chain.link(dve.tensor_copy(a_hr[:, :, :], a[:, :, :]))
                dt_chain.link(dve.tensor_copy(a_hi[:, :, :], a_hr[:, :, :].bitcast(F32)))
                dve.tensor_tensor(a_lo[:, :, :], a[:, :, :], a_hi[:, :, :], ALU.subtract).then_inc(a_ready, 1)
                dt_chain.end()

            def group_factors(b, first, gr):
                heads = slice(gr * HG, (gr + 1) * HG)
                for h in range(2):
                    dve.wait_ge(xk_ready, at(b, 2 * NG, 2 * gr + h + 1))
                    if h == 0 and (gr or not first):
                        dve.wait_ge(y_done, at(b, XT_TILES, 2 * gr))
                    c = slice(2 * h, 2 * h + 2)
                    dve.tensor_tensor(xdt[:, c], xk[:, c], dt[:, c, heads].unsqueeze(3).to_broadcast([P, 2, HG, HP]),
                                      ALU.mult).then_inc(xdt_ready, 1)
                for c in range(CH):
                    dve.wait_ge(dec_ready, at(b, NG * CH, gr * CH + c + 1))
                    dve.tensor_tensor(dec[:, c], dec[:, c], gm[:, c, :].unsqueeze(1).to_broadcast([P, HG, P]),
                                      ALU.mult).then_inc(m_ready, 1)
                    if c:
                        dve.wait_ge(e_ready, at(b, NG * (CH - 1), gr * (CH - 1) + c))
                        dve.tensor_tensor(ce[:, c - 1], ce[:, c - 1],
                                          ct[:, c * P:(c + 1) * P].unsqueeze(1).to_broadcast([NS, HG, P]),
                                          ALU.mult).then_inc(ce_ready, 1)

            def states(b, first, gr):
                for c in range(CH - 1):
                    src = (turn[0:NS, c * 256:(c + 1) * 256] if c < 2 else misc[0:NS, 0:256])
                    src = src.rearrange("p (h d) -> p h d", h=HG)
                    dve.wait_ge(st_done, at(b, NG * (CH - 1), gr * (CH - 1) + max(c + 1, 2)))
                    if c == 0:
                        dve.tensor_copy(st[:, 0], src).then_inc(st_ready, 1)
                    else:
                        dve.wait_ge(st_ready, at(b, NG * (CH - 1), gr * (CH - 1) + c))
                        whole = wd[0:NS, 1, c, gr * HG:(gr + 1) * HG].unsqueeze(2).to_broadcast([NS, HG, HP])
                        st_chain.link(dve.tensor_tensor(st[:, c], st[:, c - 1], whole, ALU.mult))
                        dve.tensor_tensor(st[:, c], st[:, c], src, ALU.add).then_inc(st_ready, 1)

            def gate(b, first, gr):
                for j in range(2):
                    n = 2 * gr + j
                    dve.wait_ge(y_done, at(b, XT_TILES, n + 1))
                    if n == 0 and not first:
                        dve.wait_ge(out_done, at(b, TT, 0))
                    dve.scalar_tensor_tensor(out=g[:, n, :], in0=xc[:, gr % 2, j, :], scalar=dcol[:, n:n + 1],
                                             in1=yp[j][:, :], op0=ALU.mult, op1=ALU.add).then_inc(y_read, 1)
                for j in range(2):
                    n = 2 * gr + j
                    dve.wait_ge(z_ready, at(b, XT_TILES, n + 1))
                    dve.wait_ge(y_read, at(b, XT_TILES, n + 1))
                    dve.tensor_tensor(g[:, n, :], g[:, n, :], zs[:, gr % 2, j, :], ALU.mult).then_inc(g_ready, 1)

            def norm(b, first):
                ln_chain.start(b)
                dve.wait_ge(rms_done, at(b, 1, 1))
                dve.tensor_scalar(rms[:, 0], misc[:, 0:TT], 1.0 / DI, LN_EPS, ALU.mult, ALU.add).then_inc(rms_in, 1)
                dve.wait_ge(x_dbl, at(b, 1, 1))
                dve.wait_ge(rms_ready, at(b, 1, 1))

                def apply(t):
                    dve.wait_ge(rstd_ready, at(b, TT, t + 1))
                    dve.tensor_scalar(x_tok[:, t, :], x_tok[:, t, :], mv[:, t, 0:1], rstd[:, 1, t:t + 1],
                                      ALU.subtract, ALU.mult).then_inc(x1_ready, 1)

                for t in range(TT):
                    dve.wait_ge(out_done, at(b, TT, t + 1))
                    dve.scalar_tensor_tensor(out=x_tok[:, t, :], in0=proj[t % 2][:, :], scalar=rms[:, 1, t:t + 1],
                                             in1=x_tok[:, t, :], op0=ALU.mult, op1=ALU.add).then_inc(out_read, 1)
                    dve.wait_ge(out_read, at(b, TT, t + 1))
                    ln_chain.link(dve.bn_stats(stats[:, t, :], x_tok[:, t, :]), (const, 5))
                    ln_chain.link(dve.bn_aggr(mv[:, t, :], stats[:, t, :]))
                    dve.tensor_scalar(rstd[:, 0, t:t + 1], mv[:, t, 1:2], LN_EPS, None, ALU.add).then_inc(var_ready, 1)
                    if t:
                        apply(t - 1)
                apply(TT - 1)
                ln_chain.end()

            def sequence(b, first):
                st_chain.start(b)
                conv_chain.start(b)
                split_x(b, first)
                conv(b, 8, 1, 0, 1)
                conv(b, 0, 2, 0, 2)
                conv(b, 1, 3, 1, 3)
                dve.wait_ge(bg_done, at(b, 1, 1))
                dve.tensor_tensor(gm[:, :, :], misc[:, :].rearrange("p (c t) -> p c t", c=CH),
                                  tri[:, :].unsqueeze(1).to_broadcast([P, CH, P]), ALU.mult)
                dve.tensor_copy(b_tok[:, :, :].rearrange("p c n -> p (c n)"),
                                yp[0][:, 0:CH * NS]).then_inc(bg_read, 1)
                step_sizes(b, first)
                dve.wait_ge(wd_ready, at(b, 1, 1))
                dve.tensor_tensor(wdt[:, :, :], wd[:, 0], dt[:, :, :], ALU.mult).then_inc(wdt_ready, 1)
                for gr in range(NG):
                    group_factors(b, first, gr)
                    if gr + 1 < NG:
                        for j in range(2):
                            conv(b, 2 * gr + 2 + j, 2 + 4 * (gr + 1) + j, j, 2 * gr + 4 + j)
                    states(b, first, gr)
                    gate(b, first, gr)
                norm(b, first)
                conv_chain.end()
                st_chain.end()

            over_sequences(dve, n_seq, sequence)

        @block.tensor
        def _(pe):
            pe.wait_ge(w_used, KT)
            pe.wait_ge(setup, KT + 1)

            def in_proj(b, first, n, col):
                bank = proj[n % 2]
                if n == 0:
                    if not first:
                        pe.wait_ge(out_read, at(b, TT, -1))
                elif n == 1:
                    if not first:
                        pe.wait_ge(out_read, at(b, TT, 0))
                elif n == 2:
                    pe.wait_ge(dt_read, at(b, 1, 1))
                elif n == 3:
                    pe.wait_ge(conv_read, at(b, 9, 1))
                elif (n - 2) % 4 < 2:
                    pe.wait_ge(z_ready, at(b, XT_TILES, 2 * ((n - 2) // 4 - 1) + (n - 2) % 4 + 1))
                else:
                    pe.wait_ge(conv_read, at(b, 9, 2 * ((n - 2) // 4) + (n - 2) % 4 - 2 + 2))
                for k in range(KT):
                    if n == 0:
                        pe.wait_ge(xt_split, at(b, KT, k + 1))
                    wh, wl = win_hi[:, k, col:col + P], win_lo[:, k, col:col + P]
                    pe.matmul(bank[:, :], wh, xt_hi[:, k, :], start=(k == 0), stop=False)
                    pe.matmul(bank[:, :], wh, xt_lo[:, k, :], start=False, stop=False)
                    ins = pe.matmul(bank[:, :], wl, xt_hi[:, k, :], start=False, stop=(k == KT - 1))
                ins.then_inc(tile_done, 1)

            def group_projections(b, first, gr):
                for j in range(2):
                    in_proj(b, first, 2 + 4 * gr + j, COL_X + (2 * gr + j) * P)
                for j in range(2):
                    in_proj(b, first, 4 + 4 * gr + j, COL_Z + (2 * gr + j) * P)

            def decays(b, first, gr):
                for h in range(2):
                    if h == 0:
                        pe.wait_ge(xc_ready, at(b, XT_TILES, 2 * gr + 2))
                        if gr == 0:
                            pe.wait_ge(wd_ready, at(b, 1, 1))
                        else:
                            pe.wait_ge(st_ready, at(b, NG * (CH - 1), gr * (CH - 1)))
                    else:
                        pe.wait_ge(xk_ready, at(b, 2 * NG, 2 * gr + 1))
                    for c in range(2):
                        for j in range(2):
                            t0 = (2 * h + c) * P
                            ins = pe.transpose(turn[:, c * 256 + j * P:c * 256 + (j + 1) * P],
                                               xc[:, gr % 2, j, t0:t0 + P], ident[:, :])
                    ins.then_inc(xk_done, 1)
                for c in range(CH):
                    pe.wait_ge(rhs_ready, at(b, NG * CH, gr * CH + c + 1))
                    if gr or c >= 2 or not first:
                        pe.wait_ge(dec_ready, at(b, NG * CH, gr * CH + c - 1))
                    hi = rhs_hi[:, c % 2].rearrange("p h t -> p (h t)")
                    lo = rhs_lo[:, c % 2].rearrange("p h t -> p (h t)")
                    pe.matmul(seg[c % 2][:, :], strict_r[:, :], hi, start=True, stop=False)
                    pe.matmul(seg[c % 2][:, :], strict_r[:, :], lo, start=False, stop=True).then_inc(seg_done, 1)
                    if c:
                        if c > 1:
                            pe.wait_ge(e_ready, at(b, NG * (CH - 1), gr * (CH - 1) + c - 1))
                        elif gr == 0:
                            pe.wait_ge(bg_read, at(b, 1, 1))
                        pe.matmul(misc[:, :], ones_r[:, :], hi, start=True, stop=False)
                        pe.matmul(misc[:, :], ones_r[:, :], lo, start=False, stop=True).then_inc(ebc_done, 1)

            def outputs(b, first, gr):
                pe.wait_ge(xw_ready, at(b, NG, gr + 1))
                pe.wait_ge(e_ready, at(b, NG * (CH - 1), (gr + 1) * (CH - 1)))
                for c in range(CH - 1):
                    dst = turn[0:NS, c * 256:(c + 1) * 256] if c < 2 else misc[0:NS, 0:256]
                    pe.matmul(dst, b_tok[:, c, :], xw[:, c].rearrange("p h d -> p (h d)"),
                              start=True, stop=True).then_inc(st_done, 1)
                if gr or not first:
                    pe.wait_ge(y_read, at(b, XT_TILES, 2 * gr))
                if gr == 0:
                    pe.wait_ge(bg_read, at(b, 1, 1))
                pe.wait_ge(xdt_ready, at(b, 2 * NG, 2 * gr + 2))
                for c in range(CH):
                    pe.wait_ge(m_ready, at(b, NG * CH, gr * CH + c + 1))
                    for j in range(2):
                        for h in range(2):
                            pe.matmul(yp[j][h * HP:(h + 1) * HP, c * P:(c + 1) * P], xdt[:, c, 2 * j + h, :],
                                      dec[:, c, 2 * j + h, :], start=(c == 0), stop=False, skip_group_check=True)
                for j in range(2):
                    for c in range(1, CH):
                        if j == 0:
                            met(pe, w_used, KT)
                            pe.wait_ge(st_ready, at(b, NG * (CH - 1), gr * (CH - 1) + c))
                            pe.wait_ge(ce_ready, at(b, NG * (CH - 1), gr * (CH - 1) + c))
                        for h in range(2):
                            ins = pe.matmul(yp[j][h * HP:(h + 1) * HP, c * P:(c + 1) * P], st[:, c - 1, 2 * j + h, :],
                                            ce[:, c - 1, 2 * j + h, :], start=False, stop=(c == CH - 1),
                                            skip_group_check=True)
                    ins.then_inc(y_done, 1)

            def sequence(b, first):
                in_proj(b, first, 0, 0)
                in_proj(b, first, 1, COL_BC)
                turn_free = value(pe, at(b, NG * (CH - 1), 0))
                raw_dt = value(pe, at(b, 1, 1))
                met(pe, w_used, KT)
                pe.wait_ge(dt_read, raw_dt)
                if not first:
                    pe.wait_ge(st_ready, turn_free)
                for c in range(CH):
                    ins = pe.transpose(turn[:, c * NH:(c + 1) * NH], dt_ch[0:NH, c * P:(c + 1) * P],
                                       ident[0:NH, 0:NH])
                ins.then_inc(dt_turned, 1)
                group_projections(b, first, 0)
                pe.wait_ge(bc_ready, at(b, 1, 1))
                if not first:
                    pe.wait_ge(rms_in, at(b, 1, 0))
                    pe.wait_ge(y_read, at(b, XT_TILES, 0))
                for c in range(CH):
                    pe.matmul(misc[:, c * P:(c + 1) * P], bt[:, c * P:(c + 1) * P], ct[:, c * P:(c + 1) * P],
                              start=True, stop=True)
                for c in range(CH):
                    ins = pe.transpose(yp[0][:, c * NS:(c + 1) * NS], bt[:, c * P:(c + 1) * P], ident[0:NS, 0:NS])
                ins.then_inc(bg_done, 1)
                pe.wait_ge(a_ready, at(b, 1, 1))
                flat = a[:, :, :].rearrange("p c h -> p (c h)")
                pe.matmul(turn[:, 0:CH * NH], strict[:, :], flat, start=True, stop=True)
                pe.matmul(turn[:, CH * NH:2 * CH * NH], onesf[:, :], flat, start=True, stop=True).then_inc(sums_done, 1)
                for gr in range(NG):
                    decays(b, first, gr)
                    if gr + 1 < NG:
                        group_projections(b, first, gr + 1)
                    outputs(b, first, gr)
                pe.wait_ge(sq_used, at(b, XT_TILES, XT_TILES))
                pe.wait_ge(st_ready, at(b, NG * (CH - 1), NG * (CH - 1)))
                for t in range(TT):
                    ins = pe.matmul(misc[:, t:t + 1], ssum[:, t * P:(t + 1) * P], onesf[:, 0:1], start=True, stop=True)
                ins.then_inc(rms_done, 1)
                for t in range(TT):
                    if t < 2:
                        pe.wait_ge(z_ready, at(b, XT_TILES, XT_TILES - 1 + t))
                    else:
                        pe.wait_ge(out_read, at(b, TT, t - 1))
                    for k in range(XT_TILES):
                        ins = pe.matmul(proj[t % 2][:, :], g[:, k, t * P:(t + 1) * P], wout[:, k, :],
                                        start=(k == 0), stop=(k == XT_TILES - 1))
                    ins.then_inc(out_done, 1)

            over_sequences(pe, n_seq, sequence)


AH = 16
AD = DM // AH
AG = P // AD
STACK = 3 * AD
SOFT_SCALE = AD ** -0.5


UNITS = KT * TT
LEAD = 5
STACKS = 3


class Turn:

    def __init__(self, b, phase, d):
        self.b, self.phase, self.d = b, phase, d

    def before(self):
        return Turn(self.b, self.phase, self.d - 1)

    def slot(self, gr):
        return (self.phase + self.d + gr) % STACKS

    def at(self, per, k):
        return at(self.b, per, k + self.d * per)

    def number(self):
        return self.b + self.d if self.d else self.b

    def first(self):
        return isinstance(self.b, int) and self.b + self.d == 0


def attention_order():
    steps = []

    def now(*names):
        steps.extend((name, 0) for name in names)

    def ahead(*names):
        steps.extend((name, 1) for name in names)

    def p1(n):
        return [("p1", n // TT, n % TT, half) for half in range(2)]

    def av(n):
        return [("av", n // TT, n % TT, half) for half in range(2)]

    def of(n, names):
        return (ahead if n >= UNITS else now)(*names(n % UNITS))

    def maxima(n, half):
        of(n + LEAD, lambda m: p1(m)[half:half + 1])

    def projection(n):
        if n in (1, 5, 9, 13):
            of(n + 3 * TT - 1, lambda m: [("qk", m // TT, 1, 0)])
        if n in (2, 6, 10, 14):
            of(n + 3 * TT - 2, lambda m: [("qk", m // TT, 0, 0)])

    for n in range(UNITS):
        gr, u = divmod(n, TT)
        products = av(n - 1) if n else [None, None]
        projects = n % TT in (1, 2)
        if u == TT - 1:
            of(n + TT, lambda m: [("neg", m // TT, 0, 0)])
            now(("st", gr, u, 0))
        maxima(n, 0)
        if n >= TT:
            now(*[("norm", gr - 1, c, 0) for c in ((), (0, 1), (2,), (3,))[u]])
        if projects:
            projection(n)
        if u < TT - 1:
            now(("st", gr, u, 0))
        if n:
            now(products[0])
        maxima(n, 1)
        if n:
            now(products[1])
        if u == 0 and n:
            now(("o", gr - 1, 0, 0))
            of(n + 2 * TT, lambda m: [("stack", m // TT, 0, 0)])
        if n == 0:
            now(("bias", 0, 0, 0))
        if n in (1, 2):
            ahead(*[("c", 2 * (n - 1) + k, 0, 0) for k in range(2)])
        if n in (3, 4):
            ahead(*[("xt", 2 * (n - 3) + k, 0, 0) for k in range(2)])
        if n in (2, 3):
            ahead(*[("x", 2 * (n - 2) + k, 0, 0) for k in range(2)])
    now(*av(UNITS - 1), ("o", KT - 1, 0, 0))
    ahead(("stack", 2, 0, 0))
    for c in range(TT):
        now(("norm", KT - 1, c, 0))
        if c != 1:
            ahead(("v", c // 2 + c // 3, 0, 0))
    ahead(("v", 3, 0, 0))
    now(*[("out", t, 0, 0) for t in range(TT)], ("end", 0, 0, 0))
    ahead(("load", 0, 0, 0))
    start = [(step, 0) for step, d in steps if d]
    last = [(step, 0) for step, d in steps if not d]
    return start, steps, last


def over_attention(eng, count, take_step, steps):
    start, steady, last = steps

    def run(b, phase, part, name):
        for step, d in part:
            take_step(step, Turn(b, phase, d), name)

    run(0, 0, start, "start")
    run(0, 0, steady, "first")
    turns = (count - 2) // STACKS
    if turns:
        with eng.Fori(0, turns) as i:
            for n in range(STACKS):
                run(i * STACKS + 1 + n, (1 + n) % STACKS, steady, "steady")
    for b in range(1 + turns * STACKS, count - 1):
        run(b, b % STACKS, steady, "steady")
    run(count - 1, (count - 1) % STACKS, last, "last")


def shared_uses(part, shift=0):
    uses = []
    for (kind, i, j, h), d in part:
        if kind == "p1":
            uses += [((kind, i, j, 2 * h + n), d + shift) for n in range(2)]
        elif kind in ("xt", "qk", "v", "neg", "out"):
            uses.append(((kind, i, j, h), d + shift))
    return uses


def bank_plan(steps):
    start, steady, last = steps
    bank_of = {use: n % 2 for n, (use, d) in enumerate(shared_uses(steady))}
    assert len(bank_of) % 2 == 0
    before = {}
    for name, past, part in (("start", [], start), ("first", shared_uses(start), steady),
                             ("steady", shared_uses(steady, -1), steady), ("last", shared_uses(steady, -1), last)):
        held = {bank_of[use]: (use, d) for use, d in past}
        for use, d in shared_uses(part):
            before[name, use] = held.get(bank_of[use])
            held[bank_of[use]] = (use, d)
    return bank_of, before


def attention_stage(nc, n_seq, x1, ctxT, wT, b_col, b_row, x2):
    steps = attention_order()
    bank_of, before = bank_plan(steps)

    with ExitStack() as ctx:
        def sb(name, shape, dt=F32):
            return ctx.enter_context(nc.sbuf_tensor("a_" + name, shape, dt))

        def ps(name, shape=(P, 512)):
            return ctx.enter_context(nc.psum_tensor("a_" + name, list(shape), F32))

        def sem(name):
            return ctx.enter_context(nc.semaphore("a_" + name))

        names = ["q", "k", "v"]
        w_hi = {n: sb(f"w{n}_hi", [P, KT, DM], F32R) for n in names}
        w_lo = {n: sb(f"w{n}_lo", [P, KT, DM], F32R) for n in names}
        w_o = sb("wo", [P, KT, DM])
        bcol = sb("bcol", [P, 2, KT])
        brow = sb("brow", [P, 2, DM])
        ident = sb("ident", [P, P])
        onesf = sb("onesf", [P, P])
        neg_half = sb("neg_half", [P, 1])
        x_tok = sb("x_tok", [P, TT, DM])
        xt_hi = sb("xt_hi", [P, KT, SEQ], F32R)
        xt_lo = sb("xt_lo", [P, KT, SEQ], F32R)
        land = sb("land", [P, 2, SEQ])
        c_hi = sb("c_hi", [P, KT, SEQ], F32R)
        c_lo = sb("c_lo", [P, KT, SEQ], F32R)
        qk_hi = sb("qk_hi", [P, 2, 2, SEQ], F32R)
        qk_lo = sb("qk_lo", [P, 2, 2, SEQ], F32R)
        qs = sb("qs", [P, STACKS, AG, SEQ], F32R)
        ks = sb("ks", [P, STACKS, AG, SEQ], F32R)
        mx = sb("mx", [P, 2, TT, AG])
        neg_hi = sb("neg_hi", [AG, SEQ], F32R)
        neg_lo = sb("neg_lo", [AG, SEQ], F32R)
        v = sb("v", [P, TT, DM])
        probs = sb("probs", [P, 2, AG, SEQ])
        den = sb("den", [P, SEQ])
        o = sb("o", [P, KT, SEQ])
        stats = sb("stats", [P, TT, 6])
        mv = sb("mv", [P, TT, 2])
        rstd = sb("rstd", [P, 2, TT])

        sp_banks = ps("scores", (P, AG, SEQ))
        shared = [ps("shared0"), ps("shared1")]
        o_bank, den_bank = ps("o_bank"), ps("den_bank")

        def bank(use):
            return shared[bank_of[use]]

        w_in = [sem("w_in0"), sem("w_in1")]
        w_used = sem("w_used")
        w_v = sem("w_v")
        small_in = sem("small_in")
        const = sem("const")
        ones_set = sem("ones_set")
        x_in = sem("x_in")
        landed = [sem("landed0"), sem("landed1")]
        c_hi_s = sem("c_hi_s")
        c_split = sem("c_split")
        xt_done = sem("xt_done")
        xt_hi_s = sem("xt_hi_s")
        xt_split = sem("xt_split")
        xb_ready = sem("xb_ready")
        qk_done = [sem("q_done"), sem("k_done")]
        qk_hi_s = [sem("q_hi_s"), sem("k_hi_s")]
        qk_split = [sem("q_split"), sem("k_split")]
        stack_in = [[sem(f"stack{i}_{n}") for i in range(2)] for n in ("sp", "pool")]
        neg_in = [sem("neg_in0"), sem("neg_in1")]
        v_done = sem("v_done")
        v_ready = sem("v_ready")
        p1_done = sem("p1_done")
        mx_ready = sem("mx_ready")
        neg_done = sem("neg_done")
        neg_v = sem("neg_v")
        neg_ready = sem("neg_ready")
        st_done = sem("st_done")
        exp_ready = sem("exp_ready")
        av_done = sem("av_done")
        o_copied = sem("o_copied")
        o_v = sem("o_v")
        o_ready = sem("o_ready")
        out_done = sem("out_done")
        out_read = sem("out_read")
        ln_v = sem("ln_v")
        var_ready = sem("var_ready")
        rstd_ready = sem("rstd_ready")
        x2_ready = sem("x2_ready")
        x2_out = [sem(f"x2_out{t}") for t in range(TT)]

        def reader(kind, i, j, h):
            return {"xt": (xt_split, TT, i + 1),
                    "qk": (qk_split[j % 2], KT, i + 1),
                    "v": (v_ready, TT, i + 1),
                    "p1": (mx_ready, AG * UNITS, AG * (TT * i + j) + h + 1),
                    "neg": (neg_ready, KT, i + 1),
                    "out": (out_read, TT, i + 1)}[kind]

        HEAD_DMAS = 16 * 3
        SHARE = [HEAD_DMAS * (AG + 1), HEAD_DMAS * (AG - 1)]

        def stack_filled(eng, gr, t, shares=(0, 1)):
            for queue in shares:
                eng.wait_ge(stack_in[queue][gr % 2], t.at(SHARE[queue] * KT // 2, SHARE[queue] * (gr // 2 + 1)))

        def stack_free(gr, t):
            if gr >= STACKS:
                return t.at(2 * UNITS, 2 * TT * (gr - STACKS + 1))
            return None if t.first() else t.before().at(2 * UNITS, 2 * TT * (gr + KT - STACKS + 1))

        def fill_stack(eng, queue, which, gr, t, heads):
            split = value(eng, t.at(KT, gr + 1))
            free = stack_free(gr, t)
            free = None if free is None else value(eng, free)
            met(eng, const, 3)
            eng.wait_ge(qk_split[which], split)
            if free is not None:
                eng.wait_ge(st_done, free)
            parts = (qk_hi, qk_hi, qk_lo) if which else (qk_hi, qk_lo, qk_hi)
            for r, part in enumerate(parts):
                dst = (ks if which else qs)[r * AD:(r + 1) * AD, t.slot(gr)]
                for h in heads:
                    eng.dma_start(dst[:, h, :].bitcast(F32),
                                  part[h * AD:(h + 1) * AD, which, gr % 2, :].bitcast(F32)
                                  ).then_inc(stack_in[queue][gr % 2], 16)

        block = ctx.enter_context(nc.Block())
        N_SMALL = 4 * 16

        @block.sync
        def _(sp):
            for i, n in enumerate(names):
                if i >= 2:
                    sp.wait_ge(w_used, i - 1)
                sp.dma_start(probs[:, i % 2], wT[i].rearrange("(k p) n -> p k n", p=P)).then_inc(w_in[i % 2], 16)
            sp.dma_start(w_o[:, :, :], wT[3].rearrange("(k p) n -> p k n", p=P)).then_inc(small_in, 16)
            sp.dma_start(bcol[:, :, :], b_col).then_inc(small_in, 16)
            for i in range(2):
                sp.dma_start(brow[:, i, :], b_row[i].partition_broadcast(P)).then_inc(small_in, 16)

            def load_x(t, n):
                if not t.first():
                    sp.wait_ge(x2_out[n], t.at(16, 0))
                sp.dma_start(x_tok[:, n, :], one(x1, t.number())[:, n * P:(n + 1) * P, :].rearrange("a p n -> p (a n)")
                             ).then_inc(x_in, 16)

            def step(what, t, part):
                kind, i, j, h = what
                if kind == "c":
                    if i >= 2:
                        sp.wait_ge(c_split, t.at(KT, i - 1))
                    elif not t.first():
                        sp.wait_ge(xt_done, t.at(TT, i - 1))
                    sp.dma_start(land[:, i % 2, :],
                                 one(ctxT, t.number())[:, i * P:(i + 1) * P, :].rearrange("a p n -> p (a n)")
                                 ).then_inc(landed[i % 2], 16)
                elif kind == "x":
                    if i < 2:
                        sp.wait_ge(c_split, t.at(KT, KT - 1 + i))
                    else:
                        sp.wait_ge(xt_done, t.at(TT, i - 1))
                    sp.dma_start(land[:, i % 2, :],
                                 one(x1, t.number())[:, i * P:(i + 1) * P, :].rearrange("a p n -> p (a n)")
                                 ).then_inc(landed[i % 2], 16)
                elif kind == "out":
                    sp.wait_ge(x2_ready, t.at(TT, i + 1))
                    sp.dma_start(one(x2, t.number())[:, i * P:(i + 1) * P, :].rearrange("a p n -> p (a n)"),
                                 x_tok[:, i, :]).then_inc(x2_out[i], 16)
                elif kind == "load":
                    for n in range(TT):
                        load_x(t, n)
                elif kind == "stack":
                    fill_stack(sp, 0, 1, i, t, range(AG - 1, AG))
                    fill_stack(sp, 0, 0, i, t, range(AG))
                elif kind == "neg":
                    sp.wait_ge(neg_ready, t.at(KT, i + 1))
                    for r, part in enumerate((neg_hi, neg_lo)):
                        sp.dma_start(qs[STACK + r:STACK + r + 1, t.slot(i)].bitcast(F32),
                                     part[:, :].bitcast(F32)).then_inc(neg_in[i % 2], 16)

            over_attention(sp, n_seq, step, steps)
            for n in range(TT):
                sp.wait_ge(x2_out[n], 16 * n_seq)

        @block.gpsimd
        def _(pool):
            pool.memset(onesf[:, :], 1.0).then_inc(const, 1)
            pool.memset(neg_half[:, :], -0.5).then_inc(const, 1)
            pool.wait_ge(const, 2)
            pool.affine_select(out=ident[:, :], in_=onesf[:, :], compare_op=ALU.is_equal, fill=0.0,
                               base=0, pattern=[[-1, P]], channel_multiplier=1).then_inc(const, 1)
            pool.wait_ge(small_in, N_SMALL)

            def power(t, n):
                pool.wait_ge(var_ready, t.at(TT, n + 1))
                pool.tensor_tensor(rstd[:, 1, n:n + 1], rstd[:, 0, n:n + 1], neg_half[:, :],
                                   ALU.pow).then_inc(rstd_ready, 1)

            def step(what, t, part):
                kind, i, j, h = what
                if kind == "stack":
                    fill_stack(pool, 1, 1, i, t, range(AG - 1))
                elif kind == "bias":
                    met(pool, const, 3)
                    pool.wait_ge(x_in, t.at(16 * TT, 16 * TT))
                    pool.tensor_tensor(x_tok[:, :, :], x_tok[:, :, :],
                                       brow[:, 1, :].unsqueeze(1).to_broadcast([P, TT, DM]), ALU.add).then_inc(xb_ready, 1)
                elif kind == "out":
                    power(t, i)

            over_attention(pool, n_seq, step, steps)

        @block.scalar
        def _(act):
            act.wait_ge(small_in, N_SMALL)

            def step(what, t, part):
                kind, i, j, h = what
                if kind == "c":
                    if i == 0 and not t.first():
                        act.wait_ge(qk_done[1], t.at(KT, 0))
                    act.wait_ge(landed[i % 2], t.at(64, 16 * (i // 2 + 1)))
                    act.activation(c_hi[:, i, :], land[:, i % 2, :], ACT.Copy).then_inc(c_hi_s, 1)
                elif kind == "xt":
                    act.wait_ge(xt_done, t.at(TT, i + 1))
                    act.activation(xt_hi[:, :, i * P:(i + 1) * P], bank(what)[:, :].rearrange("p (k n) -> p k n", n=P),
                                   ACT.Copy).then_inc(xt_hi_s, 1)
                elif kind == "qk":
                    act.wait_ge(qk_done[j], t.at(KT, i + 1))
                    if i >= 2:
                        stack_filled(act, i - 2, t, range(j + 1))
                    elif not t.first():
                        stack_filled(act, i + 2, t.before(), range(j + 1))
                    act.activation(qk_hi[:, j, i % 2, :], bank(what)[:, :], ACT.Identity, bias=bcol[:, j, i:i + 1]
                                   ).then_inc(qk_hi_s[j], 1)
                elif kind == "st":
                    n = TT * i + j
                    for half in range(2):
                        act.wait_ge(st_done, t.at(2 * UNITS, 2 * n + half + 1))
                        if half == 0 and (n >= 2 or not t.first()):
                            act.wait_ge(av_done, t.at(UNITS, n - 1))
                        act.activation(probs[:, n % 2, 2 * half:2 * half + 2],
                                       sp_banks[:, 2 * half:2 * half + 2], ACT.Exp,
                                       scale=SOFT_SCALE).then_inc(exp_ready, 1)
                elif kind == "o":
                    act.wait_ge(av_done, t.at(UNITS, TT * (i + 1)))
                    if i or not t.first():
                        act.wait_ge(o_ready, t.at(KT, i))
                    if i == 0 and not t.first():
                        act.wait_ge(out_done, t.at(TT, 0))
                    act.activation(o[:, i, :], o_bank[:, :], ACT.Copy)
                    act.activation(den[:, :], den_bank[:, :], ACT.Copy).then_inc(o_copied, 1)

            over_attention(act, n_seq, step, steps)

        @block.vector
        def _(dve):
            wchain = Chain(dve, w_v, 0)
            wchain.start(0)
            for i, n in enumerate(names):
                dve.wait_ge(w_in[i % 2], 16 * (i // 2 + 1))
                wchain.link(dve.tensor_copy(w_hi[n][:, :, :], probs[:, i % 2]))
                dve.tensor_tensor(w_lo[n][:, :, :], probs[:, i % 2], w_hi[n][:, :, :],
                                  ALU.subtract).then_inc(w_used, 1)
            dve.memset(ks[STACK:P, :, :, :].bitcast(F32), 1.0).then_inc(ones_set, 1)
            ln_chain = Chain(dve, ln_v, 2 * TT)

            def apply(t, n):
                dve.wait_ge(rstd_ready, t.at(TT, n + 1))
                dve.tensor_scalar(x_tok[:, n, :], x_tok[:, n, :], mv[:, n, 0:1], rstd[:, 1, n:n + 1],
                                  ALU.subtract, ALU.mult).then_inc(x2_ready, 1)

            def step(what, t, part):
                kind, i, j, h = what
                if kind == "c":
                    dve.wait_ge(c_hi_s, t.at(KT, i + 1))
                    dve.tensor_tensor(c_lo[:, i, :], land[:, i % 2, :], c_hi[:, i, :],
                                      ALU.subtract).then_inc(c_split, 1)
                elif kind == "xt":
                    dve.wait_ge(xt_hi_s, t.at(TT, i + 1))
                    cols = slice(i * P, (i + 1) * P)
                    dve.tensor_tensor(xt_lo[:, :, cols], bank(what)[:, :].rearrange("p (k n) -> p k n", n=P),
                                      xt_hi[:, :, cols], ALU.subtract).then_inc(xt_split, 1)
                elif kind == "qk":
                    dve.wait_ge(qk_hi_s[j], t.at(KT, i + 1))
                    dve.scalar_tensor_tensor(out=qk_lo[:, j, i % 2, :], in0=bank(what)[:, :],
                                             scalar=bcol[:, j, i:i + 1], in1=qk_hi[:, j, i % 2, :].bitcast(F32),
                                             op0=ALU.add, op1=ALU.subtract).then_inc(qk_split[j], 1)
                elif kind == "v":
                    dve.wait_ge(v_done, t.at(TT, i + 1))
                    if i == 0:
                        if part == "start":
                            dve.wait_ge(small_in, N_SMALL)
                        if not t.first():
                            dve.wait_ge(av_done, t.at(UNITS, 0))
                    dve.tensor_tensor(v[:, i, :], bank(what)[:, :], brow[:, 0, :], ALU.add).then_inc(v_ready, 1)
                elif kind == "p1":
                    for hh in (2 * h, 2 * h + 1):
                        dve.wait_ge(p1_done, t.at(AG * UNITS, AG * (TT * i + j) + hh + 1))
                        if hh == 0 and j == 0 and (i >= 2 or not t.first()):
                            dve.wait_ge(neg_done, t.at(KT, i - 1))
                        dve.tensor_reduce(mx[:, i % 2, j, hh:hh + 1], bank((kind, i, j, hh))[:, :], AX.X,
                                          ALU.max).then_inc(mx_ready, 1)
                elif kind == "neg":
                    dve.wait_ge(neg_done, t.at(KT, i + 1))
                    if i or not t.first():
                        dve.wait_ge(neg_in[(i - 1) % 2], t.at(32 * KT // 2, 32 * ((i + 1) // 2)))
                    src = bank(what)[0:AG, :]
                    dve.tensor_scalar(neg_hi[:, :], src, -1.0, None, ALU.mult).then_inc(neg_v, 1)
                    dve.wait_ge(neg_v, t.at(KT, i + 1))
                    dve.scalar_tensor_tensor(out=neg_lo[:, :], in0=src, scalar=-1.0, in1=neg_hi[:, :].bitcast(F32),
                                             op0=ALU.mult, op1=ALU.subtract).then_inc(neg_ready, 1)
                elif kind == "norm":
                    if j == 0:
                        dve.wait_ge(o_copied, t.at(KT, i + 1))
                    cols = slice(j * P, (j + 1) * P)
                    dve.reciprocal(den[:, cols], den[:, cols]).then_inc(o_v, 1)
                    if j == TT - 1:
                        dve.wait_ge(o_v, t.at(KT * TT, TT * (i + 1)))
                        dve.tensor_tensor(o[:, i, :], o[:, i, :], den[:, :], ALU.mult).then_inc(o_ready, 1)
                elif kind == "out":
                    if i == 0:
                        ln_chain.start(t.number())
                        dve.wait_ge(xb_ready, t.at(1, 1))
                    dve.wait_ge(out_done, t.at(TT, i + 1))
                    dve.tensor_tensor(x_tok[:, i, :], bank(what)[:, :], x_tok[:, i, :],
                                      ALU.add).then_inc(out_read, 1)
                    dve.wait_ge(out_read, t.at(TT, i + 1))
                    ln_chain.link(dve.bn_stats(stats[:, i, :], x_tok[:, i, :]), (const, 3))
                    ln_chain.link(dve.bn_aggr(mv[:, i, :], stats[:, i, :]))
                    dve.tensor_scalar(rstd[:, 0, i:i + 1], mv[:, i, 1:2], LN_EPS, None, ALU.add).then_inc(var_ready, 1)
                    if i:
                        apply(t, i - 1)
                elif kind == "end":
                    apply(t, TT - 1)

            over_attention(dve, n_seq, step, steps)

        @block.tensor
        def _(pe):
            pe.wait_ge(const, 3)
            pe.wait_ge(ones_set, 1)

            def take(part, use, t):
                past = before[part, use]
                if past:
                    s, per, count = reader(*past[0])
                    pe.wait_ge(s, Turn(t.b, t.phase, past[1]).at(per, count))

            def project(part, what, t, w, x_parts, cols, w_moves, done):
                take(part, what, t)
                wh, wl = w
                for k in range(KT):
                    for n, (wp, xp) in enumerate(((wh, x_parts[0]), (wh, x_parts[1]), (wl, x_parts[0]))):
                        pair = ((xp[:, k, cols], wp[:, k, :]) if w_moves else (wp[:, k, cols], xp[:, k, :]))
                        ins = pe.matmul(bank(what)[:, :], *pair, start=(k == n == 0), stop=(k == KT - 1 and n == 2))
                ins.then_inc(done, 1)

            def step(what, t, part):
                kind, i, j, h = what
                tile = slice(i * P, (i + 1) * P)
                if kind == "xt":
                    pe.wait_ge(landed[i % 2], t.at(64, 32 + 16 * (i // 2 + 1)))
                    take(part, what, t)
                    for k in range(KT):
                        ins = pe.transpose(bank(what)[:, k * P:(k + 1) * P], land[:, i % 2, k * P:(k + 1) * P],
                                           ident[:, :])
                    ins.then_inc(xt_done, 1)
                elif kind == "qk":
                    if i == 0:
                        pe.wait_ge(*((c_split, t.at(KT, KT)) if j else (xt_split, t.at(TT, TT))))
                    n = names[j]
                    project(part, what, t, (w_hi[n], w_lo[n]), (c_hi, c_lo) if j else (xt_hi, xt_lo),
                            tile, False, qk_done[j])
                elif kind == "v":
                    project(part, what, t, (w_hi["v"], w_lo["v"]), (c_hi, c_lo), tile, True, v_done)
                elif kind == "p1":
                    if j == 0 and h == 0:
                        stack_filled(pe, i, t)
                    for hh in (2 * h, 2 * h + 1):
                        use = (kind, i, j, hh)
                        take(part, use, t)
                        pe.matmul(bank(use)[:, :], qs[0:STACK, t.slot(i), hh, j * P:(j + 1) * P],
                                  ks[0:STACK, t.slot(i), hh, :], start=True, stop=True).then_inc(p1_done, 1)
                elif kind == "neg":
                    take(part, what, t)
                    pe.wait_ge(mx_ready, t.at(AG * UNITS, AG * TT * (i + 1)))
                    for n in range(TT):
                        ins = pe.transpose(bank(what)[0:AG, n * P:(n + 1) * P], mx[:, i % 2, n, :], ident[:, :])
                    ins.then_inc(neg_done, 1)
                elif kind == "st":
                    n = TT * i + j
                    if j == 0:
                        pe.wait_ge(neg_in[i % 2], t.at(32 * KT // 2, 32 * (i // 2 + 1)))
                    for hh in range(AG):
                        if hh % 2 == 0 and (n or not t.first()):
                            pe.wait_ge(exp_ready, t.at(2 * UNITS, 2 * n + hh // 2 - 1))
                        ins = pe.matmul(sp_banks[:, hh, :], ks[0:STACK + 2, t.slot(i), hh, j * P:(j + 1) * P],
                                        qs[0:STACK + 2, t.slot(i), hh, :], start=True, stop=True)
                        if hh % 2:
                            ins.then_inc(st_done, 1)
                elif kind == "av":
                    n = TT * i + j
                    if h == 0:
                        pe.wait_ge(exp_ready, t.at(2 * UNITS, 2 * n + 2))
                        if n == 0:
                            pe.wait_ge(v_ready, t.at(TT, TT))
                        if j == 0 and (i or not t.first()):
                            pe.wait_ge(o_copied, t.at(KT, i))
                    for hh in range(AG):
                        rows = slice(hh * AD, (hh + 1) * AD)
                        if h == 0:
                            pe.matmul(o_bank[rows, :], v[:, j, i * P + hh * AD:i * P + (hh + 1) * AD],
                                      probs[:, n % 2, hh, :], start=(j == 0), stop=(j == TT - 1))
                        else:
                            ins = pe.matmul(den_bank[rows, :], onesf[:, 0:AD], probs[:, n % 2, hh, :],
                                            start=(j == 0), stop=(j == TT - 1))
                    if h:
                        ins.then_inc(av_done, 1)
                elif kind == "out":
                    if i == 0:
                        pe.wait_ge(o_ready, t.at(KT, KT))
                    take(part, what, t)
                    for k in range(KT):
                        ins = pe.matmul(bank(what)[:, :], o[:, k, tile], w_o[:, k, :], start=(k == 0),
                                        stop=(k == KT - 1))
                    ins.then_inc(out_done, 1)

            over_attention(pe, n_seq, step, steps)


NE = 16
SL = 16
SLOTS = NE * SL
ST_TILES = SLOTS // P
EH = 128
W_SLOTS = 4
NORM_EPS = 1e-12


def is_zero(b):
    return isinstance(b, int) and b == 0


def at_pair(b, p, per):
    return (b - p) * (per // 2) + per


def over_pairs(eng, count, front, back):
    front(0, 0, True)
    front(1, 1, True)
    back(0, 0, True)
    if count > 2:
        with eng.Fori(0, count // 2 - 1) as i:
            front(i * 2 + 2, 0, False)
            back(i * 2 + 1, 1, False)
            front(i * 2 + 3, 1, False)
            back(i * 2 + 2, 0, False)
    back(count - 1, 1, False)


def nothing(b, p):
    pass


def over_routed(eng, count, turn=nothing, start=nothing, back=nothing, mid=nothing):
    def step(b, p, before):
        turn(before, 1 - p)
        start(b, p)
        back(before, 1 - p)
        mid(b, p)

    start(0, 0)
    mid(0, 0)
    step(1, 1, 0)
    if count > 2:
        with eng.Fori(1, count // 2) as i:
            step(i * 2, 0, i * 2 - 1)
            step(i * 2 + 1, 1, i * 2)
    turn(count - 1, 1)
    back(count - 1, 1)


def moe_stage(nc, n_seq, x2, gamma, beta, mu, scale, w1, b1, w2, b2, combine_t, slot_out, x3):
    with ExitStack() as ctx:
        def sb(name, shape, dt=F32):
            return ctx.enter_context(nc.sbuf_tensor("e_" + name, shape, dt))

        def ps(name, shape=(P, 512)):
            return ctx.enter_context(nc.psum_tensor("e_" + name, list(shape), F32))

        def sem(name):
            return ctx.enter_context(nc.semaphore("e_" + name))

        grow = sb("grow", [P, DM])
        berow = sb("berow", [P, DM])
        mu_u = sb("mu_u", [P, KT, SLOTS])
        mu_sq = sb("mu_sq", [P, KT, SLOTS])
        mu_n = sb("mu_n", [P, 2, SLOTS])
        scol = sb("scol", [P, 1])
        b1col = sb("b1col", [P, NE])
        b2t = sb("b2t", [P, ST_TILES, DM])
        ident = sb("ident", [P, P])
        onesf = sb("onesf", [P, P])
        neg_half = sb("neg_half", [P, SLOTS])
        x = sb("x", [P, 2, TT, DM])
        stats = sb("stats", [P, TT, 6])
        mv = sb("mv", [P, TT, 2])
        rstd = sb("rstd", [P, 2, TT])
        junk = sb("junk", [P, TT, DM])
        ss = sb("ss", [P, 3, TT])
        rs = sb("rs", [P, TT])
        xnt = sb("xnt", [P, KT, SEQ])
        lg = sb("lg", [P, TT, SLOTS])
        disp_t = sb("disp_t", [P, ST_TILES, SEQ])
        disp = sb("disp", [P, TT, SLOTS])
        comb = sb("comb", [P, TT, SLOTS])
        mxd = sb("mxd", [P, 2, ST_TILES])
        sd = sb("sd", [P, 2, ST_TILES])
        mxc = sb("mxc", [P, TT])
        neg_mxc = sb("neg_mxc", [P, TT])
        sc = sb("sc", [P, TT])
        rc_all = sb("rc_all", [P, n_seq, TT])
        comb_t = sb("comb_t", [P, ST_TILES, SEQ])
        slots_t = sb("slots_t", [P, KT, NE, n_seq, SL])
        w1s = sb("w1s", [P, W_SLOTS, KT, EH])
        w2s = sb("w2s", [P, W_SLOTS, DM])
        hs = sb("hs", [P, 2, P])
        so = sb("so", [P, 2, DM])
        so_in = sb("so_in", [P, 2, ST_TILES, DM])
        ct_in = sb("ct_in", [P, 2, ST_TILES, SEQ])
        rows = n_seq * SL

        turn = [ps("turn0"), ps("turn1")]
        lg_ps = ps("lg_ps", (P, TT, SLOTS))
        sl_ps = ps("sl_ps", (P, KT, SLOTS))
        ct_ps = ps("ct_ps", (P, ST_TILES, SEQ))

        const = sem("const")
        small_in = sem("small_in")
        mu_s = sem("mu_s")
        mu_ready = sem("mu_ready")
        x_in = [sem("x_in0"), sem("x_in1")]
        var_ready = sem("var_ready")
        rstd_ready = sem("rstd_ready")
        xg_ready = sem("xg_ready")
        xn_ready = sem("xn_ready")
        ss_ready = sem("ss_ready")
        ssb_ready = sem("ssb_ready")
        rn_ready = sem("rn_ready")
        rs_ready = sem("rs_ready")
        turn_done = sem("turn_done")
        turn_read = sem("turn_read")
        lg_done = sem("lg_done")
        lg_read = sem("lg_read")
        mx_ready = sem("mx_ready")
        mc_ready = sem("mc_ready")
        dn_ready = sem("dn_ready")
        disp_turned = sem("disp_turned")
        comb_ready = sem("comb_ready")
        disp_ready = sem("disp_ready")
        ln1_v = sem("ln1_v")
        sums_v = sem("sums_v")
        rc_ready = sem("rc_ready")
        ct_done = sem("ct_done")
        ct_read = sem("ct_read")
        ct_out = sem("ct_out")
        sl_done = sem("sl_done")
        sl_read = sem("sl_read")
        w_in = [sem(f"w_in{i}") for i in range(W_SLOTS)]
        h_done = sem("h_done")
        h_ready = sem("h_ready")
        e_done = sem("e_done")
        so_ready = sem("so_ready")
        so_out = [sem("so_out0"), sem("so_out1")]
        mu_done = sem("mu_done")
        c_in = [sem("c_in0"), sem("c_in1")]
        b2_added = sem("b2_added")
        x3_out = sem("x3_out")

        out_banks = [sl_ps[:, 0:2, :], sl_ps[:, 2:4, :], ct_ps[:, 0, :], ct_ps[:, 1, :]]

        def out_bank(e):
            return out_banks[e % 2].rearrange("p a n -> p (a n)")

        def c_bank(t):
            return out_bank(t) if t < 2 else out_banks[t]

        def second(pe, e):
            pe.wait_ge(h_ready, e + 1)
            if e >= 2:
                pe.wait_ge(so_ready, e - 1)
            pe.matmul(out_bank(e)[0:rows, :], hs[:, e % 2, 0:rows], w2s[:, e % W_SLOTS, :],
                      start=True, stop=True).then_inc(e_done, 1)

        out_done, out_read, var2_ready, rstd2_ready = lg_done, lg_read, var_ready, rstd_ready
        x3_ready, residual_in = xg_ready, x_in
        routed = n_seq

        block = ctx.enter_context(nc.Block())
        N_SMALL = 5 + NE
        TURNS = KT + ST_TILES

        @block.sync
        def _(sp):
            sp.dma_start(mu_u[:, :, :], mu.rearrange("(k p) n -> p k n", p=P)).then_inc(small_in, 16)
            sp.dma_start(grow[:, :], gamma.partition_broadcast(P)).then_inc(small_in, 16)
            sp.dma_start(berow[:, :], beta.partition_broadcast(P)).then_inc(small_in, 16)
            sp.dma_start(scol[:, :], scale.partition_broadcast(P)).then_inc(small_in, 16)
            sp.dma_start(b1col[:, :], b1).then_inc(small_in, 16)
            for e in range(NE):
                e0 = (e * SL) % P
                sp.dma_start(b2t[e0:e0 + SL, e * SL // P, :], b2[e].partition_broadcast(SL)).then_inc(small_in, 16)

            def load_expert(e):
                s = e % W_SLOTS
                if e >= W_SLOTS:
                    sp.wait_ge(e_done, e - W_SLOTS + 1)
                sp.dma_start(w1s[:, s], w1[e].rearrange("(k p) h -> p k h", p=P)).then_inc(w_in[s], 16)
                sp.dma_start(w2s[:, s], w2[e]).then_inc(w_in[s], 16)

            def store(e):
                sp.wait_ge(so_ready, e + 1)
                sp.dma_start(slot_out[e].rearrange("b s d -> (b s) d"), so[0:rows, e % 2, :]
                             ).then_inc(so_out[e % 2], 16)

            for e in range(W_SLOTS):
                load_expert(e)

            def load_x(b, p, landed):
                sp.dma_start(x[:, p], one(x2, b).rearrange("a (t p) n -> p (a t) n", p=P)).then_inc(landed[p], 16)

            def start(b, p):
                if not (isinstance(b, int) and b < 2):
                    sp.wait_ge(sl_done, at(b, 1, -1))
                load_x(b, p, x_in)

            def back(b, p):
                sp.wait_ge(ct_read, at(b, ST_TILES, ST_TILES))
                sp.dma_start(one(combine_t, b).rearrange("a (j p) n -> p (a j) n", p=P), comb_t[:, :, :]
                             ).then_inc(ct_out, 16)

            over_routed(sp, n_seq, start=start, back=back)

            for e in range(NE):
                if e >= W_SLOTS:
                    load_expert(e)
                store(e - 1) if e else None
            store(NE - 1)
            for p in range(2):
                sp.wait_ge(so_out[p], 16 * NE // 2)
            sp.wait_ge(ct_out, 16 * n_seq)

            def combine(b, p, first):
                if not first:
                    sp.wait_ge(out_done, routed + at(b, TT, -TT))
                    sp.wait_ge(x3_out, at(b, 16 * TT, -16 * TT))
                src = slot_out.rearrange("e b s d -> b e s d")
                for j in range(ST_TILES):
                    n = P // SL
                    for e in range(n):
                        sp.dma_start(so_in[e * SL:(e + 1) * SL, p, j, :],
                                     one(src, b)[:, j * n + e].rearrange("a s d -> (a s) d")).then_inc(c_in[p], 16)
                sp.dma_start(ct_in[:, p], one(combine_t, b).rearrange("a (j p) n -> p (a j) n", p=P)
                             ).then_inc(c_in[p], 16)
                load_x(b, p, residual_in)

            def stores(b, p, first):
                for t in range(TT):
                    sp.wait_ge(x3_ready, routed + at(b, TT, t + 1))
                    sp.dma_start(one(x3, b)[:, t * P:(t + 1) * P, :].rearrange("a p n -> p (a n)"),
                                 x[:, p, t, :]).then_inc(x3_out, 16)

            over_pairs(sp, n_seq, combine, stores)
            sp.wait_ge(x3_out, 16 * TT * n_seq)

        @block.gpsimd
        def _(pool):
            pool.memset(onesf[:, :], 1.0).then_inc(const, 1)
            pool.memset(neg_half[:, :], -0.5).then_inc(const, 1)
            pool.wait_ge(const, 2)
            pool.affine_select(out=ident[:, :], in_=onesf[:, :], compare_op=ALU.is_equal, fill=0.0,
                               base=0, pattern=[[-1, P]], channel_multiplier=1).then_inc(const, 1)
            pool.wait_ge(mu_s, 2)
            pool.tensor_tensor(mu_n[:, 1], mu_n[:, 0], neg_half[:, :], ALU.pow).then_inc(mu_s, 1)

            def start(b, p):
                pool.wait_ge(var_ready, at(b, 1, 1))
                pool.tensor_tensor(rstd[:, 1], rstd[:, 0], neg_half[:, 0:TT], ALU.pow).then_inc(rstd_ready, 1)
                pool.wait_ge(xg_ready, at(b, 1, 1))
                pool.tensor_tensor(x[:, p], x[:, p], berow[:, :].unsqueeze(1).to_broadcast([P, TT, DM]),
                                   ALU.add).then_inc(xn_ready, 1)
                pool.wait_ge(ssb_ready, at(b, 1, 1))
                pool.tensor_tensor(ss[:, 2], ss[:, 1], neg_half[:, 0:TT], ALU.pow).then_inc(rn_ready, 1)

            over_routed(pool, n_seq, start=start)

            def combine(b, p, first):
                pool.wait_ge(c_in[p], at_pair(b, p, 16 * (NE + 1)))
                pool.tensor_tensor(so_in[:, p], so_in[:, p], b2t[:, :, :], ALU.add).then_inc(b2_added, 1)

            def powers(b, p, first):
                for t in range(TT):
                    pool.wait_ge(var2_ready, routed + at(b, TT, t + 1))
                    pool.tensor_tensor(rstd[:, 1, t:t + 1], rstd[:, 0, t:t + 1], neg_half[:, 0:1],
                                       ALU.pow).then_inc(rstd2_ready, 1)

            over_pairs(pool, n_seq, combine, powers)

        @block.scalar
        def _(act):
            act.wait_ge(small_in, 16 * N_SMALL)
            act.activation(mu_sq[:, :, :], mu_u[:, :, :], ACT.Square).then_inc(mu_s, 1)

            def start(b, p):
                act.wait_ge(xn_ready, at(b, 1, 1))
                for t in range(TT):
                    ins = act.activation(junk[:, t, :], x[:, p, t, :], ACT.Square, accum_out=ss[:, 0, t:t + 1])
                ins.then_inc(ss_ready, 1)
                for k in range(KT):
                    act.wait_ge(turn_done, at(b, TURNS, k + 1))
                    act.activation(xnt[:, k, :], turn[k % 2][:, :], ACT.Copy).then_inc(turn_read, 1)
                act.wait_ge(lg_done, at(b, 1, 1))
                act.wait_ge(rs_ready, at(b, 1, 1))
                for t in range(TT):
                    ins = act.activation(lg[:, t, :], lg_ps[:, t, :], ACT.Identity, scale=rs[:, t:t + 1])
                ins.then_inc(lg_read, 1)

            def back(b, p):
                for j in range(ST_TILES):
                    act.wait_ge(ct_done, at(b, ST_TILES, j + 1))
                    if j == 0 and not is_zero(b):
                        act.wait_ge(ct_out, at(b, 16, 0))
                    act.activation(comb_t[:, j, :], ct_ps[:, j, :], ACT.Copy).then_inc(ct_read, 1)

            def mid(b, p):
                for j in range(ST_TILES):
                    act.wait_ge(turn_done, at(b, TURNS, KT + j + 1))
                    act.wait_ge(mx_ready, at(b, ST_TILES, j + 1))
                    act.activation(disp_t[:, j, :], turn[j % 2][:, :], ACT.Exp, bias=mxd[:, 1, j:j + 1],
                                   accum_out=sd[:, 0, j:j + 1]).then_inc(turn_read, 1)
                act.wait_ge(mc_ready, at(b, 1, 1))
                for t in range(TT):
                    ins = act.activation(comb[:, t, :], lg[:, t, :], ACT.Exp, bias=neg_mxc[:, t:t + 1],
                                         accum_out=sc[:, t:t + 1])
                ins.then_inc(comb_ready, 1)

            over_routed(act, n_seq, start=start, back=back, mid=mid)

            for e in range(NE):
                act.wait_ge(h_done, e + 1)
                if e >= 2:
                    act.wait_ge(e_done, e - 1)
                act.activation(hs[:, e % 2, 0:rows], turn[e % 2][:, 0:rows], ACT.Gelu,
                               bias=b1col[:, e:e + 1]).then_inc(h_ready, 1)

        @block.vector
        def _(dve):
            dve.wait_ge(mu_done, 1)
            dve.tensor_scalar(mu_n[:, 0], lg_ps[:, 0, :], NORM_EPS ** 2, None, ALU.max).then_inc(mu_s, 1)
            dve.wait_ge(mu_s, 3)
            for k in range(KT):
                ins = dve.tensor_tensor(mu_u[:, k, :], mu_u[:, k, :], mu_n[:, 1], ALU.mult)
            ins.then_inc(mu_ready, 1)
            ln = Chain(dve, ln1_v, 3)
            sums = Chain(dve, sums_v, 2 * ST_TILES + 1)

            def start(b, p):
                ln.start(b)
                dve.wait_ge(x_in[p], at_pair(b, p, 16))
                for t in range(TT):
                    ins = dve.bn_stats(stats[:, t, :], x[:, p, t, :])
                ln.link(ins, (const, 3))
                for t in range(TT):
                    ins = dve.bn_aggr(mv[:, t, :], stats[:, t, :])
                ln.link(ins)
                dve.tensor_scalar(rstd[:, 0], mv[:, :, 1], LN_EPS, None, ALU.add).then_inc(var_ready, 1)
                dve.wait_ge(rstd_ready, at(b, 1, 1))
                for t in range(TT):
                    ins = dve.tensor_scalar(x[:, p, t, :], x[:, p, t, :], mv[:, t, 0:1], rstd[:, 1, t:t + 1],
                                            ALU.subtract, ALU.mult)
                ln.link(ins)
                dve.tensor_tensor(x[:, p], x[:, p], grow[:, :].unsqueeze(1).to_broadcast([P, TT, DM]),
                                  ALU.mult).then_inc(xg_ready, 1)
                ln.end()
                dve.wait_ge(ss_ready, at(b, 1, 1))
                dve.tensor_scalar(ss[:, 1], ss[:, 0], NORM_EPS ** 2, None, ALU.max).then_inc(ssb_ready, 1)
                dve.wait_ge(rn_ready, at(b, 1, 1))
                dve.tensor_scalar(rs[:, :], ss[:, 2], scol[:, 0:1], None, ALU.mult).then_inc(rs_ready, 1)

            def mid(b, p):
                sums.start(b)
                for j in range(ST_TILES):
                    dve.wait_ge(turn_done, at(b, TURNS, KT + j + 1))
                    sums.link(dve.tensor_reduce(mxd[:, 0, j:j + 1], turn[j % 2][:, :], AX.X, ALU.max))
                    dve.tensor_scalar(mxd[:, 1, j:j + 1], mxd[:, 0, j:j + 1], -1.0, None, ALU.mult
                                      ).then_inc(mx_ready, 1)
                sums.link(dve.tensor_reduce(mxc[:, :], lg[:, :, :], AX.X, ALU.max))
                dve.tensor_scalar(neg_mxc[:, :], mxc[:, :], -1.0, None, ALU.mult).then_inc(mc_ready, 1)
                for j in range(ST_TILES):
                    dve.wait_ge(turn_read, at(b, TURNS, KT + j + 1))
                    sums.link(dve.reciprocal(sd[:, 1, j:j + 1], sd[:, 0, j:j + 1]))
                    ins = dve.tensor_scalar(disp_t[:, j, :], disp_t[:, j, :], sd[:, 1, j:j + 1], None, ALU.mult)
                ins.then_inc(dn_ready, 1)
                dve.wait_ge(comb_ready, at(b, 1, 1))
                dve.reciprocal(rc_all[:, bass.ds(b, 1), :].rearrange("p a t -> p (a t)"), sc[:, :]
                               ).then_inc(rc_ready, 1)
                sums.end()

            def turned(b, p):
                dve.wait_ge(disp_turned, at(b, 1, 1))
                for half in range(2):
                    t2 = slice(half * TT // 2, (half + 1) * TT // 2)
                    ins = dve.tensor_copy(disp[:, t2, :], lg_ps[:, t2, :])
                ins.then_inc(disp_ready, 1)

            def back(b, p):
                dve.wait_ge(sl_done, at(b, 1, 1))
                for k in range(KT):
                    ins = dve.tensor_copy(slots_t[:, k, :, bass.ds(b, 1), :].rearrange("p e a s -> p e (a s)"),
                                          sl_ps[:, k, :].rearrange("p (e s) -> p e s", s=SL))
                ins.then_inc(sl_read, 1)

            over_routed(dve, n_seq, turn=turned, start=start, back=back, mid=mid)

            for e in range(NE):
                dve.wait_ge(e_done, e + 1)
                if e >= 2:
                    dve.wait_ge(so_out[e % 2], 16 * (e // 2))
                dve.tensor_copy(so[0:rows, e % 2, :], out_bank(e)[0:rows, :]).then_inc(so_ready, 1)

            ln_chain = Chain(dve, ln1_v, 2 * TT, 3 * n_seq)

            def output(b, p, first):
                ln_chain.start(b)
                dve.wait_ge(residual_in[p], 16 * n_seq // 2 + at_pair(b, p, 16))

                def apply(t):
                    dve.wait_ge(rstd2_ready, routed + at(b, TT, t + 1))
                    dve.tensor_scalar(x[:, p, t, :], x[:, p, t, :], mv[:, t, 0:1], rstd[:, 1, t:t + 1],
                                      ALU.subtract, ALU.mult).then_inc(x3_ready, 1)

                for t in range(TT):
                    dve.wait_ge(out_done, routed + at(b, TT, t + 1))
                    dve.scalar_tensor_tensor(out=x[:, p, t, :], in0=c_bank(t)[:, :],
                                             scalar=rc_all[:, bass.ds(b, 1), t:t + 1].rearrange("p a t -> p (a t)"),
                                             in1=x[:, p, t, :], op0=ALU.mult, op1=ALU.add).then_inc(out_read, 1)
                    dve.wait_ge(out_read, routed + at(b, TT, t + 1))
                    ln_chain.link(dve.bn_stats(stats[:, t, :], x[:, p, t, :]), (const, 3))
                    ln_chain.link(dve.bn_aggr(mv[:, t, :], stats[:, t, :]))
                    dve.tensor_scalar(rstd[:, 0, t:t + 1], mv[:, t, 1:2], LN_EPS, None, ALU.add).then_inc(var2_ready, 1)
                    if t:
                        apply(t - 1)
                apply(TT - 1)
                ln_chain.end()

            over_pairs(dve, n_seq, lambda b, p, first: None, output)

        @block.tensor
        def _(pe):
            pe.wait_ge(const, 3)
            pe.wait_ge(mu_s, 1)
            for k in range(KT):
                ins = pe.matmul(lg_ps[:, 0, :], onesf[:, :], mu_sq[:, k, :], start=(k == 0), stop=(k == KT - 1))
            ins.then_inc(mu_done, 1)
            pe.wait_ge(mu_ready, 1)

            def turned(b, p):
                pe.wait_ge(dn_ready, at(b, 1, 1))
                for t in range(TT):
                    for j in range(ST_TILES):
                        ins = pe.transpose(lg_ps[:, t, j * P:(j + 1) * P], disp_t[:, j, t * P:(t + 1) * P],
                                           ident[:, :])
                ins.then_inc(disp_turned, 1)

            def free_turn(b, n):
                if n >= 2 or not is_zero(b):
                    pe.wait_ge(turn_read, at(b, TURNS, n - 1))

            def start(b, p):
                pe.wait_ge(xn_ready, at(b, 1, 1))
                for k in range(KT):
                    free_turn(b, k)
                    for t in range(TT):
                        ins = pe.transpose(turn[k % 2][:, t * P:(t + 1) * P], x[:, p, t, k * P:(k + 1) * P],
                                           ident[:, :])
                    ins.then_inc(turn_done, 1)
                pe.wait_ge(turn_read, at(b, TURNS, KT))
                if not is_zero(b):
                    pe.wait_ge(disp_ready, at(b, 1, 0))
                for t in range(TT):
                    for k in range(KT):
                        ins = pe.matmul(lg_ps[:, t, :], xnt[:, k, t * P:(t + 1) * P], mu_u[:, k, :],
                                        start=(k == 0), stop=(k == KT - 1))
                ins.then_inc(lg_done, 1)

            def mid(b, p):
                pe.wait_ge(lg_read, at(b, 1, 1))
                for j in range(ST_TILES):
                    free_turn(b, KT + j)
                    for t in range(TT):
                        ins = pe.transpose(turn[j % 2][:, t * P:(t + 1) * P], lg[:, t, j * P:(j + 1) * P],
                                           ident[:, :])
                    ins.then_inc(turn_done, 1)

            def back(b, p):
                pe.wait_ge(comb_ready, at(b, 1, 1))
                if not is_zero(b):
                    pe.wait_ge(ct_read, at(b, ST_TILES, 0))
                for j in range(ST_TILES):
                    for t in range(TT):
                        ins = pe.transpose(ct_ps[:, j, t * P:(t + 1) * P], comb[:, t, j * P:(j + 1) * P],
                                           ident[:, :])
                    ins.then_inc(ct_done, 1)
                pe.wait_ge(disp_ready, at(b, 1, 1))
                if not is_zero(b):
                    pe.wait_ge(sl_read, at(b, 1, 0))
                for k in range(KT):
                    for t in range(TT):
                        ins = pe.matmul(sl_ps[:, k, :], x[:, p, t, k * P:(k + 1) * P], disp[:, t, :],
                                        start=(t == 0), stop=(t == TT - 1))
                ins.then_inc(sl_done, 1)

            over_routed(pe, n_seq, turn=turned, start=start, back=back, mid=mid)

            pe.wait_ge(sl_read, n_seq)
            for e in range(NE):
                s = e % W_SLOTS
                pe.wait_ge(w_in[s], 32 * (e // W_SLOTS + 1))
                if e >= 2:
                    pe.wait_ge(h_ready, e - 1)
                for k in range(KT):
                    ins = pe.matmul(turn[e % 2][:, 0:rows], w1s[:, s, k, :],
                                    slots_t[:, k, e].rearrange("p b s -> p (b s)"), start=(k == 0), stop=(k == KT - 1))
                ins.then_inc(h_done, 1)
                if e:
                    second(pe, e - 1)
            second(pe, NE - 1)

            def combine(b, p, first):
                pe.wait_ge(b2_added, at(b, 1, 1))
                for t in range(TT):
                    if not is_zero(b):
                        pe.wait_ge(out_read, routed + at(b, TT, t + 1 - TT))
                    elif t == 0:
                        pe.wait_ge(so_ready, NE)
                    for j in range(ST_TILES):
                        ins = pe.matmul(c_bank(t)[:, :], ct_in[:, p, j, t * P:(t + 1) * P], so_in[:, p, j, :],
                                        start=(j == 0), stop=(j == ST_TILES - 1))
                    ins.then_inc(out_done, 1)

            over_pairs(pe, n_seq, lambda b, p, first: None, combine)


def decoder(nc, n_seq, a, out):
    def scratch(name, shape):
        return nc.dram_tensor(name, shape, F32, kind="Internal").ap()

    x1 = scratch("x1", [n_seq, SEQ, DM])
    x2 = scratch("x2", [n_seq, SEQ, DM])
    combine_t = scratch("combine_t", [n_seq, SLOTS, SEQ])
    slot_out = scratch("slot_out", [NE, n_seq, SL, DM])
    mamba_stage(nc, n_seq, a["x_t"], a["x"], a["w_in_t"], a["conv_w"], a["conv_b"], a["dt_bias"], a["a_log"],
                a["d_skip"], a["norm_w"], a["w_out_t"], x1)
    attention_stage(nc, n_seq, x1, a["context_t"], [a["wq_t"], a["wk_t"], a["wv_t"], a["wo_t"]], a["b_qk"],
                    [a["bv"], a["bo"]], x2)
    moe_stage(nc, n_seq, x2, a["gamma"], a["beta"], a["mu"], a["scale"], a["w1"], a["b1_t"], a["w2"], a["b2"],
              combine_t, slot_out, out)


def lay_out(inputs):
    i = {name: np.asarray(v) for name, v in inputs.items()}
    m, t, f = "L0_attn_", "L0_xattn_", "L0_ffn_"
    di, ds = 2 * DM, 64
    z, x, bm, cm, dt = np.split(i[m + "W_in"], [di, 2 * di, 2 * di + ds, 2 * di + 2 * ds])
    ch = (di + 2 * ds) // P
    a = {
        "x": i["x"], "x_t": i["x"].transpose(0, 2, 1), "context_t": i["ctx_1024"].transpose(0, 2, 1),
        "w_in_t": np.concatenate([dt, z, x, bm, cm]).T,
        "conv_w": i[m + "conv_w"].reshape(ch, P, -1).transpose(1, 0, 2),
        "conv_b": i[m + "conv_b"].reshape(ch, P).T,
        "dt_bias": i[m + "dt_bias"], "a_log": i[m + "A_log"],
        "d_skip": i[m + "D"].reshape(-1, 2).T, "norm_w": i[m + "norm_w"].reshape(-1, P).T,
        "w_out_t": i[m + "W_out"].T,
        "b_qk": np.stack([i[t + "bq"], i[t + "bk"]]).reshape(2, KT, P).transpose(2, 0, 1),
        "bv": i[t + "bv"], "bo": i[t + "bo"],
        "gamma": i[f + "ln_gamma"], "beta": i[f + "ln_beta"], "mu": i[f + "mu"].reshape(DM, SLOTS),
        "scale": i[f + "scale"], "w1": i[f + "w1"], "b1_t": i[f + "b1"].T, "w2": i[f + "w2"], "b2": i[f + "b2"],
    }
    for n in "qkvo":
        a[f"w{n}_t"] = i[t + "W" + n].T
    return {name: np.ascontiguousarray(v) for name, v in a.items()}


def kernel(**inputs):
    import concourse.bacc as bacc
    from concourse.bass_utils import run_bass_kernel_spmd

    nc = bacc.Bacc("TRN2", target_bir_lowering=False, num_devices=1)
    arrays = lay_out(inputs)
    a = {name: nc.dram_tensor(f"{name}_in", v.shape, mybir.dt.from_np(v.dtype), kind="ExternalInput").ap()
         for name, v in arrays.items()}
    n_seq = arrays["x"].shape[0]
    out = nc.dram_tensor("out", (n_seq, SEQ, DM), F32, kind="ExternalOutput").ap()
    decoder(nc, n_seq, a, out)
    result = run_bass_kernel_spmd(nc, [{f"{name}_in": v for name, v in arrays.items()}], core_ids=[0])
    return result.results[0]["out"]
```

```python
from contextlib import ExitStack

import numpy as np

import concourse.bass as bass
from concourse import mybir

F32 = mybir.dt.float32
F32R = mybir.dt.float32r
ALU = mybir.AluOpType
ACT = mybir.ActivationFunctionType
AX = mybir.AxisListType

P = 128
SEQ = 512
DM = 512
KT = DM // P
TT = SEQ // P
LN_EPS = 1e-5


def at(b, per, k):
    return b * per + k


def value(eng, n):
    return n if isinstance(n, int) else eng.bass.snap(n, engines=[eng.engine])


class Chain:

    def __init__(self, eng, sem, per, had=0):
        self.eng, self.sem, self.per, self.had = eng, sem, per, had

    def start(self, b, k=0):
        self.base, self.k = self.had + b * self.per, k

    def link(self, ins, before=None):
        ins.then_inc(self.sem, 1)
        self.k += 1
        if before:
            count = value(self.eng, self.base + self.k)
            met(self.eng, *before)
            self.eng.wait_ge(self.sem, count)
        else:
            self.eng.wait_ge(self.sem, self.base + self.k)

    def end(self):
        assert self.k == self.per, (self.k, self.per)


def met(eng, sem, value):
    eng.wait_ge(sem, value)


def over_sequences(eng, count, body):
    body(0, True)
    if count > 1:
        with eng.Fori(1, count) as i:
            body(i, False)


def over_overlapped(eng, count, head, body):
    head(0)
    body(0, True, True)
    if count > 2:
        with eng.Fori(1, count - 1) as i:
            body(i, False, True)
    body(count - 1, False, False)


def one(ap, b):
    return ap[bass.ds(b, 1)]


DI = 1024
NH = 16
HP = 64
NS = 64
XT_TILES = DI // P
CH = 4
HG = 4
NG = NH // HG
COLS = NH + 2 * DI + 2 * NS
COL_Z, COL_X, COL_BC = NH, NH + DI, NH + 2 * DI


def mamba_stage(nc, n_seq, xT, x, winT, conv_w, conv_b, dt_bias, a_log, d_skip, norm_w, woutT, x1):
    with ExitStack() as ctx:
        def sb(name, shape, dt=F32):
            return ctx.enter_context(nc.sbuf_tensor("m_" + name, shape, dt))

        def ps(name):
            return ctx.enter_context(nc.psum_tensor("m_" + name, [P, 512], F32))

        def sem(name):
            return ctx.enter_context(nc.semaphore("m_" + name))

        win_hi = sb("win_hi", [P, KT, COLS], F32R)
        win_lo = sb("win_lo", [P, KT, COLS], F32R)
        wout = sb("wout", [P, XT_TILES, DM])
        cw = sb("cw", [P, 9, 4])
        cb = sb("cb", [P, 9])
        dcol = sb("dcol", [P, XT_TILES])
        nw = sb("nw", [P, XT_TILES])
        dtb = sb("dtb", [P, NH])
        aneg = sb("aneg", [P, NH])
        tri = sb("tri", [P, P])
        strict = sb("strict", [P, P])
        ident = sb("ident", [P, P])
        onesf = sb("onesf", [P, P])
        strict_r = sb("strict_r", [P, P], F32R)
        ones_r = sb("ones_r", [P, P], F32R)
        neg_half = sb("neg_half", [P, TT])
        xt_in = sb("xt_in", [P, KT, SEQ])
        xt_hi = sb("xt_hi", [P, KT, SEQ], F32R)
        xt_lo = sb("xt_lo", [P, KT, SEQ], F32R)
        x_tok = sb("x_tok", [P, TT, DM])
        dt_ch = xt_in[0:32, 0, :]
        dt = sb("dt", [P, CH, NH])
        a = sb("a", [P, CH, NH])
        a_hi = sb("a_hi", [P, CH, NH])
        a_lo = sb("a_lo", [P, CH, NH])
        a_hr = sb("a_hr", [P, CH, NH], F32R)
        wd = sb("wd", [P, 2, CH, NH])
        wdt = sb("wdt", [P, CH, NH])
        acc = sb("acc", [P, 2, SEQ])
        xc = sb("xc", [P, 2, 2, SEQ])
        zs = sb("zs", [P, 2, 2, SEQ])
        bt = sb("bt", [NS, SEQ])
        ct = sb("ct", [NS, SEQ])
        b_tok = sb("b_tok", [P, CH, NS])
        gm = sb("gm", [P, CH, P])
        rhs_hi = sb("rhs_hi", [P, 2, HG, P], F32R)
        rhs_lo = sb("rhs_lo", [P, 2, HG, P], F32R)
        dec = sb("dec", [P, CH, HG, P])
        ce = sb("ce", [NS, CH - 1, HG, P])
        xk = sb("xk", [P, CH, HG, HP])
        xdt = sb("xdt", [P, CH, HG, HP])
        xw = sb("xw", [P, CH - 1, HG, HP])
        st = sb("st", [NS, CH - 1, HG, HP])
        g = sb("g", [P, XT_TILES, SEQ])
        sq = sb("sq", [P, 2, SEQ])
        sm = sq[:, 0, :].rearrange("p (i n) -> p i n", i=8)
        ssum = sb("ssum", [P, SEQ])
        rms = sb("rms", [P, 2, TT])
        stats = sb("stats", [P, TT, 6])
        mv = sb("mv", [P, TT, 2])
        rstd = sb("rstd", [P, 2, TT])
        half_w = COLS // 2
        g_flat = g[:, :, :].rearrange("p a b -> p (a b)")
        dec_flat = dec[:, :, :, :].rearrange("p c h n -> p (c h n)")
        staging = [[g_flat[:, n * half_w:(n + 1) * half_w] for n in range(2)],
                   [g_flat[:, 2 * half_w:3 * half_w], dec_flat[:, 0:half_w]]]

        proj = [ps("proj0"), ps("proj1")]
        seg = [ps("seg0"), ps("seg1")]
        misc, turn = ps("misc"), ps("turn")
        yp = [ps("y0"), ps("y1")]

        w_in = [sem("w_in0"), sem("w_in1")]
        w_used = sem("w_used")
        small_in = sem("small_in")
        const = sem("const")
        setup = sem("setup")
        setup_a = sem("setup_a")
        xt_landed = sem("xt_landed")
        xt_split = sem("xt_split")
        xt_hi_s = sem("xt_hi_s")
        x_in = sem("x_in")
        x_dbl = sem("x_dbl")
        tile_done = sem("tile_done")
        dt_read = sem("dt_read")
        dt_turned = sem("dt_turned")
        a_ready = sem("a_ready")
        sums_done = sem("sums_done")
        wd_ready = sem("wd_ready")
        wdt_ready = sem("wdt_ready")
        dtv = sem("dtv")
        dta = sem("dta")
        taps0 = sem("taps0")
        conv_read = sem("conv_read")
        conv_v = sem("conv_v")
        bc_ready = sem("bc_ready")
        xc_ready = sem("xc_ready")
        z_ready = sem("z_ready")
        bg_done = sem("bg_done")
        bg_read = sem("bg_read")
        rhs_ready = sem("rhs_ready")
        seg_done = sem("seg_done")
        dec_ready = sem("dec_ready")
        m_ready = sem("m_ready")
        ebc_done = sem("ebc_done")
        e_ready = sem("e_ready")
        ce_ready = sem("ce_ready")
        xk_done = sem("xk_done")
        xk_ready = sem("xk_ready")
        xdt_ready = sem("xdt_ready")
        xw_ready = sem("xw_ready")
        st_done = sem("st_done")
        st_v = sem("st_v")
        st_ready = sem("st_ready")
        y_done = sem("y_done")
        y_read = sem("y_read")
        g_ready = sem("g_ready")
        sq_ready = sem("sq_ready")
        sq_used = sem("sq_used")
        rms_done = sem("rms_done")
        rms_in = sem("rms_in")
        rms_ready = sem("rms_ready")
        out_done = sem("out_done")
        out_read = sem("out_read")
        ln_v = sem("ln_v")
        var_ready = sem("var_ready")
        rstd_ready = sem("rstd_ready")
        x1_ready = sem("x1_ready")
        x1_out = sem("x1_out")

        block = ctx.enter_context(nc.Block())
        N_SMALL = 7
        W_OUT_IN = 32 * KT // 2 + 16

        @block.sync
        def _(sp):
            for k in range(KT):
                if k == 2:
                    sp.dma_start(cw[:, :, :], conv_w).then_inc(small_in, 16)
                    sp.dma_start(cb[:, :], conv_b).then_inc(small_in, 16)
                    sp.dma_start(nw[:, :], norm_w).then_inc(small_in, 16)
                    sp.dma_start(dtb[:, :], dt_bias.partition_broadcast(P)).then_inc(small_in, 16)
                    sp.dma_start(aneg[:, :], a_log.partition_broadcast(P)).then_inc(small_in, 16)
                    for half in range(2):
                        sp.dma_start(dcol[half * HP:(half + 1) * HP, :],
                                     d_skip[half].partition_broadcast(HP)
                                     ).then_inc(small_in, 16)
                if k >= 2:
                    sp.wait_ge(w_used, k - 1)
                for n in range(2):
                    sp.dma_start(staging[k % 2][n], winT[k * P:(k + 1) * P, n * half_w:(n + 1) * half_w]
                                 ).then_inc(w_in[k % 2], 16)

            def load_transposed(b, first):
                if not first:
                    sp.wait_ge(xt_split, at(b, KT, 0))
                    sp.wait_ge(dt_turned, at(b, 1, 0))
                sp.dma_start(xt_in[:, :, :], one(xT, b).rearrange("a (k p) n -> p (a k) n", p=P)
                             ).then_inc(xt_landed, 16)

            def load_residual(b, first):
                if not first:
                    sp.wait_ge(x1_out, at(b, 16 * TT, 0))
                sp.dma_start(x_tok[:, :, :], one(x, b).rearrange("a (t p) n -> p (a t) n", p=P)).then_inc(x_in, 16)

            def head(b):
                load_transposed(b, True)
                load_residual(b, True)
                sp.wait_ge(w_used, KT - 1)
                sp.dma_start(wout[:, :, :], woutT.rearrange("(c p) n -> p c n", p=P)).then_inc(w_in[0], 16)

            def body(b, first, more):
                if more:
                    load_transposed(b + 1, False)
                for t in range(TT):
                    sp.wait_ge(x1_ready, at(b, TT, t + 1))
                    sp.dma_start(one(x1, b)[:, t * P:(t + 1) * P, :].rearrange("a p n -> p (a n)"),
                                 x_tok[:, t, :]).then_inc(x1_out, 16)
                if more:
                    load_residual(b + 1, False)

            over_overlapped(sp, n_seq, head, body)
            sp.wait_ge(x1_out, 16 * TT * n_seq)

        @block.gpsimd
        def _(pool):
            pool.memset(onesf[:, :], 1.0).then_inc(const, 1)
            pool.memset(neg_half[:, :], -0.5).then_inc(const, 1)
            pool.wait_ge(const, 2)
            pool.affine_select(out=tri[:, :], in_=onesf[:, :], compare_op=ALU.is_ge, fill=0.0,
                               base=0, pattern=[[1, P]], channel_multiplier=-1).then_inc(const, 1)
            pool.affine_select(out=strict[:, :], in_=onesf[:, :], compare_op=ALU.is_ge, fill=0.0,
                               base=-1, pattern=[[-1, P]], channel_multiplier=1).then_inc(const, 1)
            pool.affine_select(out=ident[:, :], in_=onesf[:, :], compare_op=ALU.is_equal, fill=0.0,
                               base=0, pattern=[[-1, P]], channel_multiplier=1).then_inc(const, 1)
            pool.wait_ge(const, 5)
            pool.wait_ge(small_in, 16 * N_SMALL)
            pool.wait_ge(w_in[0], W_OUT_IN)
            pool.tensor_tensor(wout[:, :, :], wout[:, :, :], nw[:, :].unsqueeze(2).to_broadcast([P, XT_TILES, DM]),
                               ALU.mult).then_inc(const, 1)

            def masked_decays(b, first, gr, c):
                if c >= 2:
                    if c == 2:
                        pool.wait_ge(seg_done, at(b, NG * CH, gr * CH + 1))
                    else:
                        pool.wait_ge(ebc_done, at(b, NG * (CH - 1), gr * (CH - 1) + 1))
                elif gr or not first:
                    pool.wait_ge(ebc_done, at(b, NG * (CH - 1), (gr - 1) * (CH - 1) + 2 + c))
                heads = slice(gr * HG, (gr + 1) * HG)
                shape = [P, HG, P]
                m = tri[:, :].unsqueeze(1).to_broadcast(shape)
                pool.tensor_tensor(rhs_hi[:, c % 2], a_hi[:, c, heads].unsqueeze(2).to_broadcast(shape), m, ALU.mult)
                pool.tensor_tensor(rhs_lo[:, c % 2], a_lo[:, c, heads].unsqueeze(2).to_broadcast(shape), m,
                                   ALU.mult).then_inc(rhs_ready, 1)

            def weighted_x(b, first, gr):
                pool.wait_ge(xk_ready, at(b, 2 * NG, 2 * gr + 2))
                if gr == 0:
                    pool.wait_ge(wdt_ready, at(b, 1, 1))
                if gr or not first:
                    pool.wait_ge(st_done, at(b, NG * (CH - 1), gr * (CH - 1)))
                w = wdt[:, 0:CH - 1, gr * HG:(gr + 1) * HG].unsqueeze(3).to_broadcast([P, CH - 1, HG, HP])
                pool.tensor_tensor(xw[:, :, :, :], xk[:, 0:CH - 1], w, ALU.mult).then_inc(xw_ready, 1)

            def sum_squares(b, first, gr):
                for j in range(2):
                    n = 2 * gr + j
                    if n == 0:
                        squares = value(pool, at(b, XT_TILES, 1))
                        met(pool, const, 5)
                        pool.wait_ge(sq_ready, squares)
                        if not first:
                            pool.wait_ge(rms_done, at(b, 1, 0))
                        pool.tensor_copy(ssum[:, :], sq[:, 0, :]).then_inc(sq_used, 1)
                    else:
                        pool.wait_ge(sq_ready, at(b, XT_TILES, n + 1))
                        pool.wait_ge(sq_used, at(b, XT_TILES, n))
                        pool.tensor_tensor(ssum[:, :], ssum[:, :], sq[:, j, :], ALU.add).then_inc(sq_used, 1)

            def head(b, first=True):
                pool.wait_ge(a_ready, at(b, 1, 1))
                for c in range(2):
                    masked_decays(b, first, 0, c)

            def body(b, first, more):
                for gr in range(NG):
                    for c in range(0 if gr else 2, CH):
                        masked_decays(b, first, gr, c)
                    weighted_x(b, first, gr)
                    if gr:
                        sum_squares(b, first, gr - 1)
                sum_squares(b, first, NG - 1)
                pool.wait_ge(rms_in, at(b, 1, 1))
                pool.tensor_tensor(rms[:, 1], rms[:, 0], neg_half[:, :], ALU.pow).then_inc(rms_ready, 1)
                if more:
                    head(b + 1, False)
                for t in range(TT):
                    pool.wait_ge(var_ready, at(b, TT, t + 1))
                    pool.tensor_tensor(rstd[:, 1, t:t + 1], rstd[:, 0, t:t + 1], neg_half[:, 0:1],
                                       ALU.pow).then_inc(rstd_ready, 1)

            over_overlapped(pool, n_seq, head, body)

        @block.scalar
        def _(act):
            act.wait_ge(small_in, 16 * N_SMALL)
            act.activation(aneg[:, :], aneg[:, :], ACT.Exp).then_inc(setup_a, 1)

            def conv_tap0(b, n, tile, slot):
                act.wait_ge(tile_done, at(b, 18, tile + 1))
                act.activation(acc[:, slot, :], proj[tile % 2][:, :], ACT.Identity, bias=cb[:, n:n + 1],
                               scale=cw[:, n, 3:4]).then_inc(taps0, 1)

            def x_high(b, first):
                if not first:
                    act.wait_ge(tile_done, at(b, 18, 0))
                act.wait_ge(xt_landed, at(b, 16, 16))
                for k in range(KT):
                    act.activation(xt_hi[:, k, :], xt_in[:, k, :], ACT.Copy).then_inc(xt_hi_s, 1)

            def x_tap0(b, first, n):
                if n == 0:
                    act.wait_ge(bc_ready, at(b, 1, 1))
                elif n == 1:
                    if not first:
                        act.wait_ge(xc_ready, at(b, XT_TILES, 0))
                else:
                    act.wait_ge(xc_ready, at(b, XT_TILES, n - 1))
                conv_tap0(b, n, 2 + 4 * (n // 2) + n % 2, n % 2)

            def silus(b, first, gr):
                for j in range(2):
                    n = 2 * gr + j
                    act.wait_ge(conv_read, at(b, 9, n + 2))
                    if gr >= 2 or not first:
                        act.wait_ge(g_ready, at(b, XT_TILES, 2 * (gr - 2) + 2))
                    act.activation(xc[:, gr % 2, j, :], acc[:, j, :], ACT.Silu).then_inc(xc_ready, 1)
                for j in range(2):
                    act.wait_ge(tile_done, at(b, 18, 2 + 4 * gr + 2 + j + 1))
                    act.activation(zs[:, gr % 2, j, :], proj[j][:, :], ACT.Silu).then_inc(z_ready, 1)

            def raw_steps(b, first):
                act.wait_ge(tile_done, at(b, 18, 1))
                if not first:
                    act.wait_ge(dt_turned, at(b, 1, 0))
                act.activation(dt_ch[0:NH, :], proj[0][0:NH, :], ACT.Copy).then_inc(dt_read, 1)

            def bc_tap0(b, first):
                if not first:
                    act.wait_ge(xc_ready, at(b, XT_TILES, 0))
                conv_tap0(b, 8, 1, 0)

            def decays(b, first, gr, between):
                for h in range(2):
                    act.wait_ge(xk_done, at(b, 2 * NG, 2 * gr + h + 1))
                    if h == 0 and (gr or not first):
                        act.wait_ge(xdt_ready, at(b, 2 * NG, 2 * gr))
                        act.wait_ge(xw_ready, at(b, NG, gr))
                    act.activation(xk[:, 2 * h:2 * h + 2].rearrange("p c h d -> p (c h d)"),
                                   turn[:, :], ACT.Copy).then_inc(xk_ready, 1)
                for c in range(CH):
                    act.wait_ge(seg_done, at(b, NG * CH, gr * CH + c + 1))
                    if c == 0 and (gr or not first):
                        act.wait_ge(y_done, at(b, XT_TILES, 2 * gr))
                    act.activation(dec[:, c], seg[c % 2][:, :], ACT.Exp).then_inc(dec_ready, 1)
                    if c:
                        act.wait_ge(ebc_done, at(b, NG * (CH - 1), gr * (CH - 1) + c))
                        act.activation(ce[:, c - 1], misc[0:NS, :], ACT.Exp).then_inc(e_ready, 1)
                    if c in (1, 2) and between:
                        between[c - 1]()

            def squares(b, first, gr):
                for j in range(2):
                    n = 2 * gr + j
                    act.wait_ge(g_ready, at(b, XT_TILES, n + 1))
                    if n >= 2 or not first:
                        act.wait_ge(sq_used, at(b, XT_TILES, n - 1))
                    act.activation(sq[:, j, :], g[:, n, :], ACT.Square).then_inc(sq_ready, 1)

            def head(b, first=True):
                if first:
                    x_high(b, True)
                    raw_steps(b, True)
                    bc_tap0(b, True)
                act.wait_ge(conv_read, at(b, 9, 1))
                if not first:
                    act.wait_ge(bg_done, at(b, 1, 0))
                    act.wait_ge(ce_ready, at(b, NG * (CH - 1), 0))
                act.activation(bt[:, :], acc[0:NS, 0, :], ACT.Silu)
                act.activation(ct[:, :], acc[NS:P, 0, :], ACT.Silu).then_inc(bc_ready, 1)
                for n in range(2):
                    x_tap0(b, first, n)
                silus(b, first, 0)
                act.wait_ge(dtv, at(b, 14, 3))
                act.activation(sm[:, 2], sm[:, 1], ACT.Exp).then_inc(dta, 1)
                act.wait_ge(dtv, at(b, 14, 4))
                act.activation(sm[:, 4], sm[:, 3], ACT.Ln).then_inc(dta, 1)
                act.wait_ge(sums_done, at(b, 1, 1))
                if not first:
                    act.wait_ge(st_ready, at(b, NG * (CH - 1), 0))
                act.activation(wd[:, :, :, :].rearrange("p a c h -> p (a c h)"), turn[:, 0:2 * CH * NH],
                               ACT.Exp).then_inc(wd_ready, 1)

            def body(b, first, more):
                for gr in range(NG):
                    if gr + 1 < NG:
                        between = [lambda n=2 * gr + 2 + j: x_tap0(b, first, n) for j in range(2)]
                    else:
                        between = more and [lambda: x_high(b + 1, False), lambda: None]
                    decays(b, first, gr, between)
                    if gr + 1 == NG and more:
                        raw_steps(b + 1, False)
                        bc_tap0(b + 1, False)
                    if gr + 1 < NG:
                        silus(b, first, gr + 1)
                    if gr == 0:
                        act.wait_ge(x_in, at(b, 16, 16))
                        act.activation(x_tok[:, :, :], x_tok[:, :, :], ACT.Copy, scale=2.0).then_inc(x_dbl, 1)
                    squares(b, first, gr)
                if more:
                    head(b + 1, False)

            over_overlapped(act, n_seq, head, body)

        @block.vector
        def _(dve):
            chain = Chain(dve, setup, 0)
            chain.start(0)
            dve.wait_ge(const, 5)
            dve.tensor_copy(strict_r[:, :], strict[:, :])
            dve.tensor_copy(ones_r[:, :], onesf[:, :])
            for k in range(KT):
                dve.wait_ge(w_in[k % 2], 32 * (k // 2 + 1))
                for n in range(2):
                    ins = dve.tensor_copy(win_hi[:, k, n * half_w:(n + 1) * half_w], staging[k % 2][n])
                chain.link(ins)
                for n in range(2):
                    cols = slice(n * half_w, (n + 1) * half_w)
                    ins = dve.tensor_tensor(win_lo[:, k, cols], staging[k % 2][n], win_hi[:, k, cols], ALU.subtract)
                ins.then_inc(w_used, 1)
            dve.wait_ge(setup_a, 1)
            chain.link(dve.tensor_scalar(aneg[:, :], aneg[:, :], -1.0, -1e30, ALU.mult, ALU.max))

            dt_chain = Chain(dve, dtv, 14)
            conv_chain = Chain(dve, conv_v, 18)
            st_chain = Chain(dve, st_v, 8)
            ln_chain = Chain(dve, ln_v, 2 * TT)

            def conv(b, n, tile, slot, done):
                dve.wait_ge(taps0, at(b, 9, done))
                conv_chain.start(b, 2 * (done - 1))
                for i in range(3):
                    s = i + 1
                    ins = dve.scalar_tensor_tensor(out=acc[:, slot, s:SEQ], in0=proj[tile % 2][:, 0:SEQ - s],
                                                   scalar=cw[:, n, 2 - i:3 - i], in1=acc[:, slot, s:SEQ],
                                                   op0=ALU.mult, op1=ALU.add)
                    if i < 2:
                        conv_chain.link(ins)
                ins.then_inc(conv_read, 1)

            def split_x(b):
                for k in range(KT):
                    dve.wait_ge(xt_hi_s, at(b, KT, k + 1))
                    dve.tensor_tensor(xt_lo[:, k, :], xt_in[:, k, :], xt_hi[:, k, :],
                                      ALU.subtract).then_inc(xt_split, 1)

            def step_sizes(b, first):
                dt_chain.start(b)
                sc = [sm[:, i] for i in range(8)]
                dve.wait_ge(dt_turned, at(b, 1, 1))
                if not first:
                    dve.wait_ge(rhs_ready, at(b, NG * CH, 0))
                    dve.wait_ge(xw_ready, at(b, NG, 0))
                dt_chain.link(dve.tensor_tensor(sc[0].rearrange("p (c h) -> p c h", h=NH),
                                                turn[:, 0:CH * NH].rearrange("p (c h) -> p c h", h=NH),
                                                dtb[:, :].unsqueeze(1).to_broadcast([P, CH, NH]), ALU.add))
                dt_chain.link(dve.tensor_scalar(sc[5], sc[0], -1.0, None, ALU.mult))
                dt_chain.link(dve.tensor_tensor(sc[1], sc[0], sc[5], ALU.min))
                dve.wait_ge(dta, at(b, 2, 1))
                dt_chain.link(dve.tensor_scalar(sc[3], sc[2], 1.0, None, ALU.add))
                dt_chain.link(dve.tensor_scalar(sc[7], sc[3], 1.0, None, ALU.is_equal))
                dt_chain.link(dve.scalar_tensor_tensor(out=sc[5], in0=sc[3], scalar=-1.0, in1=sc[7],
                                                       op0=ALU.add, op1=ALU.add))
                dt_chain.link(dve.reciprocal(sc[6], sc[5]))
                dve.wait_ge(dta, at(b, 2, 2))
                dt_chain.link(dve.tensor_tensor(sc[4], sc[4], sc[6], ALU.mult))
                dt_chain.link(dve.tensor_tensor(sc[5], sc[4], sc[7], ALU.add))
                dt_chain.link(dve.tensor_tensor(sc[6], sc[5], sc[2], ALU.mult))
                flat = dt[:, :, :].rearrange("p c h -> p (c h)")
                dt_chain.link(dve.scalar_tensor_tensor(out=flat, in0=sc[0], scalar=0.0, in1=sc[6],
                                                       op0=ALU.max, op1=ALU.add))
                dt_chain.link(dve.tensor_tensor(a[:, :, :], dt[:, :, :],
                                                aneg[:, :].unsqueeze(1).to_broadcast([P, CH, NH]), ALU.mult))
                dt_chain.link(dve.tensor_copy(a_hr[:, :, :], a[:, :, :]))
                dt_chain.link(dve.tensor_copy(a_hi[:, :, :], a_hr[:, :, :].bitcast(F32)))
                dve.tensor_tensor(a_lo[:, :, :], a[:, :, :], a_hi[:, :, :], ALU.subtract).then_inc(a_ready, 1)
                dt_chain.end()

            def group_factors(b, first, gr, between):
                heads = slice(gr * HG, (gr + 1) * HG)
                for h in range(2):
                    dve.wait_ge(xk_ready, at(b, 2 * NG, 2 * gr + h + 1))
                    if h == 0 and (gr or not first):
                        dve.wait_ge(y_done, at(b, XT_TILES, 2 * gr))
                    c = slice(2 * h, 2 * h + 2)
                    dve.tensor_tensor(xdt[:, c], xk[:, c], dt[:, c, heads].unsqueeze(3).to_broadcast([P, 2, HG, HP]),
                                      ALU.mult).then_inc(xdt_ready, 1)
                if gr == 0:
                    dve.wait_ge(bg_read, at(b, 1, 1))
                for c in range(CH):
                    dve.wait_ge(dec_ready, at(b, NG * CH, gr * CH + c + 1))
                    dve.tensor_tensor(dec[:, c], dec[:, c], gm[:, c, :].unsqueeze(1).to_broadcast([P, HG, P]),
                                      ALU.mult).then_inc(m_ready, 1)
                    if c:
                        dve.wait_ge(e_ready, at(b, NG * (CH - 1), gr * (CH - 1) + c))
                        dve.tensor_tensor(ce[:, c - 1], ce[:, c - 1],
                                          ct[:, c * P:(c + 1) * P].unsqueeze(1).to_broadcast([NS, HG, P]),
                                          ALU.mult).then_inc(ce_ready, 1)
                    if c in (1, 2) and between:
                        between[c - 1]()

            def states(b, first, gr):
                for c in range(CH - 1):
                    src = (turn[0:NS, c * 256:(c + 1) * 256] if c < 2 else misc[0:NS, 0:256])
                    src = src.rearrange("p (h d) -> p h d", h=HG)
                    dve.wait_ge(st_done, at(b, NG * (CH - 1), gr * (CH - 1) + max(c + 1, 2)))
                    if c == 0:
                        dve.tensor_copy(st[:, 0], src).then_inc(st_ready, 1)
                    else:
                        dve.wait_ge(st_ready, at(b, NG * (CH - 1), gr * (CH - 1) + c))
                        whole = wd[0:NS, 1, c, gr * HG:(gr + 1) * HG].unsqueeze(2).to_broadcast([NS, HG, HP])
                        st_chain.link(dve.tensor_tensor(st[:, c], st[:, c - 1], whole, ALU.mult))
                        dve.tensor_tensor(st[:, c], st[:, c], src, ALU.add).then_inc(st_ready, 1)

            def gate(b, first, gr):
                for j in range(2):
                    n = 2 * gr + j
                    dve.wait_ge(y_done, at(b, XT_TILES, n + 1))
                    if n == 0 and not first:
                        dve.wait_ge(out_done, at(b, TT, 0))
                    dve.scalar_tensor_tensor(out=g[:, n, :], in0=xc[:, gr % 2, j, :], scalar=dcol[:, n:n + 1],
                                             in1=yp[j][:, :], op0=ALU.mult, op1=ALU.add).then_inc(y_read, 1)
                for j in range(2):
                    n = 2 * gr + j
                    dve.wait_ge(z_ready, at(b, XT_TILES, n + 1))
                    dve.wait_ge(y_read, at(b, XT_TILES, n + 1))
                    dve.tensor_tensor(g[:, n, :], g[:, n, :], zs[:, gr % 2, j, :], ALU.mult).then_inc(g_ready, 1)

            def norm_scale(b):
                dve.wait_ge(rms_done, at(b, 1, 1))
                dve.tensor_scalar(rms[:, 0], misc[:, 0:TT], 1.0 / DI, LN_EPS, ALU.mult, ALU.add).then_inc(rms_in, 1)

            def norm(b, t):
                if t == 0:
                    ln_chain.start(b)
                    dve.wait_ge(x_dbl, at(b, 1, 1))
                    dve.wait_ge(rms_ready, at(b, 1, 1))
                dve.wait_ge(out_done, at(b, TT, t + 1))
                dve.scalar_tensor_tensor(out=x_tok[:, t, :], in0=seg[t % 2][:, :], scalar=rms[:, 1, t:t + 1],
                                         in1=x_tok[:, t, :], op0=ALU.mult, op1=ALU.add).then_inc(out_read, 1)
                dve.wait_ge(out_read, at(b, TT, t + 1))
                ln_chain.link(dve.bn_stats(stats[:, t, :], x_tok[:, t, :]), (const, 5))
                ln_chain.link(dve.bn_aggr(mv[:, t, :], stats[:, t, :]))
                dve.tensor_scalar(rstd[:, 0, t:t + 1], mv[:, t, 1:2], LN_EPS, None, ALU.add).then_inc(var_ready, 1)

            def apply_norm(b):
                for t in range(TT):
                    dve.wait_ge(rstd_ready, at(b, TT, t + 1))
                    dve.tensor_scalar(x_tok[:, t, :], x_tok[:, t, :], mv[:, t, 0:1], rstd[:, 1, t:t + 1],
                                      ALU.subtract, ALU.mult).then_inc(x1_ready, 1)

            def head_convs(b, part):
                if part == 0:
                    conv(b, 8, 1, 0, 1)
                else:
                    conv(b, 0, 2, 0, 2)
                    conv(b, 1, 3, 1, 3)

            def head_products(b):
                dve.wait_ge(bg_done, at(b, 1, 1))
                dve.tensor_tensor(gm[:, :, :], misc[:, :].rearrange("p (c t) -> p c t", c=CH),
                                  tri[:, :].unsqueeze(1).to_broadcast([P, CH, P]), ALU.mult)
                dve.tensor_copy(b_tok[:, :, :].rearrange("p c n -> p (c n)"),
                                yp[0][:, 0:CH * NS]).then_inc(bg_read, 1)

            def head_weights(b):
                dve.wait_ge(wd_ready, at(b, 1, 1))
                dve.tensor_tensor(wdt[:, :, :], wd[:, 0], dt[:, :, :], ALU.mult).then_inc(wdt_ready, 1)

            def head(b):
                split_x(b)
                head_convs(b, 0)
                head_convs(b, 1)
                step_sizes(b, True)
                head_products(b)
                head_weights(b)

            def body(b, first, more):
                st_chain.start(b)
                for gr in range(NG):
                    if gr + 1 < NG:
                        between = [lambda j=j: conv(b, 2 * gr + 2 + j, 2 + 4 * (gr + 1) + j, j, 2 * gr + 4 + j)
                                   for j in range(2)]
                    else:
                        between = more and [lambda: split_x(b + 1), lambda: None]
                    group_factors(b, first, gr, between)
                    states(b, first, gr)
                    if gr + 1 == NG and more:
                        head_convs(b + 1, 0)
                    gate(b, first, gr)
                st_chain.end()
                if more:
                    head_convs(b + 1, 1)
                norm_scale(b)
                norm(b, 0)
                if more:
                    step_sizes(b + 1, False)
                    head_products(b + 1)
                norm(b, 1)
                norm(b, 2)
                if more:
                    head_weights(b + 1)
                norm(b, 3)
                ln_chain.end()
                apply_norm(b)

            over_overlapped(dve, n_seq, head, body)

        @block.tensor
        def _(pe):
            pe.wait_ge(w_used, KT)
            pe.wait_ge(setup, KT + 1)

            def in_proj(b, first, n, col):
                bank = proj[n % 2]
                if n < 2:
                    if not first:
                        pe.wait_ge(z_ready, at(b, XT_TILES, n - 1))
                elif n == 2:
                    pe.wait_ge(dt_read, at(b, 1, 1))
                elif n == 3:
                    pe.wait_ge(conv_read, at(b, 9, 1))
                elif (n - 2) % 4 < 2:
                    pe.wait_ge(z_ready, at(b, XT_TILES, 2 * ((n - 2) // 4 - 1) + (n - 2) % 4 + 1))
                else:
                    pe.wait_ge(conv_read, at(b, 9, 2 * ((n - 2) // 4) + (n - 2) % 4 - 2 + 2))
                for k in range(KT):
                    if n == 0:
                        pe.wait_ge(xt_split, at(b, KT, k + 1))
                    wh, wl = win_hi[:, k, col:col + P], win_lo[:, k, col:col + P]
                    pe.matmul(bank[:, :], wh, xt_hi[:, k, :], start=(k == 0), stop=False)
                    pe.matmul(bank[:, :], wh, xt_lo[:, k, :], start=False, stop=False)
                    ins = pe.matmul(bank[:, :], wl, xt_hi[:, k, :], start=False, stop=(k == KT - 1))
                ins.then_inc(tile_done, 1)

            def decays(b, first, gr, between):
                for h in range(2):
                    if h == 0:
                        pe.wait_ge(xc_ready, at(b, XT_TILES, 2 * gr + 2))
                        if gr == 0:
                            pe.wait_ge(wd_ready, at(b, 1, 1))
                        else:
                            pe.wait_ge(st_ready, at(b, NG * (CH - 1), gr * (CH - 1)))
                    else:
                        pe.wait_ge(xk_ready, at(b, 2 * NG, 2 * gr + 1))
                    for c in range(2):
                        for j in range(2):
                            t0 = (2 * h + c) * P
                            ins = pe.transpose(turn[:, c * 256 + j * P:c * 256 + (j + 1) * P],
                                               xc[:, gr % 2, j, t0:t0 + P], ident[:, :])
                    ins.then_inc(xk_done, 1)
                    if h == 0 and between:
                        between[0]()
                for c in range(CH):
                    pe.wait_ge(rhs_ready, at(b, NG * CH, gr * CH + c + 1))
                    if gr or c >= 2:
                        pe.wait_ge(dec_ready, at(b, NG * CH, gr * CH + c - 1))
                    elif not first:
                        pe.wait_ge(out_read, at(b, TT, c - 1))
                    hi = rhs_hi[:, c % 2].rearrange("p h t -> p (h t)")
                    lo = rhs_lo[:, c % 2].rearrange("p h t -> p (h t)")
                    pe.matmul(seg[c % 2][:, :], strict_r[:, :], hi, start=True, stop=False)
                    pe.matmul(seg[c % 2][:, :], strict_r[:, :], lo, start=False, stop=True).then_inc(seg_done, 1)
                    if c:
                        if c > 1:
                            pe.wait_ge(e_ready, at(b, NG * (CH - 1), gr * (CH - 1) + c - 1))
                        elif gr == 0:
                            pe.wait_ge(bg_read, at(b, 1, 1))
                        pe.matmul(misc[:, :], ones_r[:, :], hi, start=True, stop=False)
                        pe.matmul(misc[:, :], ones_r[:, :], lo, start=False, stop=True).then_inc(ebc_done, 1)
                    if c == 1 and between:
                        between[1]()

            def added_states(b, first, gr):
                pe.wait_ge(xw_ready, at(b, NG, gr + 1))
                pe.wait_ge(e_ready, at(b, NG * (CH - 1), (gr + 1) * (CH - 1)))
                for c in range(CH - 1):
                    dst = turn[0:NS, c * 256:(c + 1) * 256] if c < 2 else misc[0:NS, 0:256]
                    pe.matmul(dst, b_tok[:, c, :], xw[:, c].rearrange("p h d -> p (h d)"),
                              start=True, stop=True).then_inc(st_done, 1)

            def local_outputs(b, first, gr):
                if gr or not first:
                    pe.wait_ge(y_read, at(b, XT_TILES, 2 * gr))
                if gr == 0:
                    pe.wait_ge(bg_read, at(b, 1, 1))
                pe.wait_ge(xdt_ready, at(b, 2 * NG, 2 * gr + 2))
                for c in range(CH):
                    pe.wait_ge(m_ready, at(b, NG * CH, gr * CH + c + 1))
                    for j in range(2):
                        for h in range(2):
                            pe.matmul(yp[j][h * HP:(h + 1) * HP, c * P:(c + 1) * P], xdt[:, c, 2 * j + h, :],
                                      dec[:, c, 2 * j + h, :], start=(c == 0), stop=False, skip_group_check=True)

            def carried_outputs(b, gr):
                for j in range(2):
                    for c in range(1, CH):
                        if j == 0:
                            met(pe, w_used, KT)
                            pe.wait_ge(st_ready, at(b, NG * (CH - 1), gr * (CH - 1) + c))
                            pe.wait_ge(ce_ready, at(b, NG * (CH - 1), gr * (CH - 1) + c))
                        for h in range(2):
                            ins = pe.matmul(yp[j][h * HP:(h + 1) * HP, c * P:(c + 1) * P], st[:, c - 1, 2 * j + h, :],
                                            ce[:, c - 1, 2 * j + h, :], start=False, stop=(c == CH - 1),
                                            skip_group_check=True)
                    ins.then_inc(y_done, 1)

            def turn_steps(b, first):
                turn_free = value(pe, at(b, NG * (CH - 1), 0))
                raw_dt = value(pe, at(b, 1, 1))
                met(pe, w_used, KT)
                pe.wait_ge(dt_read, raw_dt)
                if not first:
                    pe.wait_ge(st_ready, turn_free)
                for c in range(CH):
                    ins = pe.transpose(turn[:, c * NH:(c + 1) * NH], dt_ch[0:NH, c * P:(c + 1) * P],
                                       ident[0:NH, 0:NH])
                ins.then_inc(dt_turned, 1)

            def products(b, first):
                pe.wait_ge(bc_ready, at(b, 1, 1))
                if not first:
                    pe.wait_ge(rms_in, at(b, 1, 0))
                    pe.wait_ge(y_read, at(b, XT_TILES, 0))
                for c in range(CH):
                    pe.matmul(misc[:, c * P:(c + 1) * P], bt[:, c * P:(c + 1) * P], ct[:, c * P:(c + 1) * P],
                              start=True, stop=True)
                for c in range(CH):
                    ins = pe.transpose(yp[0][:, c * NS:(c + 1) * NS], bt[:, c * P:(c + 1) * P], ident[0:NS, 0:NS])
                ins.then_inc(bg_done, 1)

            def decay_sums(b):
                pe.wait_ge(a_ready, at(b, 1, 1))
                flat = a[:, :, :].rearrange("p c h -> p (c h)")
                pe.matmul(turn[:, 0:CH * NH], strict[:, :], flat, start=True, stop=True)
                pe.matmul(turn[:, CH * NH:2 * CH * NH], onesf[:, :], flat, start=True, stop=True).then_inc(sums_done, 1)

            def mean_square(b):
                pe.wait_ge(sq_used, at(b, XT_TILES, XT_TILES))
                pe.wait_ge(st_ready, at(b, NG * (CH - 1), NG * (CH - 1)))
                for t in range(TT):
                    ins = pe.matmul(misc[:, t:t + 1], ssum[:, t * P:(t + 1) * P], onesf[:, 0:1], start=True, stop=True)
                ins.then_inc(rms_done, 1)

            def out_proj(b, t):
                if t == 0:
                    pe.wait_ge(const, 6)
                    pe.wait_ge(g_ready, at(b, XT_TILES, XT_TILES))
                if t < 2:
                    pe.wait_ge(dec_ready, at(b, NG * CH, NG * CH - 1 + t))
                else:
                    pe.wait_ge(out_read, at(b, TT, t - 1))
                for k in range(XT_TILES):
                    ins = pe.matmul(seg[t % 2][:, :], g[:, k, t * P:(t + 1) * P], wout[:, k, :],
                                    start=(k == 0), stop=(k == XT_TILES - 1))
                ins.then_inc(out_done, 1)

            def x_tile(b, first, n):
                in_proj(b, first, 2 + 4 * (n // 2) + n % 2, COL_X + n * P)

            def z_tile(b, first, gr, j):
                in_proj(b, first, 4 + 4 * gr + j, COL_Z + (2 * gr + j) * P)

            def head(b):
                in_proj(b, True, 0, 0)
                in_proj(b, True, 1, COL_BC)
                turn_steps(b, True)
                for n in range(2):
                    x_tile(b, True, n)
                for j in range(2):
                    z_tile(b, True, 0, j)
                products(b, True)
                decay_sums(b)

            def body(b, first, more):
                for gr in range(NG):
                    if gr + 1 < NG:
                        between = [lambda n=2 * gr + 2 + j: x_tile(b, first, n) for j in range(2)]
                    else:
                        between = None
                    decays(b, first, gr, between)
                    if gr + 1 < NG:
                        z_tile(b, first, gr + 1, 0)
                    elif more:
                        in_proj(b + 1, False, 0, 0)
                    added_states(b, first, gr)
                    local_outputs(b, first, gr)
                    if gr + 1 < NG:
                        z_tile(b, first, gr + 1, 1)
                    elif more:
                        in_proj(b + 1, False, 1, COL_BC)
                    carried_outputs(b, gr)
                if more:
                    for n in range(2):
                        x_tile(b + 1, False, n)
                    turn_steps(b + 1, False)
                out_proj(b, 0)
                mean_square(b)
                if more:
                    for j in range(2):
                        z_tile(b + 1, False, 0, j)
                out_proj(b, 1)
                if more:
                    products(b + 1, False)
                out_proj(b, 2)
                if more:
                    decay_sums(b + 1)
                out_proj(b, 3)

            over_overlapped(pe, n_seq, head, body)


AH = 16
AD = DM // AH
AG = P // AD
STACK = 3 * AD
SOFT_SCALE = AD ** -0.5


UNITS = KT * TT
LEAD = 5
STACKS = 3


class Turn:

    def __init__(self, b, phase, d):
        self.b, self.phase, self.d = b, phase, d

    def before(self):
        return Turn(self.b, self.phase, self.d - 1)

    def slot(self, gr):
        return (self.phase + self.d + gr) % STACKS

    def at(self, per, k):
        return at(self.b, per, k + self.d * per)

    def number(self):
        return self.b + self.d if self.d else self.b

    def first(self):
        return isinstance(self.b, int) and self.b + self.d == 0


def attention_order():
    steps = []

    def now(*names):
        steps.extend((name, 0) for name in names)

    def ahead(*names):
        steps.extend((name, 1) for name in names)

    def p1(n):
        return [("p1", n // TT, n % TT, half) for half in range(2)]

    def av(n):
        return [("av", n // TT, n % TT, half) for half in range(2)]

    def of(n, names):
        return (ahead if n >= UNITS else now)(*names(n % UNITS))

    def maxima(n, half):
        of(n + LEAD, lambda m: p1(m)[half:half + 1])

    def projection(n):
        if n in (1, 5, 9, 13):
            of(n + 3 * TT - 1, lambda m: [("qk", m // TT, 1, 0)])
        if n in (2, 6, 10, 14):
            of(n + 3 * TT - 2, lambda m: [("qk", m // TT, 0, 0)])

    for n in range(UNITS):
        gr, u = divmod(n, TT)
        products = av(n - 1) if n else [None, None]
        projects = n % TT in (1, 2)
        if u == TT - 1:
            of(n + TT, lambda m: [("neg", m // TT, 0, 0)])
            now(("st", gr, u, 0))
        maxima(n, 0)
        if n >= TT:
            now(*[("norm", gr - 1, c, 0) for c in ((), (0, 1), (2,), (3,))[u]])
        if projects:
            projection(n)
        if u < TT - 1:
            now(("st", gr, u, 0))
        if n:
            now(products[0])
        maxima(n, 1)
        if n:
            now(products[1])
        if u == 0 and n:
            now(("o", gr - 1, 0, 0))
            of(n + 2 * TT, lambda m: [("stack", m // TT, 0, 0)])
        if n == 0:
            now(("bias", 0, 0, 0))
        if n in (1, 2):
            ahead(*[("c", 2 * (n - 1) + k, 0, 0) for k in range(2)])
        if n in (3, 4):
            ahead(*[("xt", 2 * (n - 3) + k, 0, 0) for k in range(2)])
        if n in (2, 3):
            ahead(*[("x", 2 * (n - 2) + k, 0, 0) for k in range(2)])
    now(*av(UNITS - 1), ("o", KT - 1, 0, 0))
    ahead(("stack", 2, 0, 0))
    for c in range(TT):
        now(("norm", KT - 1, c, 0))
        if c != 1:
            ahead(("v", c // 2 + c // 3, 0, 0))
    ahead(("v", 3, 0, 0))
    now(*[("out", t, 0, 0) for t in range(TT)], ("end", 0, 0, 0))
    ahead(("load", 0, 0, 0))
    start = [(step, 0) for step, d in steps if d]
    last = [(step, 0) for step, d in steps if not d]
    return start, steps, last


def over_attention(eng, count, take_step, steps):
    start, steady, last = steps

    def run(b, phase, part, name):
        for step, d in part:
            take_step(step, Turn(b, phase, d), name)

    run(0, 0, start, "start")
    run(0, 0, steady, "first")
    turns = (count - 2) // STACKS
    if turns:
        with eng.Fori(0, turns) as i:
            for n in range(STACKS):
                run(i * STACKS + 1 + n, (1 + n) % STACKS, steady, "steady")
    for b in range(1 + turns * STACKS, count - 1):
        run(b, b % STACKS, steady, "steady")
    run(count - 1, (count - 1) % STACKS, last, "last")


def shared_uses(part, shift=0):
    uses = []
    for (kind, i, j, h), d in part:
        if kind == "p1":
            uses += [((kind, i, j, 2 * h + n), d + shift) for n in range(2)]
        elif kind in ("xt", "qk", "v", "neg", "out"):
            uses.append(((kind, i, j, h), d + shift))
    return uses


def bank_plan(steps):
    start, steady, last = steps
    bank_of = {use: n % 2 for n, (use, d) in enumerate(shared_uses(steady))}
    assert len(bank_of) % 2 == 0
    before = {}
    for name, past, part in (("start", [], start), ("first", shared_uses(start), steady),
                             ("steady", shared_uses(steady, -1), steady), ("last", shared_uses(steady, -1), last)):
        held = {bank_of[use]: (use, d) for use, d in past}
        for use, d in shared_uses(part):
            before[name, use] = held.get(bank_of[use])
            held[bank_of[use]] = (use, d)
    return bank_of, before


def attention_stage(nc, n_seq, x1, ctxT, wT, b_col, b_row, x2):
    steps = attention_order()
    bank_of, before = bank_plan(steps)

    with ExitStack() as ctx:
        def sb(name, shape, dt=F32):
            return ctx.enter_context(nc.sbuf_tensor("a_" + name, shape, dt))

        def ps(name, shape=(P, 512)):
            return ctx.enter_context(nc.psum_tensor("a_" + name, list(shape), F32))

        def sem(name):
            return ctx.enter_context(nc.semaphore("a_" + name))

        names = ["q", "k", "v"]
        w_hi = {n: sb(f"w{n}_hi", [P, KT, DM], F32R) for n in names}
        w_lo = {n: sb(f"w{n}_lo", [P, KT, DM], F32R) for n in names}
        w_o = sb("wo", [P, KT, DM])
        bcol = sb("bcol", [P, 2, KT])
        brow = sb("brow", [P, 2, DM])
        ident = sb("ident", [P, P])
        onesf = sb("onesf", [P, P])
        neg_half = sb("neg_half", [P, 1])
        x_tok = sb("x_tok", [P, TT, DM])
        xt_hi = sb("xt_hi", [P, KT, SEQ], F32R)
        xt_lo = sb("xt_lo", [P, KT, SEQ], F32R)
        land = sb("land", [P, 2, SEQ])
        c_hi = sb("c_hi", [P, KT, SEQ], F32R)
        c_lo = sb("c_lo", [P, KT, SEQ], F32R)
        qk_hi = sb("qk_hi", [P, 2, 2, SEQ], F32R)
        qk_lo = sb("qk_lo", [P, 2, 2, SEQ], F32R)
        qs = sb("qs", [P, STACKS, AG, SEQ], F32R)
        ks = sb("ks", [P, STACKS, AG, SEQ], F32R)
        mx = sb("mx", [P, 2, TT, AG])
        neg_hi = sb("neg_hi", [AG, SEQ], F32R)
        neg_lo = sb("neg_lo", [AG, SEQ], F32R)
        v = sb("v", [P, TT, DM])
        probs = sb("probs", [P, 2, AG, SEQ])
        den = sb("den", [P, SEQ])
        o = sb("o", [P, KT, SEQ])
        stats = sb("stats", [P, TT, 6])
        mv = sb("mv", [P, TT, 2])
        rstd = sb("rstd", [P, 2, TT])

        sp_banks = ps("scores", (P, AG, SEQ))
        shared = [ps("shared0"), ps("shared1")]
        o_bank, den_bank = ps("o_bank"), ps("den_bank")

        def bank(use):
            return shared[bank_of[use]]

        w_in = [sem("w_in0"), sem("w_in1")]
        w_used = sem("w_used")
        w_v = sem("w_v")
        small_in = sem("small_in")
        const = sem("const")
        ones_set = sem("ones_set")
        x_in = sem("x_in")
        landed = [sem("landed0"), sem("landed1")]
        c_hi_s = sem("c_hi_s")
        c_split = sem("c_split")
        xt_done = sem("xt_done")
        xt_hi_s = sem("xt_hi_s")
        xt_split = sem("xt_split")
        xb_ready = sem("xb_ready")
        qk_done = [sem("q_done"), sem("k_done")]
        qk_hi_s = [sem("q_hi_s"), sem("k_hi_s")]
        qk_split = [sem("q_split"), sem("k_split")]
        stack_in = [[sem(f"stack{i}_{n}") for i in range(2)] for n in ("sp", "pool")]
        neg_in = [sem("neg_in0"), sem("neg_in1")]
        v_done = sem("v_done")
        v_ready = sem("v_ready")
        p1_done = sem("p1_done")
        mx_ready = sem("mx_ready")
        neg_done = sem("neg_done")
        neg_v = sem("neg_v")
        neg_ready = sem("neg_ready")
        st_done = sem("st_done")
        exp_ready = sem("exp_ready")
        av_done = sem("av_done")
        o_copied = sem("o_copied")
        o_v = sem("o_v")
        o_ready = sem("o_ready")
        out_done = sem("out_done")
        out_read = sem("out_read")
        ln_v = sem("ln_v")
        var_ready = sem("var_ready")
        rstd_ready = sem("rstd_ready")
        x2_ready = sem("x2_ready")
        x2_out = [sem(f"x2_out{t}") for t in range(TT)]

        def reader(kind, i, j, h):
            return {"xt": (xt_split, TT, i + 1),
                    "qk": (qk_split[j % 2], KT, i + 1),
                    "v": (v_ready, TT, i + 1),
                    "p1": (mx_ready, AG * UNITS, AG * (TT * i + j) + h + 1),
                    "neg": (neg_ready, KT, i + 1),
                    "out": (out_read, TT, i + 1)}[kind]

        HEAD_DMAS = 16 * 3
        SHARE = [HEAD_DMAS * (AG + 1), HEAD_DMAS * (AG - 1)]

        def stack_filled(eng, gr, t, shares=(0, 1)):
            for queue in shares:
                eng.wait_ge(stack_in[queue][gr % 2], t.at(SHARE[queue] * KT // 2, SHARE[queue] * (gr // 2 + 1)))

        def stack_free(gr, t):
            if gr >= STACKS:
                return t.at(2 * UNITS, 2 * TT * (gr - STACKS + 1))
            return None if t.first() else t.before().at(2 * UNITS, 2 * TT * (gr + KT - STACKS + 1))

        def fill_stack(eng, queue, which, gr, t, heads):
            split = value(eng, t.at(KT, gr + 1))
            free = stack_free(gr, t)
            free = None if free is None else value(eng, free)
            met(eng, const, 3)
            eng.wait_ge(qk_split[which], split)
            if free is not None:
                eng.wait_ge(st_done, free)
            parts = (qk_hi, qk_hi, qk_lo) if which else (qk_hi, qk_lo, qk_hi)
            for r, part in enumerate(parts):
                dst = (ks if which else qs)[r * AD:(r + 1) * AD, t.slot(gr)]
                for h in heads:
                    eng.dma_start(dst[:, h, :].bitcast(F32),
                                  part[h * AD:(h + 1) * AD, which, gr % 2, :].bitcast(F32)
                                  ).then_inc(stack_in[queue][gr % 2], 16)

        block = ctx.enter_context(nc.Block())
        N_SMALL = 4 * 16

        @block.sync
        def _(sp):
            sp.dma_start(probs[:, 0], wT[0].rearrange("(k p) n -> p k n", p=P)).then_inc(w_in[0], 16)
            sp.dma_start(probs[:, 1], wT[1].rearrange("(k p) n -> p k n", p=P)).then_inc(w_in[1], 16)
            sp.dma_start(bcol[:, :, :], b_col).then_inc(small_in, 16)
            for i in range(2):
                sp.dma_start(brow[:, i, :], b_row[i].partition_broadcast(P)).then_inc(small_in, 16)

            def load_rest():
                sp.wait_ge(w_used, 1)
                sp.dma_start(probs[:, 0], wT[2].rearrange("(k p) n -> p k n", p=P)).then_inc(w_in[0], 16)
                sp.dma_start(w_o[:, :, :], wT[3].rearrange("(k p) n -> p k n", p=P)).then_inc(small_in, 16)

            def load_x(t, n):
                if not t.first():
                    sp.wait_ge(x2_out[n], t.at(16, 0))
                sp.dma_start(x_tok[:, n, :], one(x1, t.number())[:, n * P:(n + 1) * P, :].rearrange("a p n -> p (a n)")
                             ).then_inc(x_in, 16)

            def step(what, t, part):
                kind, i, j, h = what
                if kind == "c":
                    if part == "start" and i == 2:
                        load_rest()
                    if i >= 2:
                        sp.wait_ge(c_split, t.at(KT, i - 1))
                    elif not t.first():
                        sp.wait_ge(xt_done, t.at(TT, i - 1))
                    sp.dma_start(land[:, i % 2, :],
                                 one(ctxT, t.number())[:, i * P:(i + 1) * P, :].rearrange("a p n -> p (a n)")
                                 ).then_inc(landed[i % 2], 16)
                elif kind == "x":
                    if i < 2:
                        sp.wait_ge(c_split, t.at(KT, KT - 1 + i))
                    else:
                        sp.wait_ge(xt_done, t.at(TT, i - 1))
                    sp.dma_start(land[:, i % 2, :],
                                 one(x1, t.number())[:, i * P:(i + 1) * P, :].rearrange("a p n -> p (a n)")
                                 ).then_inc(landed[i % 2], 16)
                elif kind == "out":
                    sp.wait_ge(x2_ready, t.at(TT, i + 1))
                    sp.dma_start(one(x2, t.number())[:, i * P:(i + 1) * P, :].rearrange("a p n -> p (a n)"),
                                 x_tok[:, i, :]).then_inc(x2_out[i], 16)
                elif kind == "load":
                    for n in range(TT):
                        load_x(t, n)
                elif kind == "stack":
                    fill_stack(sp, 0, 1, i, t, range(AG - 1, AG))
                    fill_stack(sp, 0, 0, i, t, range(AG))
                elif kind == "neg":
                    sp.wait_ge(neg_ready, t.at(KT, i + 1))
                    for r, part in enumerate((neg_hi, neg_lo)):
                        sp.dma_start(qs[STACK + r:STACK + r + 1, t.slot(i)].bitcast(F32),
                                     part[:, :].bitcast(F32)).then_inc(neg_in[i % 2], 16)

            over_attention(sp, n_seq, step, steps)
            for n in range(TT):
                sp.wait_ge(x2_out[n], 16 * n_seq)

        @block.gpsimd
        def _(pool):
            pool.memset(onesf[:, :], 1.0).then_inc(const, 1)
            pool.memset(neg_half[:, :], -0.5).then_inc(const, 1)
            pool.wait_ge(const, 2)
            pool.affine_select(out=ident[:, :], in_=onesf[:, :], compare_op=ALU.is_equal, fill=0.0,
                               base=0, pattern=[[-1, P]], channel_multiplier=1).then_inc(const, 1)
            pool.wait_ge(const, 3)
            pool.memset(ks[STACK:P, :, :, :].bitcast(F32), 1.0).then_inc(ones_set, 1)
            pool.wait_ge(small_in, N_SMALL)

            def power(t, n):
                pool.wait_ge(var_ready, t.at(TT, n + 1))
                pool.tensor_tensor(rstd[:, 1, n:n + 1], rstd[:, 0, n:n + 1], neg_half[:, :],
                                   ALU.pow).then_inc(rstd_ready, 1)

            def step(what, t, part):
                kind, i, j, h = what
                if kind == "stack":
                    fill_stack(pool, 1, 1, i, t, range(AG - 1))
                elif kind == "bias":
                    met(pool, const, 3)
                    pool.wait_ge(x_in, t.at(16 * TT, 16 * TT))
                    pool.tensor_tensor(x_tok[:, :, :], x_tok[:, :, :],
                                       brow[:, 1, :].unsqueeze(1).to_broadcast([P, TT, DM]), ALU.add).then_inc(xb_ready, 1)
                elif kind == "out":
                    power(t, i)

            over_attention(pool, n_seq, step, steps)

        @block.scalar
        def _(act):
            def step(what, t, part):
                kind, i, j, h = what
                if kind == "c":
                    if i == 0 and not t.first():
                        act.wait_ge(qk_done[1], t.at(KT, 0))
                    act.wait_ge(landed[i % 2], t.at(64, 16 * (i // 2 + 1)))
                    act.activation(c_hi[:, i, :], land[:, i % 2, :], ACT.Copy).then_inc(c_hi_s, 1)
                elif kind == "xt":
                    act.wait_ge(xt_done, t.at(TT, i + 1))
                    act.activation(xt_hi[:, :, i * P:(i + 1) * P], bank(what)[:, :].rearrange("p (k n) -> p k n", n=P),
                                   ACT.Copy).then_inc(xt_hi_s, 1)
                elif kind == "qk":
                    if part == "start" and i == 0 and j == 0:
                        act.wait_ge(small_in, N_SMALL)
                    act.wait_ge(qk_done[j], t.at(KT, i + 1))
                    if i >= 2:
                        stack_filled(act, i - 2, t, range(j + 1))
                    elif not t.first():
                        stack_filled(act, i + 2, t.before(), range(j + 1))
                    act.activation(qk_hi[:, j, i % 2, :], bank(what)[:, :], ACT.Identity, bias=bcol[:, j, i:i + 1]
                                   ).then_inc(qk_hi_s[j], 1)
                elif kind == "st":
                    n = TT * i + j
                    for half in range(2):
                        act.wait_ge(st_done, t.at(2 * UNITS, 2 * n + half + 1))
                        if half == 0 and (n >= 2 or not t.first()):
                            act.wait_ge(av_done, t.at(UNITS, n - 1))
                        act.activation(probs[:, n % 2, 2 * half:2 * half + 2],
                                       sp_banks[:, 2 * half:2 * half + 2], ACT.Exp,
                                       scale=SOFT_SCALE).then_inc(exp_ready, 1)
                elif kind == "o":
                    act.wait_ge(av_done, t.at(UNITS, TT * (i + 1)))
                    if i or not t.first():
                        act.wait_ge(o_ready, t.at(KT, i))
                    if i == 0 and not t.first():
                        act.wait_ge(out_done, t.at(TT, 0))
                    act.activation(o[:, i, :], o_bank[:, :], ACT.Copy)
                    act.activation(den[:, :], den_bank[:, :], ACT.Copy).then_inc(o_copied, 1)

            over_attention(act, n_seq, step, steps)

        @block.vector
        def _(dve):
            wchain = Chain(dve, w_v, 0)
            wchain.start(0)

            def split_weight(i, n):
                dve.wait_ge(w_in[i % 2], 16 * (i // 2 + 1))
                wchain.link(dve.tensor_copy(w_hi[n][:, :, :], probs[:, i % 2]))
                dve.tensor_tensor(w_lo[n][:, :, :], probs[:, i % 2], w_hi[n][:, :, :],
                                  ALU.subtract).then_inc(w_used, 1)

            for i in range(2):
                split_weight(i, names[i])
            ln_chain = Chain(dve, ln_v, 2 * TT)

            def apply(t, n):
                dve.wait_ge(rstd_ready, t.at(TT, n + 1))
                dve.tensor_scalar(x_tok[:, n, :], x_tok[:, n, :], mv[:, n, 0:1], rstd[:, 1, n:n + 1],
                                  ALU.subtract, ALU.mult).then_inc(x2_ready, 1)

            def step(what, t, part):
                kind, i, j, h = what
                if kind == "c":
                    dve.wait_ge(c_hi_s, t.at(KT, i + 1))
                    dve.tensor_tensor(c_lo[:, i, :], land[:, i % 2, :], c_hi[:, i, :],
                                      ALU.subtract).then_inc(c_split, 1)
                elif kind == "xt":
                    dve.wait_ge(xt_hi_s, t.at(TT, i + 1))
                    cols = slice(i * P, (i + 1) * P)
                    dve.tensor_tensor(xt_lo[:, :, cols], bank(what)[:, :].rearrange("p (k n) -> p k n", n=P),
                                      xt_hi[:, :, cols], ALU.subtract).then_inc(xt_split, 1)
                elif kind == "qk":
                    dve.wait_ge(qk_hi_s[j], t.at(KT, i + 1))
                    dve.scalar_tensor_tensor(out=qk_lo[:, j, i % 2, :], in0=bank(what)[:, :],
                                             scalar=bcol[:, j, i:i + 1], in1=qk_hi[:, j, i % 2, :].bitcast(F32),
                                             op0=ALU.add, op1=ALU.subtract).then_inc(qk_split[j], 1)
                elif kind == "v":
                    if part == "start" and i == 0:
                        split_weight(2, names[2])
                    dve.wait_ge(v_done, t.at(TT, i + 1))
                    if i == 0:
                        if part == "start":
                            dve.wait_ge(small_in, N_SMALL)
                        if not t.first():
                            dve.wait_ge(av_done, t.at(UNITS, 0))
                    dve.tensor_tensor(v[:, i, :], bank(what)[:, :], brow[:, 0, :], ALU.add).then_inc(v_ready, 1)
                elif kind == "p1":
                    for hh in (2 * h, 2 * h + 1):
                        dve.wait_ge(p1_done, t.at(AG * UNITS, AG * (TT * i + j) + hh + 1))
                        if hh == 0 and j == 0 and (i >= 2 or not t.first()):
                            dve.wait_ge(neg_done, t.at(KT, i - 1))
                        dve.tensor_reduce(mx[:, i % 2, j, hh:hh + 1], bank((kind, i, j, hh))[:, :], AX.X,
                                          ALU.max).then_inc(mx_ready, 1)
                elif kind == "neg":
                    dve.wait_ge(neg_done, t.at(KT, i + 1))
                    if i or not t.first():
                        dve.wait_ge(neg_in[(i - 1) % 2], t.at(32 * KT // 2, 32 * ((i + 1) // 2)))
                    src = bank(what)[0:AG, :]
                    dve.tensor_scalar(neg_hi[:, :], src, -1.0, None, ALU.mult).then_inc(neg_v, 1)
                    dve.wait_ge(neg_v, t.at(KT, i + 1))
                    dve.scalar_tensor_tensor(out=neg_lo[:, :], in0=src, scalar=-1.0, in1=neg_hi[:, :].bitcast(F32),
                                             op0=ALU.mult, op1=ALU.subtract).then_inc(neg_ready, 1)
                elif kind == "norm":
                    if j == 0:
                        dve.wait_ge(o_copied, t.at(KT, i + 1))
                    cols = slice(j * P, (j + 1) * P)
                    dve.reciprocal(den[:, cols], den[:, cols]).then_inc(o_v, 1)
                    if j == TT - 1:
                        dve.wait_ge(o_v, t.at(KT * TT, TT * (i + 1)))
                        dve.tensor_tensor(o[:, i, :], o[:, i, :], den[:, :], ALU.mult).then_inc(o_ready, 1)
                elif kind == "out":
                    if i == 0:
                        ln_chain.start(t.number())
                        dve.wait_ge(xb_ready, t.at(1, 1))
                    dve.wait_ge(out_done, t.at(TT, i + 1))
                    dve.tensor_tensor(x_tok[:, i, :], bank(what)[:, :], x_tok[:, i, :],
                                      ALU.add).then_inc(out_read, 1)
                    dve.wait_ge(out_read, t.at(TT, i + 1))
                    ln_chain.link(dve.bn_stats(stats[:, i, :], x_tok[:, i, :]), (const, 3))
                    ln_chain.link(dve.bn_aggr(mv[:, i, :], stats[:, i, :]))
                    dve.tensor_scalar(rstd[:, 0, i:i + 1], mv[:, i, 1:2], LN_EPS, None, ALU.add).then_inc(var_ready, 1)
                    if i:
                        apply(t, i - 1)
                elif kind == "end":
                    apply(t, TT - 1)

            over_attention(dve, n_seq, step, steps)

        @block.tensor
        def _(pe):
            pe.wait_ge(const, 3)
            pe.wait_ge(ones_set, 1)

            def take(part, use, t):
                past = before[part, use]
                if past:
                    s, per, count = reader(*past[0])
                    pe.wait_ge(s, Turn(t.b, t.phase, past[1]).at(per, count))

            def project(part, what, t, w, x_parts, cols, w_moves, done):
                take(part, what, t)
                wh, wl = w
                for k in range(KT):
                    for n, (wp, xp) in enumerate(((wh, x_parts[0]), (wh, x_parts[1]), (wl, x_parts[0]))):
                        pair = ((xp[:, k, cols], wp[:, k, :]) if w_moves else (wp[:, k, cols], xp[:, k, :]))
                        ins = pe.matmul(bank(what)[:, :], *pair, start=(k == n == 0), stop=(k == KT - 1 and n == 2))
                ins.then_inc(done, 1)

            def step(what, t, part):
                kind, i, j, h = what
                tile = slice(i * P, (i + 1) * P)
                if kind == "xt":
                    pe.wait_ge(landed[i % 2], t.at(64, 32 + 16 * (i // 2 + 1)))
                    take(part, what, t)
                    for k in range(KT):
                        ins = pe.transpose(bank(what)[:, k * P:(k + 1) * P], land[:, i % 2, k * P:(k + 1) * P],
                                           ident[:, :])
                    ins.then_inc(xt_done, 1)
                elif kind == "qk":
                    if i == 0:
                        pe.wait_ge(*((c_split, t.at(KT, KT)) if j else (xt_split, t.at(TT, TT))))
                    n = names[j]
                    project(part, what, t, (w_hi[n], w_lo[n]), (c_hi, c_lo) if j else (xt_hi, xt_lo),
                            tile, False, qk_done[j])
                elif kind == "v":
                    if part == "start" and i == 0:
                        pe.wait_ge(w_used, 3)
                    project(part, what, t, (w_hi["v"], w_lo["v"]), (c_hi, c_lo), tile, True, v_done)
                elif kind == "p1":
                    if j == 0 and h == 0:
                        stack_filled(pe, i, t)
                    for hh in (2 * h, 2 * h + 1):
                        use = (kind, i, j, hh)
                        take(part, use, t)
                        pe.matmul(bank(use)[:, :], qs[0:STACK, t.slot(i), hh, j * P:(j + 1) * P],
                                  ks[0:STACK, t.slot(i), hh, :], start=True, stop=True).then_inc(p1_done, 1)
                elif kind == "neg":
                    take(part, what, t)
                    pe.wait_ge(mx_ready, t.at(AG * UNITS, AG * TT * (i + 1)))
                    for n in range(TT):
                        ins = pe.transpose(bank(what)[0:AG, n * P:(n + 1) * P], mx[:, i % 2, n, :], ident[:, :])
                    ins.then_inc(neg_done, 1)
                elif kind == "st":
                    n = TT * i + j
                    if j == 0:
                        pe.wait_ge(neg_in[i % 2], t.at(32 * KT // 2, 32 * (i // 2 + 1)))
                    for hh in range(AG):
                        if hh % 2 == 0 and (n or not t.first()):
                            pe.wait_ge(exp_ready, t.at(2 * UNITS, 2 * n + hh // 2 - 1))
                        ins = pe.matmul(sp_banks[:, hh, :], ks[0:STACK + 2, t.slot(i), hh, j * P:(j + 1) * P],
                                        qs[0:STACK + 2, t.slot(i), hh, :], start=True, stop=True)
                        if hh % 2:
                            ins.then_inc(st_done, 1)
                elif kind == "av":
                    n = TT * i + j
                    if h == 0:
                        pe.wait_ge(exp_ready, t.at(2 * UNITS, 2 * n + 2))
                        if n == 0:
                            pe.wait_ge(v_ready, t.at(TT, TT))
                        if j == 0 and (i or not t.first()):
                            pe.wait_ge(o_copied, t.at(KT, i))
                    for hh in range(AG):
                        rows = slice(hh * AD, (hh + 1) * AD)
                        if h == 0:
                            pe.matmul(o_bank[rows, :], v[:, j, i * P + hh * AD:i * P + (hh + 1) * AD],
                                      probs[:, n % 2, hh, :], start=(j == 0), stop=(j == TT - 1))
                        else:
                            ins = pe.matmul(den_bank[rows, :], onesf[:, 0:AD], probs[:, n % 2, hh, :],
                                            start=(j == 0), stop=(j == TT - 1))
                    if h:
                        ins.then_inc(av_done, 1)
                elif kind == "out":
                    if i == 0:
                        pe.wait_ge(o_ready, t.at(KT, KT))
                    take(part, what, t)
                    for k in range(KT):
                        ins = pe.matmul(bank(what)[:, :], o[:, k, tile], w_o[:, k, :], start=(k == 0),
                                        stop=(k == KT - 1))
                    ins.then_inc(out_done, 1)

            over_attention(pe, n_seq, step, steps)


NE = 16
SL = 16
SLOTS = NE * SL
ST_TILES = SLOTS // P
EH = 128
B_SLOTS = 4
X_BUFS = 3
NORM_EPS = 1e-12


def is_zero(b):
    return isinstance(b, int) and b == 0


def at_pair(b, p, per):
    return (b - p) * (per // 2) + per


def over_pairs(eng, count, front, back):
    front(0, 0, True)
    front(1, 1, True)
    back(0, 0, True)
    if count > 2:
        with eng.Fori(0, count // 2 - 1) as i:
            front(i * 2 + 2, 0, False)
            back(i * 2 + 1, 1, False)
            front(i * 2 + 3, 1, False)
            back(i * 2 + 2, 0, False)
    back(count - 1, 1, False)


def over_routed(eng, count, step, ready=None, finish=None):
    if ready:
        ready(0, 0, 0)
    step(0, 0, False, (1, 1, 0))
    turns = (count - 2) // X_BUFS
    if turns:
        with eng.Fori(0, turns) as i:
            for n in range(X_BUFS):
                step(i * X_BUFS + 1 + n, (1 + n) % X_BUFS, True,
                     (i * X_BUFS + 2 + n, (2 + n) % X_BUFS, i + (2 + n) // X_BUFS))
    for b in range(1 + turns * X_BUFS, count - 1):
        step(b, b % X_BUFS, True, (b + 1, (b + 1) % X_BUFS, (b + 1) // X_BUFS))
    step(count - 1, (count - 1) % X_BUFS, True, None)
    if finish:
        finish(count - 1, (count - 1) % X_BUFS)


def moe_stage(nc, n_seq, x2, gamma, beta, mu, scale, w1, b1, w2, b2, combine_t, slot_out, x3):
    with ExitStack() as ctx:
        def sb(name, shape, dt=F32):
            return ctx.enter_context(nc.sbuf_tensor("e_" + name, shape, dt))

        def ps(name, shape=(P, 512)):
            return ctx.enter_context(nc.psum_tensor("e_" + name, list(shape), F32))

        def sem(name):
            return ctx.enter_context(nc.semaphore("e_" + name))

        grow = sb("grow", [P, DM])
        berow = sb("berow", [P, DM])
        mu_u = sb("mu_u", [P, KT, SLOTS])
        mu_sq = sb("mu_sq", [P, KT, SLOTS])
        mu_n = sb("mu_n", [P, 2, ST_TILES])
        mu_diag = sb("mu_diag", [P, ST_TILES, P])
        scol = sb("scol", [P, 1])
        b1col = sb("b1col", [P, NE])
        b2row = sb("b2row", [P, B_SLOTS, DM])
        ident = sb("ident", [P, P])
        onesf = sb("onesf", [P, P])
        neg_half = sb("neg_half", [P, TT])
        x = sb("x", [P, X_BUFS, TT, DM])
        stats = sb("stats", [P, TT, 6])
        mv = sb("mv", [P, TT, 2])
        rstd = sb("rstd", [P, 2, TT])
        junk = sb("junk", [P, TT, DM])
        ss = sb("ss", [P, 3, TT])
        rs = sb("rs", [P, TT])
        xnt = sb("xnt", [P, KT, SEQ])
        lg = sb("lg", [P, TT, SLOTS])
        disp_t = sb("disp_t", [P, ST_TILES, SEQ])
        disp = sb("disp", [P, TT, SLOTS])
        comb = sb("comb", [P, TT, SLOTS])
        mxd = sb("mxd", [P, 2, ST_TILES])
        sd = sb("sd", [P, 2, ST_TILES])
        mxc = sb("mxc", [P, TT])
        neg_mxc = sb("neg_mxc", [P, TT])
        sc = sb("sc", [P, TT])
        rc_all = sb("rc_all", [P, n_seq, TT])
        comb_t = sb("comb_t", [P, ST_TILES, SEQ])
        slots_t = sb("slots_t", [P, KT, NE, n_seq, SL])
        w1s = sb("w1s", [P, NE, KT, EH])
        w2s = sb("w2s", [P, NE, DM])
        hs = sb("hs", [P, 2, P])
        so = sb("so", [P, 2, DM])
        so_in = sb("so_in", [P, 2, ST_TILES, DM])
        ct_in = sb("ct_in", [P, 2, ST_TILES, SEQ])
        rows = n_seq * SL

        turn = [ps("turn0"), ps("turn1")]
        lg_ps = ps("lg_ps", (P, TT, SLOTS))
        sl_ps = ps("sl_ps", (P, KT, SLOTS))
        ct_ps = ps("ct_ps", (P, ST_TILES, SEQ))

        const = sem("const")
        small_in = sem("small_in")
        mu_in = sem("mu_in")
        mu_s = sem("mu_s")
        mu_ready = sem("mu_ready")
        x_in = [sem(f"x_in{i}") for i in range(X_BUFS)]
        var_ready = sem("var_ready")
        rstd_ready = sem("rstd_ready")
        xg_ready = sem("xg_ready")
        xn_ready = sem("xn_ready")
        ss_ready = sem("ss_ready")
        ssb_ready = sem("ssb_ready")
        rn_ready = sem("rn_ready")
        rs_ready = sem("rs_ready")
        turn_done = sem("turn_done")
        turn_read = sem("turn_read")
        lg_done = sem("lg_done")
        lg_read = sem("lg_read")
        mx_ready = sem("mx_ready")
        mc_ready = sem("mc_ready")
        dn_ready = sem("dn_ready")
        disp_turned = sem("disp_turned")
        comb_ready = sem("comb_ready")
        disp_ready = sem("disp_ready")
        ln1_v = sem("ln1_v")
        sums_v = sem("sums_v")
        rc_ready = sem("rc_ready")
        ct_done = sem("ct_done")
        ct_read = sem("ct_read")
        ct_out = sem("ct_out")
        sl_done = sem("sl_done")
        sl_read = sem("sl_read")
        w_in = sem("w_in")
        b2_in = [sem(f"b2_in{i}") for i in range(B_SLOTS)]
        h_done = sem("h_done")
        h_ready = sem("h_ready")
        e_done = sem("e_done")
        so_ready = sem("so_ready")
        so_out = [sem("so_out0"), sem("so_out1")]
        c_in = [sem("c_in0"), sem("c_in1")]
        x3_out = sem("x3_out")

        out_banks = [sl_ps[:, 0:2, :], sl_ps[:, 2:4, :], ct_ps[:, 0, :], ct_ps[:, 1, :]]

        def out_bank(e):
            return out_banks[e % 2].rearrange("p a n -> p (a n)")

        def c_bank(t):
            return out_bank(t) if t < 2 else out_banks[t]

        def second(pe, e):
            pe.wait_ge(h_ready, e + 1)
            if e >= 2:
                pe.wait_ge(so_ready, e - 1)
            pe.matmul(out_bank(e)[0:rows, :], hs[:, e % 2, 0:rows], w2s[:, e, :],
                      start=True, stop=True).then_inc(e_done, 1)

        out_done, out_read, var2_ready, rstd2_ready = lg_done, lg_read, var_ready, rstd_ready
        x3_ready, residual_in = xg_ready, x_in
        routed = n_seq

        block = ctx.enter_context(nc.Block())
        N_SMALL = 4
        TURNS = KT + ST_TILES

        @block.sync
        def _(sp):
            def load_x(b, p, landed):
                sp.dma_start(x[:, p], one(x2, b).rearrange("a (t p) n -> p (a t) n", p=P)).then_inc(landed[p], 16)

            sp.dma_start(mu_u[:, :, :], mu.rearrange("(k p) n -> p k n", p=P)).then_inc(mu_in, 16)
            load_x(0, 0, x_in)
            sp.dma_start(grow[:, :], gamma.partition_broadcast(P)).then_inc(small_in, 16)
            sp.dma_start(berow[:, :], beta.partition_broadcast(P)).then_inc(small_in, 16)
            sp.dma_start(scol[:, :], scale.partition_broadcast(P)).then_inc(small_in, 16)
            sp.dma_start(b1col[:, :], b1).then_inc(small_in, 16)
            load_x(1, 1, x_in)

            def load_bias(e):
                sp.dma_start(b2row[:, e % B_SLOTS, :], b2[e].partition_broadcast(P)).then_inc(b2_in[e % B_SLOTS], 16)

            for e in range(NE):
                sp.dma_start(w1s[:, e], w1[e].rearrange("(k p) h -> p k h", p=P)).then_inc(w_in, 16)
                sp.dma_start(w2s[:, e], w2[e]).then_inc(w_in, 16)
            for e in range(B_SLOTS):
                load_bias(e)

            def keep_combine(b):
                sp.wait_ge(ct_read, at(b, ST_TILES, ST_TILES))
                sp.dma_start(one(combine_t, b).rearrange("a (j p) n -> p (a j) n", p=P), comb_t[:, :, :]
                             ).then_inc(ct_out, 16)

            def step(b, p, past, after):
                if after and past:
                    sp.wait_ge(sl_done, at(b, 1, 0))
                    load_x(b + 1, (p + 1) % X_BUFS, x_in)
                if past:
                    keep_combine(b - 1)

            over_routed(sp, n_seq, step, finish=lambda b, p: keep_combine(b))

            def load_weights(b, p):
                sp.dma_start(ct_in[:, p], one(combine_t, b).rearrange("a (j p) n -> p (a j) n", p=P)
                             ).then_inc(c_in[p], 16)

            def load_slots(b, p):
                sp.dma_start(so_in[:, p], one(slot_out, b).rearrange("a (j e) s d -> (e s) (a j) d", j=ST_TILES)
                             ).then_inc(c_in[p], 16)

            sp.wait_ge(sl_done, 1 + n_seq)
            sp.wait_ge(ct_out, 16 * n_seq)
            for b in range(2):
                load_weights(b, b)
                load_x(b, b, residual_in)
            for e in range(NE):
                sp.wait_ge(so_ready, e + 1)
                sp.dma_start(slot_out[:, e], so[0:rows, e % 2, :]).then_inc(so_out[e % 2], 16)
                if e + B_SLOTS < NE:
                    load_bias(e + B_SLOTS)
            for p in range(2):
                sp.wait_ge(so_out[p], 16 * NE // 2)

            def combine(b, p, first):
                if first:
                    load_slots(b, p)
                    return
                sp.wait_ge(out_done, routed + at(b, TT, -TT))
                load_weights(b, p)
                load_slots(b, p)
                sp.wait_ge(x3_out, at(b, 16 * TT, -16 * TT))
                load_x(b, p, residual_in)

            def stores(b, p, first):
                for t in range(TT):
                    sp.wait_ge(x3_ready, 2 * routed + at(b, TT, t + 1))
                    sp.dma_start(one(x3, b)[:, t * P:(t + 1) * P, :].rearrange("a p n -> p (a n)"),
                                 x[:, p, t, :]).then_inc(x3_out, 16)

            over_pairs(sp, n_seq, combine, stores)
            sp.wait_ge(x3_out, 16 * TT * n_seq)

        @block.gpsimd
        def _(pool):
            pool.memset(onesf[:, :], 1.0).then_inc(const, 1)
            pool.memset(neg_half[:, :], -0.5).then_inc(const, 1)
            pool.wait_ge(const, 2)
            pool.affine_select(out=ident[:, :], in_=onesf[:, :], compare_op=ALU.is_equal, fill=0.0,
                               base=0, pattern=[[-1, P]], channel_multiplier=1).then_inc(const, 1)
            pool.wait_ge(mu_s, 3)
            pool.tensor_tensor(mu_n[:, 1], mu_n[:, 0], neg_half[:, 0:ST_TILES], ALU.pow).then_inc(mu_s, 1)

            def ready(b, p, turn):
                pool.wait_ge(small_in, 16 * N_SMALL)
                pool.wait_ge(var_ready, at(b, 1, 1))
                pool.tensor_tensor(rstd[:, 1], rstd[:, 0], neg_half[:, 0:TT], ALU.pow).then_inc(rstd_ready, 1)
                for half in range(2):
                    pool.wait_ge(xg_ready, at(b, 2, half + 1))
                    tiles = slice(half * TT // 2, (half + 1) * TT // 2)
                    ins = pool.tensor_tensor(x[:, p, tiles], x[:, p, tiles],
                                             berow[:, :].unsqueeze(1).to_broadcast([P, TT // 2, DM]), ALU.add)
                ins.then_inc(xn_ready, 1)

            def norm_power(b):
                pool.wait_ge(ssb_ready, at(b, 1, 1))
                pool.tensor_tensor(ss[:, 2], ss[:, 1], neg_half[:, 0:TT], ALU.pow).then_inc(rn_ready, 1)

            def step(b, p, past, after):
                norm_power(b)
                if after:
                    ready(*after)

            over_routed(pool, n_seq, step, ready)

            def powers(b, p, first):
                for t in range(TT):
                    pool.wait_ge(var2_ready, routed + at(b, TT, t + 1))
                    pool.tensor_tensor(rstd[:, 1, t:t + 1], rstd[:, 0, t:t + 1], neg_half[:, 0:1],
                                       ALU.pow).then_inc(rstd2_ready, 1)

            over_pairs(pool, n_seq, powers, lambda b, p, first: None)

        @block.scalar
        def _(act):
            act.wait_ge(mu_in, 16)
            act.activation(mu_sq[:, :, :], mu_u[:, :, :], ACT.Square).then_inc(mu_s, 1)
            act.wait_ge(small_in, 16 * N_SMALL)

            def combine_weights(b):
                act.wait_ge(mc_ready, at(b, 1, 1))
                for t in range(TT):
                    ins = act.activation(comb[:, t, :], lg[:, t, :], ACT.Exp, bias=neg_mxc[:, t:t + 1],
                                         accum_out=sc[:, t:t + 1])
                ins.then_inc(comb_ready, 1)

            def turned_combine(b):
                for j in range(ST_TILES):
                    act.wait_ge(ct_done, at(b, ST_TILES, j + 1))
                    if j == 0 and not is_zero(b):
                        act.wait_ge(ct_out, at(b, 16, 0))
                    act.activation(comb_t[:, j, :], ct_ps[:, j, :], ACT.Copy).then_inc(ct_read, 1)

            def step(b, p, past, after):
                for k in range(KT):
                    act.wait_ge(turn_done, at(b, TURNS, k + 1))
                    act.activation(xnt[:, k, :], turn[k % 2][:, :], ACT.Copy).then_inc(turn_read, 1)
                if past:
                    combine_weights(b - 1)
                act.wait_ge(xn_ready, at(b, 1, 1))
                for t in range(TT):
                    ins = act.activation(junk[:, t, :], x[:, p, t, :], ACT.Square, accum_out=ss[:, 0, t:t + 1])
                ins.then_inc(ss_ready, 1)
                act.wait_ge(lg_done, at(b, 1, 1))
                act.wait_ge(rs_ready, at(b, 1, 1))
                for t in range(TT):
                    ins = act.activation(lg[:, t, :], lg_ps[:, t, :], ACT.Identity, scale=rs[:, t:t + 1])
                ins.then_inc(lg_read, 1)
                if past:
                    turned_combine(b - 1)
                for j in range(ST_TILES):
                    act.wait_ge(turn_done, at(b, TURNS, KT + j + 1))
                    act.wait_ge(mx_ready, at(b, ST_TILES, j + 1))
                    act.activation(disp_t[:, j, :], turn[j % 2][:, :], ACT.Exp, bias=mxd[:, 1, j:j + 1],
                                   accum_out=sd[:, 0, j:j + 1]).then_inc(turn_read, 1)

            def finish(b, p):
                combine_weights(b)
                turned_combine(b)

            over_routed(act, n_seq, step, finish=finish)

            for e in range(NE):
                act.wait_ge(h_done, e + 1)
                if e >= 2:
                    act.wait_ge(e_done, e - 1)
                act.activation(hs[:, e % 2, 0:rows], turn[e % 2][:, 0:rows], ACT.Gelu,
                               bias=b1col[:, e:e + 1]).then_inc(h_ready, 1)

        @block.vector
        def _(dve):
            dve.wait_ge(mu_s, 2)
            dve.tensor_scalar(mu_n[:, 0], turn[0][:, 0:ST_TILES], NORM_EPS ** 2, None, ALU.max).then_inc(mu_s, 1)
            dve.wait_ge(mu_s, 4)
            dve.wait_ge(const, 3)
            for j in range(ST_TILES):
                ins = dve.tensor_scalar(mu_diag[:, j, :], ident[:, :], mu_n[:, 1, j:j + 1], None, ALU.mult)
            ins.then_inc(mu_s, 1)
            dve.wait_ge(sl_done, 1)
            for k in range(KT):
                ins = dve.tensor_tensor(mu_u[:, k, :], mu_u[:, k, :], lg_ps[:, 0, :], ALU.mult)
            ins.then_inc(mu_ready, 1)
            ln = Chain(dve, ln1_v, 4)
            sums = Chain(dve, sums_v, 2 * ST_TILES + 1)

            def ready(b, p, turn):
                if is_zero(b):
                    dve.wait_ge(small_in, 16 * N_SMALL)
                ln.start(b)
                dve.wait_ge(x_in[p], turn * 16 + 16)
                for t in range(TT):
                    ins = dve.bn_stats(stats[:, t, :], x[:, p, t, :])
                ln.link(ins, (const, 3))
                for t in range(TT):
                    ins = dve.bn_aggr(mv[:, t, :], stats[:, t, :])
                ln.link(ins)
                dve.tensor_scalar(rstd[:, 0], mv[:, :, 1], LN_EPS, None, ALU.add).then_inc(var_ready, 1)
                dve.wait_ge(rstd_ready, at(b, 1, 1))
                for half in range(2):
                    tiles = range(half * TT // 2, (half + 1) * TT // 2)
                    for t in tiles:
                        ins = dve.tensor_scalar(x[:, p, t, :], x[:, p, t, :], mv[:, t, 0:1], rstd[:, 1, t:t + 1],
                                                ALU.subtract, ALU.mult)
                    ln.link(ins)
                    both = x[:, p, tiles[0]:tiles[-1] + 1]
                    dve.tensor_tensor(both, both, grow[:, :].unsqueeze(1).to_broadcast([P, TT // 2, DM]),
                                      ALU.mult).then_inc(xg_ready, 1)
                ln.end()

            def row_scales(b):
                dve.wait_ge(ss_ready, at(b, 1, 1))
                dve.tensor_scalar(ss[:, 1], ss[:, 0], NORM_EPS ** 2, None, ALU.max).then_inc(ssb_ready, 1)
                dve.wait_ge(rn_ready, at(b, 1, 1))
                dve.tensor_scalar(rs[:, :], ss[:, 2], scol[:, 0:1], None, ALU.mult).then_inc(rs_ready, 1)

            def weights(b):
                sums.start(b)
                for j in range(ST_TILES):
                    dve.wait_ge(turn_done, at(b, TURNS, KT + j + 1))
                    sums.link(dve.tensor_reduce(mxd[:, 0, j:j + 1], turn[j % 2][:, :], AX.X, ALU.max))
                    dve.tensor_scalar(mxd[:, 1, j:j + 1], mxd[:, 0, j:j + 1], -1.0, None, ALU.mult
                                      ).then_inc(mx_ready, 1)
                sums.link(dve.tensor_reduce(mxc[:, :], lg[:, :, :], AX.X, ALU.max))
                dve.tensor_scalar(neg_mxc[:, :], mxc[:, :], -1.0, None, ALU.mult).then_inc(mc_ready, 1)
                for j in range(ST_TILES):
                    dve.wait_ge(turn_read, at(b, TURNS, KT + j + 1))
                    sums.link(dve.reciprocal(sd[:, 1, j:j + 1], sd[:, 0, j:j + 1]))
                    ins = dve.tensor_scalar(disp_t[:, j, :], disp_t[:, j, :], sd[:, 1, j:j + 1], None, ALU.mult)
                ins.then_inc(dn_ready, 1)
                sums.end()

            def turned(b):
                dve.wait_ge(disp_turned, at(b, 1, 1))
                for half in range(2):
                    t2 = slice(half * TT // 2, (half + 1) * TT // 2)
                    ins = dve.tensor_copy(disp[:, t2, :], lg_ps[:, t2, :])
                ins.then_inc(disp_ready, 1)

            def combine_sums(b):
                dve.wait_ge(comb_ready, at(b, 1, 1))
                dve.reciprocal(rc_all[:, bass.ds(b, 1), :].rearrange("p a t -> p (a t)"), sc[:, :]
                               ).then_inc(rc_ready, 1)

            def keep_slots(b):
                dve.wait_ge(sl_done, at(b, 1, 2))
                for k in range(KT):
                    ins = dve.tensor_copy(slots_t[:, k, :, bass.ds(b, 1), :].rearrange("p e a s -> p e (a s)"),
                                          sl_ps[:, k, :].rearrange("p (e s) -> p e s", s=SL))
                ins.then_inc(sl_read, 1)

            def step(b, p, past, after):
                if past:
                    turned(b - 1)
                    combine_sums(b - 1)
                row_scales(b)
                if after:
                    ready(*after)
                if past:
                    keep_slots(b - 1)
                weights(b)

            def finish(b, p):
                turned(b)
                combine_sums(b)
                keep_slots(b)

            over_routed(dve, n_seq, step, ready, finish)

            for e in range(NE):
                dve.wait_ge(e_done, e + 1)
                if e >= 2:
                    dve.wait_ge(so_out[e % 2], 16 * (e // 2))
                dve.wait_ge(b2_in[e % B_SLOTS], 16 * (e // B_SLOTS + 1))
                dve.tensor_tensor(so[0:rows, e % 2, :], out_bank(e)[0:rows, :], b2row[0:rows, e % B_SLOTS, :],
                                  ALU.add).then_inc(so_ready, 1)

            ln_chain = Chain(dve, ln1_v, 2 * TT, 4 * n_seq)

            def output(b, p, first):
                ln_chain.start(b)
                dve.wait_ge(residual_in[p], 16 * len(range(p, n_seq, X_BUFS)) + at_pair(b, p, 16))

                for t in range(TT):
                    dve.wait_ge(out_done, routed + at(b, TT, t + 1))
                    dve.scalar_tensor_tensor(out=x[:, p, t, :], in0=c_bank(t)[:, :],
                                             scalar=rc_all[:, bass.ds(b, 1), t:t + 1].rearrange("p a t -> p (a t)"),
                                             in1=x[:, p, t, :], op0=ALU.mult, op1=ALU.add).then_inc(out_read, 1)
                    dve.wait_ge(out_read, routed + at(b, TT, t + 1))
                    ln_chain.link(dve.bn_stats(stats[:, t, :], x[:, p, t, :]), (const, 3))
                    ln_chain.link(dve.bn_aggr(mv[:, t, :], stats[:, t, :]))
                    dve.tensor_scalar(rstd[:, 0, t:t + 1], mv[:, t, 1:2], LN_EPS, None, ALU.add).then_inc(var2_ready, 1)
                for t in range(TT):
                    dve.wait_ge(rstd2_ready, routed + at(b, TT, t + 1))
                    dve.tensor_scalar(x[:, p, t, :], x[:, p, t, :], mv[:, t, 0:1], rstd[:, 1, t:t + 1],
                                      ALU.subtract, ALU.mult).then_inc(x3_ready, 1)
                ln_chain.end()

            over_pairs(dve, n_seq, lambda b, p, first: None, output)

        @block.tensor
        def _(pe):
            pe.wait_ge(const, 3)
            pe.wait_ge(mu_s, 1)
            for j in range(ST_TILES):
                for k in range(KT):
                    ins = pe.matmul(turn[0][:, j:j + 1], mu_sq[:, k, j * P:(j + 1) * P], onesf[:, 0:1],
                                    start=(k == 0), stop=(k == KT - 1))
            ins.then_inc(mu_s, 1)
            pe.wait_ge(mu_s, 5)
            for j in range(ST_TILES):
                ins = pe.matmul(lg_ps[:, 0, j * P:(j + 1) * P], onesf[:, :], mu_diag[:, j, :], start=True, stop=True)
            ins.then_inc(sl_done, 1)
            pe.wait_ge(mu_ready, 1)

            def turned(b):
                pe.wait_ge(dn_ready, at(b, 1, 1))
                for t in range(TT):
                    for j in range(ST_TILES):
                        ins = pe.transpose(lg_ps[:, t, j * P:(j + 1) * P], disp_t[:, j, t * P:(t + 1) * P],
                                           ident[:, :])
                ins.then_inc(disp_turned, 1)

            def free_turn(b, n):
                if n >= 2 or not is_zero(b):
                    pe.wait_ge(turn_read, at(b, TURNS, n - 1))

            def transposes(b, p):
                pe.wait_ge(xn_ready, at(b, 1, 1))
                for k in range(KT):
                    free_turn(b, k)
                    for t in range(TT):
                        ins = pe.transpose(turn[k % 2][:, t * P:(t + 1) * P], x[:, p, t, k * P:(k + 1) * P],
                                           ident[:, :])
                    ins.then_inc(turn_done, 1)

            def logits(b):
                pe.wait_ge(turn_read, at(b, TURNS, KT))
                if not is_zero(b):
                    pe.wait_ge(disp_ready, at(b, 1, 0))
                for t in range(TT):
                    for k in range(KT):
                        ins = pe.matmul(lg_ps[:, t, :], xnt[:, k, t * P:(t + 1) * P], mu_u[:, k, :],
                                        start=(k == 0), stop=(k == KT - 1))
                ins.then_inc(lg_done, 1)

            def mid(b):
                pe.wait_ge(lg_read, at(b, 1, 1))
                for j in range(ST_TILES):
                    free_turn(b, KT + j)
                    for t in range(TT):
                        ins = pe.transpose(turn[j % 2][:, t * P:(t + 1) * P], lg[:, t, j * P:(j + 1) * P],
                                           ident[:, :])
                    ins.then_inc(turn_done, 1)

            def back(b, p):
                pe.wait_ge(comb_ready, at(b, 1, 1))
                if not is_zero(b):
                    pe.wait_ge(ct_read, at(b, ST_TILES, 0))
                for j in range(ST_TILES):
                    for t in range(TT):
                        ins = pe.transpose(ct_ps[:, j, t * P:(t + 1) * P], comb[:, t, j * P:(j + 1) * P],
                                           ident[:, :])
                    ins.then_inc(ct_done, 1)
                pe.wait_ge(disp_ready, at(b, 1, 1))
                if not is_zero(b):
                    pe.wait_ge(sl_read, at(b, 1, 0))
                for k in range(KT):
                    for t in range(TT):
                        ins = pe.matmul(sl_ps[:, k, :], x[:, p, t, k * P:(k + 1) * P], disp[:, t, :],
                                        start=(t == 0), stop=(t == TT - 1))
                ins.then_inc(sl_done, 1)

            def step(b, p, past, after):
                transposes(b, p)
                if past:
                    turned(b - 1)
                logits(b)
                if past:
                    back(b - 1, (p - 1) % X_BUFS)
                mid(b)

            def finish(b, p):
                turned(b)
                back(b, p)

            over_routed(pe, n_seq, step, finish=finish)

            pe.wait_ge(sl_read, n_seq)
            for e in range(NE):
                if e == 0:
                    pe.wait_ge(w_in, 32 * NE)
                if e >= 2:
                    pe.wait_ge(h_ready, e - 1)
                for k in range(KT):
                    ins = pe.matmul(turn[e % 2][:, 0:rows], w1s[:, e, k, :],
                                    slots_t[:, k, e].rearrange("p b s -> p (b s)"), start=(k == 0), stop=(k == KT - 1))
                ins.then_inc(h_done, 1)
                if e:
                    second(pe, e - 1)
            second(pe, NE - 1)

            def combine(b, p, first):
                pe.wait_ge(c_in[p], at_pair(b, p, 32))
                for t in range(TT):
                    if not is_zero(b):
                        pe.wait_ge(out_read, routed + at(b, TT, t + 1 - TT))
                    elif t == 0:
                        pe.wait_ge(so_ready, NE)
                    for j in range(ST_TILES):
                        ins = pe.matmul(c_bank(t)[:, :], ct_in[:, p, j, t * P:(t + 1) * P], so_in[:, p, j, :],
                                        start=(j == 0), stop=(j == ST_TILES - 1))
                    ins.then_inc(out_done, 1)

            over_pairs(pe, n_seq, lambda b, p, first: None, combine)


def decoder(nc, n_seq, a, out):
    def scratch(name, shape):
        return nc.dram_tensor(name, shape, F32, kind="Internal").ap()

    x1 = scratch("x1", [n_seq, SEQ, DM])
    x2 = scratch("x2", [n_seq, SEQ, DM])
    combine_t = scratch("combine_t", [n_seq, SLOTS, SEQ])
    slot_out = scratch("slot_out", [n_seq, NE, SL, DM])
    mamba_stage(nc, n_seq, a["x_t"], a["x"], a["w_in_t"], a["conv_w"], a["conv_b"], a["dt_bias"], a["a_log"],
                a["d_skip"], a["norm_w"], a["w_out_t"], x1)
    attention_stage(nc, n_seq, x1, a["context_t"], [a["wq_t"], a["wk_t"], a["wv_t"], a["wo_t"]], a["b_qk"],
                    [a["bv"], a["bo"]], x2)
    moe_stage(nc, n_seq, x2, a["gamma"], a["beta"], a["mu"], a["scale"], a["w1"], a["b1_t"], a["w2"], a["b2"],
              combine_t, slot_out, out)


def lay_out(inputs):
    i = {name: np.asarray(v) for name, v in inputs.items()}
    m, t, f = "L0_attn_", "L0_xattn_", "L0_ffn_"
    di, ds = 2 * DM, 64
    z, x, bm, cm, dt = np.split(i[m + "W_in"], [di, 2 * di, 2 * di + ds, 2 * di + 2 * ds])
    ch = (di + 2 * ds) // P
    a = {
        "x": i["x"], "x_t": i["x"].transpose(0, 2, 1), "context_t": i["ctx_1024"].transpose(0, 2, 1),
        "w_in_t": np.concatenate([dt, z, x, bm, cm]).T,
        "conv_w": i[m + "conv_w"].reshape(ch, P, -1).transpose(1, 0, 2),
        "conv_b": i[m + "conv_b"].reshape(ch, P).T,
        "dt_bias": i[m + "dt_bias"], "a_log": i[m + "A_log"],
        "d_skip": i[m + "D"].reshape(-1, 2).T, "norm_w": i[m + "norm_w"].reshape(-1, P).T,
        "w_out_t": i[m + "W_out"].T,
        "b_qk": np.stack([i[t + "bq"], i[t + "bk"]]).reshape(2, KT, P).transpose(2, 0, 1),
        "bv": i[t + "bv"], "bo": i[t + "bo"],
        "gamma": i[f + "ln_gamma"], "beta": i[f + "ln_beta"], "mu": i[f + "mu"].reshape(DM, SLOTS),
        "scale": i[f + "scale"], "w1": i[f + "w1"], "b1_t": i[f + "b1"].T, "w2": i[f + "w2"], "b2": i[f + "b2"],
    }
    for n in "qkvo":
        a[f"w{n}_t"] = i[t + "W" + n].T
    return {name: np.ascontiguousarray(v) for name, v in a.items()}


def kernel(**inputs):
    import concourse.bacc as bacc
    from concourse.bass_utils import run_bass_kernel_spmd

    nc = bacc.Bacc("TRN2", target_bir_lowering=False, num_devices=1)
    arrays = lay_out(inputs)
    a = {name: nc.dram_tensor(f"{name}_in", v.shape, mybir.dt.from_np(v.dtype), kind="ExternalInput").ap()
         for name, v in arrays.items()}
    n_seq = arrays["x"].shape[0]
    out = nc.dram_tensor("out", (n_seq, SEQ, DM), F32, kind="ExternalOutput").ap()
    decoder(nc, n_seq, a, out)
    result = run_bass_kernel_spmd(nc, [{f"{name}_in": v for name, v in arrays.items()}], core_ids=[0])
    return result.results[0]["out"]
```
